# Optimizing a Trainium2 kernel written in Bass

```python
import numpy as np
import jax
import jax.numpy as jnp

def _softmax(x, axis=-1):
    return jax.nn.softmax(x, axis=axis)

def _gelu(x):
    return jax.nn.gelu(x, approximate=True)

def _silu(x):
    return jax.nn.silu(x)

def _sigmoid(x):
    return jax.nn.sigmoid(x)

def _layernorm(x, axis=-1, eps=1e-05):
    m = jnp.mean(x, axis=axis, keepdims=True)
    v = jnp.var(x, axis=axis, keepdims=True)
    return (x - m) / jnp.sqrt(v + eps)

def _scatter_add(tgt, idx, src, axis=0):
    return tgt.at[idx].add(src)

def _segment_sum(src, seg, n):
    return jax.ops.segment_sum(src, seg, n)
kernel_name = 'mk_hybrid_d1_jaxref_r8_13b4f2'

def setup_inputs(seed: int=0):
    np.random.seed(seed)
    _w = jnp.asarray

    def _L0_attn_a_setup():
        import jax, jax.numpy as jnp
        import numpy as np
        N_LAYERS = 4
        D_MODEL = 128
        D_INNER = 256
        DT_RANK = 64
        D_STATE = 16
        D_CONV = 4
        EPS = 1e-05

        def _rms(x, w):
            return x * jax.lax.rsqrt(jnp.mean(x * x, axis=-1, keepdims=True) + EPS) * w

        def _silu(x):
            return x * jax.nn.sigmoid(x)
        key = jax.random.key(seed)
        ks = jax.random.split(key, 8)
        B, L = (2, 128)
        s = 0.02
        nl, dm, di = (N_LAYERS, D_MODEL, D_INNER)
        return {'x': jax.random.normal(ks[0], (B, L, dm), dtype=jnp.float32), 'norm_w': jnp.ones((nl, dm), dtype=jnp.float32), 'W_in': jax.random.normal(ks[1], (nl, 2 * di, dm), dtype=jnp.float32) * s, 'conv_w': jax.random.normal(ks[2], (nl, di, D_CONV), dtype=jnp.float32) * s, 'conv_b': jnp.zeros((nl, di), dtype=jnp.float32), 'W_x': jax.random.normal(ks[3], (nl, DT_RANK + 2 * D_STATE, di), dtype=jnp.float32) * s, 'W_dt': jax.random.normal(ks[4], (nl, di, DT_RANK), dtype=jnp.float32) * DT_RANK ** (-0.5), 'b_dt': jax.random.normal(ks[5], (nl, di), dtype=jnp.float32) - 3.0, 'A_log': jax.random.uniform(ks[6], (nl, di, D_STATE), dtype=jnp.float32) * 2.0, 'D': jnp.ones((nl, di), dtype=jnp.float32), 'W_out': jax.random.normal(ks[7], (nl, dm, di), dtype=jnp.float32) * s}
    _L0_attn_a_in = _L0_attn_a_setup()

    def _L0_attn_b_setup():
        import math
        import jax, jax.numpy as jnp
        import numpy as np
        N_HEADS = 16

        def _phi(x, rf, m):
            norms_sq = jnp.sum(x * x, axis=-1, keepdims=True)
            proj = jnp.einsum('bhtd,md->bhtm', x, rf)
            scale = jnp.exp(-norms_sq * 0.5) / math.sqrt(m)
            return jnp.concatenate([jnp.cos(proj), jnp.sin(proj)], axis=-1) * scale
        key = jax.random.key(seed)
        ks = jax.random.split(key, 6)
        B, T, D = (2, 512, 128)
        m, dh = (32, D // N_HEADS)
        x = jax.random.normal(ks[0], (B, T, D), dtype=jnp.float32)
        s = 1.0 / math.sqrt(D)
        wq = jax.random.normal(ks[1], (D, D), dtype=jnp.float32) * s
        wk = jax.random.normal(ks[2], (D, D), dtype=jnp.float32) * s
        wv = jax.random.normal(ks[3], (D, D), dtype=jnp.float32) * s
        wo = jax.random.normal(ks[4], (D, D), dtype=jnp.float32) * s
        rf = jax.random.normal(ks[5], (m, dh), dtype=jnp.float32) / math.sqrt(dh)
        return {'x': x, 'wq': wq, 'wk': wk, 'wv': wv, 'wo': wo, 'rf': rf}
    _L0_attn_b_in = _L0_attn_b_setup()

    def _L0_ffn_setup():
        import jax, jax.numpy as jnp
        import numpy as np
        EMBED_DIM = 128
        HIDDEN_DIM = 512
        NUM_EXPERTS = 8
        TOP_K = 2
        key = jax.random.key(seed)
        ks = jax.random.split(key, 4)
        std1 = float(np.sqrt(2.0 / EMBED_DIM))
        std2 = float(np.sqrt(2.0 / HIDDEN_DIM))
        x = jax.random.normal(ks[0], (1, 256, EMBED_DIM), dtype=jnp.float32)
        w_router = jax.random.normal(ks[1], (EMBED_DIM, NUM_EXPERTS), dtype=jnp.float32) * 0.02
        w1 = jax.random.normal(ks[2], (NUM_EXPERTS, EMBED_DIM, HIDDEN_DIM), dtype=jnp.float32) * std1
        b1 = jnp.zeros((NUM_EXPERTS, HIDDEN_DIM), dtype=jnp.float32)
        w2 = jax.random.normal(ks[3], (NUM_EXPERTS, HIDDEN_DIM, EMBED_DIM), dtype=jnp.float32) * std2
        b2 = jnp.zeros((NUM_EXPERTS, EMBED_DIM), dtype=jnp.float32)
        return {'x': x, 'w_router': w_router, 'w1': w1, 'b1': b1, 'w2': w2, 'b2': b2}
    _L0_ffn_in = _L0_ffn_setup()
    _d = {'L0_attn_a_x': _L0_attn_a_in['x'], 'L0_attn_a_norm_w': _L0_attn_a_in['norm_w'], 'L0_attn_a_W_in': _L0_attn_a_in['W_in'], 'L0_attn_a_conv_w': _L0_attn_a_in['conv_w'], 'L0_attn_a_conv_b': _L0_attn_a_in['conv_b'], 'L0_attn_a_W_x': _L0_attn_a_in['W_x'], 'L0_attn_a_W_dt': _L0_attn_a_in['W_dt'], 'L0_attn_a_b_dt': _L0_attn_a_in['b_dt'], 'L0_attn_a_A_log': _L0_attn_a_in['A_log'], 'L0_attn_a_D': _L0_attn_a_in['D'], 'L0_attn_a_W_out': _L0_attn_a_in['W_out'], 'L0_attn_b_wq': _L0_attn_b_in['wq'], 'L0_attn_b_wk': _L0_attn_b_in['wk'], 'L0_attn_b_wv': _L0_attn_b_in['wv'], 'L0_attn_b_wo': _L0_attn_b_in['wo'], 'L0_attn_b_rf': _L0_attn_b_in['rf'], 'L0_ffn_w_router': _L0_ffn_in['w_router'], 'L0_ffn_w1': _L0_ffn_in['w1'], 'L0_ffn_b1': _L0_ffn_in['b1'], 'L0_ffn_w2': _L0_ffn_in['w2'], 'L0_ffn_b2': _L0_ffn_in['b2']}
    _x0 = _d['L0_attn_a_x']
    _d['L0_attn_a_x'] = jax.random.normal(jax.random.fold_in(jax.random.key(seed), 1), (2, 1024, 128), dtype=_x0.dtype)
    del _x0
    return _d

def reference(L0_attn_a_x, L0_attn_a_norm_w, L0_attn_a_W_in, L0_attn_a_conv_w, L0_attn_a_conv_b, L0_attn_a_W_x, L0_attn_a_W_dt, L0_attn_a_b_dt, L0_attn_a_A_log, L0_attn_a_D, L0_attn_a_W_out, L0_attn_b_wq, L0_attn_b_wk, L0_attn_b_wv, L0_attn_b_wo, L0_attn_b_rf, L0_ffn_w_router, L0_ffn_w1, L0_ffn_b1, L0_ffn_w2, L0_ffn_b2):

    def _L0_attn_a_ref(x, norm_w, W_in, conv_w, conv_b, W_x, W_dt, b_dt, A_log, D, W_out):
        import jax, jax.numpy as jnp
        import numpy as np
        N_LAYERS = 4
        D_MODEL = 128
        D_INNER = 256
        DT_RANK = 64
        D_STATE = 16
        D_CONV = 4
        EPS = 1e-05

        def _rms(x, w):
            return x * jax.lax.rsqrt(jnp.mean(x * x, axis=-1, keepdims=True) + EPS) * w

        def _silu(x):
            return x * jax.nn.sigmoid(x)
        nl = W_in.shape[0]
        L = x.shape[1]
        dc = conv_w.shape[-1]
        n = A_log.shape[-1]
        rk = W_dt.shape[-1]

        def combine(left, right):
            a1, b1 = left
            a2, b2 = right
            return (a2 * a1, a2 * b1 + b2)
        for i in range(nl):
            h = _rms(x, norm_w[i])
            xz = jnp.einsum('bld,ed->ble', h, W_in[i])
            xi, z = jnp.split(xz, 2, axis=-1)
            xp = jnp.pad(xi, ((0, 0), (dc - 1, 0), (0, 0)))
            xc = conv_b[i] + sum((xp[:, k:k + L, :] * conv_w[i][:, k] for k in range(dc)))
            xc = _silu(xc)
            dbc = jnp.einsum('bld,ed->ble', xc, W_x[i])
            delta, Bm, Cm = jnp.split(dbc, [rk, rk + n], axis=-1)
            delta = jax.nn.softplus(jnp.einsum('blr,dr->bld', delta, W_dt[i]) + b_dt[i])
            A = -jnp.exp(A_log[i])
            deltaA = jnp.exp(delta[..., None] * A)
            BX = (delta * xc)[..., None] * Bm[:, :, None, :]
            _, hs = jax.lax.associative_scan(combine, (deltaA, BX), axis=1)
            y = jnp.einsum('bldn,bln->bld', hs, Cm) + D[i] * xc
            out = jnp.einsum('bld,ed->ble', y * _silu(z), W_out[i])
            x = x + out
        return x

    def _L0_attn_b_ref(x, wq, wk, wv, wo, rf):
        import math
        import jax, jax.numpy as jnp
        import numpy as np
        N_HEADS = 16

        def _phi(x, rf, m):
            norms_sq = jnp.sum(x * x, axis=-1, keepdims=True)
            proj = jnp.einsum('bhtd,md->bhtm', x, rf)
            scale = jnp.exp(-norms_sq * 0.5) / math.sqrt(m)
            return jnp.concatenate([jnp.cos(proj), jnp.sin(proj)], axis=-1) * scale
        B, T, D = x.shape
        H = N_HEADS
        Dh = D // H
        m = rf.shape[0]

        def heads(w):
            return (x @ w.T).reshape(B, T, H, Dh).transpose(0, 2, 1, 3)
        Q, K, V = (heads(wq), heads(wk), heads(wv))
        Qf = _phi(Q, rf, m)
        Kf = _phi(K, rf, m)
        KV = jnp.einsum('bhnd,bhnv->bhdv', Kf, V)
        QKV = jnp.einsum('bhnd,bhdv->bhnv', Qf, KV)
        K_sum = jnp.sum(Kf, axis=2)
        Z = jnp.maximum(jnp.einsum('bhnd,bhd->bhn', Qf, K_sum)[..., None], 1e-06)
        out = (QKV / Z).transpose(0, 2, 1, 3).reshape(B, T, D)
        return out @ wo.T

    def _L0_ffn_ref(x, w_router, w1, b1, w2, b2):
        import jax, jax.numpy as jnp
        import numpy as np
        EMBED_DIM = 128
        HIDDEN_DIM = 512
        NUM_EXPERTS = 8
        TOP_K = 2
        orig_shape = x.shape
        xf = x.reshape(-1, EMBED_DIM)
        logits = xf @ w_router
        probs = jax.nn.softmax(logits, axis=-1)
        topk_w, topk_idx = jax.lax.top_k(probs, TOP_K)
        mask = jax.nn.one_hot(topk_idx, NUM_EXPERTS, dtype=xf.dtype)
        weights = jnp.sum(topk_w[..., None] * mask, axis=1)
        h = jnp.einsum('te,ieh->tih', xf, w1) + b1
        h = jax.nn.gelu(h)
        out = jnp.einsum('tih,ihe->tie', h, w2) + b2
        out = jnp.sum(out * weights[..., None], axis=1)
        return out.reshape(orig_shape)
    x = L0_attn_a_x
    x = x + _L0_attn_a_ref(_layernorm(x, axis=-1), L0_attn_a_norm_w, L0_attn_a_W_in, L0_attn_a_conv_w, L0_attn_a_conv_b, L0_attn_a_W_x, L0_attn_a_W_dt, L0_attn_a_b_dt, L0_attn_a_A_log, L0_attn_a_D, L0_attn_a_W_out)
    x = x + _L0_ffn_ref(_layernorm(x, axis=-1), L0_ffn_w_router, L0_ffn_w1, L0_ffn_b1, L0_ffn_w2, L0_ffn_b2)
    x = x + _L0_attn_b_ref(_layernorm(x, axis=-1), L0_attn_b_wq, L0_attn_b_wk, L0_attn_b_wv, L0_attn_b_wo, L0_attn_b_rf)
    x = x + _L0_ffn_ref(_layernorm(x, axis=-1), L0_ffn_w_router, L0_ffn_w1, L0_ffn_b1, L0_ffn_w2, L0_ffn_b2)
    return x

_drawn_inputs = setup_inputs


def setup_inputs(seed=0):
    import zlib

    import numpy as np

    out = dict(_drawn_inputs(seed))
    spreads = {'L0_attn_a_norm_w': (1.0, 0.6),
     'L0_attn_a_conv_b': (0.0, 0.66),
     'L0_attn_a_D': (1.0, 0.6),
     'L0_ffn_b1': (0.0, 2.0),
     'L0_ffn_b2': (0.0, 2.0)}
    factors = {'L0_attn_a_W_in': 7.481,
     'L0_attn_a_conv_w': 8.0,
     'L0_attn_a_W_x': 8.0,
     'L0_attn_a_W_dt': 8.0,
     'L0_attn_a_b_dt': 8.0,
     'L0_attn_a_A_log': 8.0,
     'L0_attn_a_W_out': 5.838,
     'L0_attn_b_wq': 64.0,
     'L0_attn_b_wk': 64.0,
     'L0_attn_b_wv': 64.0,
     'L0_attn_b_wo': 64.0,
     'L0_attn_b_rf': 64.0,
     'L0_ffn_w_router': 8.0,
     'L0_ffn_w1': 8.0,
     'L0_ffn_w2': 8.0}
    for name, (base, spread) in spreads.items():
        noise = np.random.default_rng([zlib.crc32(name.encode()), seed]).standard_normal(out[name].shape)
        drawn = base * np.exp(spread * noise) if base else spread * noise
        out[name] = jnp.asarray(drawn.astype(out[name].dtype))
    for name, factor in factors.items():
        out[name] = (out[name] * factor).astype(out[name].dtype)
    return out
```

```python
from contextlib import ExitStack

import numpy as np
import concourse.bass as bass
from concourse import mybir

ALU = mybir.AluOpType
ACT = mybir.ActivationFunctionType
AX = mybir.AxisListType
F32 = mybir.dt.float32
BF16 = mybir.dt.bfloat16

P = 128
BATCH, SEQ = 2, 1024
TOK = BATCH * SEQ
T = 512
CHUNKS = TOK // T
EPS = 1e-5

LAYERS = 4
INNER = 256
HALVES = INNER // P
RANK = 64
STATES = 16
TAPS = 4
PAIRS = LAYERS * BATCH
NPAR = 3
RING = 4
POOL_N = (1, 4, 7, 9, 12, 14)
DVE_N = tuple(n for n in range(STATES) if n not in POOL_N)

EXPERTS = 8
HIDDEN = 512
HB = HIDDEN // P
EW = HIDDEN + HB * P + HB + 1

HEADS = 16
DH = P // HEADS
M = 32
HG = P // M
GROUPS = HEADS // HG
VW = DH + 1

A_RF = 4 * P
A_HS = A_RF + HEADS * M
A_MASK = A_HS + HEADS
AW = A_MASK + HG * VW

O_WX = 2 * INNER
WX = NPAR * 2 * STATES + RANK
O_NORM = O_WX + HALVES * WX
O_CB = O_NORM + 1
O_BDT = O_CB + HALVES
PW = O_BDT + HALVES
OW = HALVES * P + HALVES

C_EPS, C_M1, C_M2, C_HPI, NCONST = 0, 1, 2, 3, 4


class Group:
    pass


def wait(eng, sem, value):
    if isinstance(value, int) and value <= 0:
        return
    eng.wait_ge(sem, value)


def norm_semaphores(sem, phase):
    s = Group()
    s.mean = sem(phase + "_mean")
    s.cen = sem(phase + "_cen")
    s.sq = sem(phase + "_sq")
    s.var = sem(phase + "_var")
    s.ln = sem(phase + "_ln")
    s.rstd = sem(phase + "_rstd")
    s.out = sem(phase + "_out")
    return s


def ln_tensor(pe, s, k, bufs, r):
    for c in range(CHUNKS):
        n = CHUNKS * r + c
        wait(pe, s.cen, n)
        pe.matmul(bufs.ps[0][:], k.mean_w[:], k.x(c), start=True, stop=True).then_inc(s.mean, 1)
        pe.wait_ge(s.sq, n + 1)
        wait(pe, s.ln, n)
        pe.matmul(bufs.ps[1][:], k.mean_w[:], bufs.sq[:], start=True, stop=True).then_inc(s.var, 1)


def ln_scalar(act, s, k, bufs, r):
    for c in range(CHUNKS):
        n = CHUNKS * r + c
        act.wait_ge(s.cen, n + 1)
        wait(act, s.var, n)
        act.activation(bufs.sq[:], bufs.cen[:, c % 2, :], ACT.Square).then_inc(s.sq, 1)
        act.wait_ge(s.var, n + 1)
        wait(act, s.out, n - 1)
        act.activation(bufs.rs[:, c % 2, :], bufs.ps[1][:], ACT.Ln, bias=k.const[:, C_EPS:C_EPS + 1]).then_inc(s.ln, 1)
        act.wait_ge(s.ln, n + 1)
        act.activation(bufs.rs[:, c % 2, :], bufs.rs[:, c % 2, :], ACT.Exp, scale=-0.5).then_inc(s.rstd, 1)


def ln_vector(dve, s, k, bufs, r, out, out_sem=None):
    for c in range(CHUNKS + 1):
        n = CHUNKS * r + c
        if c < CHUNKS:
            dve.wait_ge(s.mean, n + 1)
            wait(dve, s.out, n - 1)
            dve.tensor_tensor(bufs.cen[:, c % 2, :], k.x(c), bufs.ps[0][:], ALU.subtract).then_inc(s.cen, 1)
        if c >= 1:
            dve.wait_ge(s.rstd, n)
            b = (c - 1) % 2
            dve.tensor_tensor(out[:, (c - 1) * T:c * T], bufs.cen[:, b, :], bufs.rs[:, b, :], ALU.mult).then_inc(s.out, 1)
            if out_sem:
                dve.wait_ge(s.out, n)
                dve.sem_inc(out_sem, 1)


STEPS = CHUNKS
TB = TOK // P


def expert_semaphores(sem, phase):
    s = Group()
    s.w0 = sem(phase + "_w0")
    s.w1 = sem(phase + "_w1")
    s.logits = sem(phase + "_logits")
    s.shift = sem(phase + "_shift")
    s.ex = sem(phase + "_ex")
    s.route = sem(phase + "_route")
    s.wlo = sem(phase + "_wlo")
    s.wT_ps = sem(phase + "_wT_ps")
    s.wT = sem(phase + "_wT")
    s.wb_ps = sem(phase + "_wb_ps")
    s.wb = sem(phase + "_wb")
    s.h_ps = sem(phase + "_h_ps")
    s.gel = sem(phase + "_gel")
    s.y_ps = sem(phase + "_y_ps")
    s.part = sem(phase + "_part")
    s.acc = sem(phase + "_acc")
    return s


def rows3(t):
    return t[:].rearrange("p (b e) -> p b e", e=EXPERTS)


def per_block(t):
    return t[:].rearrange("p (b o) -> p b o", o=1).broadcast_to([P, TB, EXPERTS])


def ffn_loads(sp, s, k, f, d):
    sp.dma_start(f.w[0][:], d.ew[0]).then_inc(s.w0, 16)
    sp.dma_start(f.w[1][:], d.ew[1]).then_inc(s.w1, 16)
    with sp.Fori(1, EXPERTS // 2) as ep:
        for i, ws in enumerate((s.w0, s.w1)):
            e = 2 * ep + i
            sp.wait_ge(s.part, STEPS * (e - 1))
            sp.dma_start(f.w[i][:], d.ew[e]).then_inc(ws, 16)


def ffn_tensor(pe, s, k, f, xn, ln_out, r):
    pe.wait_ge(ln_out, CHUNKS * (r + 1))
    for b in range(TB):
        mm = pe.matmul(f.ps[0][:, b * EXPERTS:(b + 1) * EXPERTS], xn[:, b * P:(b + 1) * P], f.wr[:],
                       start=True, stop=True)
    mm.then_inc(s.logits, 1)
    pe.wait_ge(s.wlo, 1)
    for half in range(2):
        wT = f.ps[half][0:NPAR * EXPERTS, :].bitcast(BF16)
        for b in range(TB // 2):
            mm = pe.transpose(wT[:, b * P:(b + 1) * P], f.w3[:, half * TB // 2 + b, :], k.ident_b[:])
        mm.then_inc(s.wT_ps, 1)
    for i in range(EXPERTS * STEPS):
        e, t = i // STEPS, i % STEPS
        if i < 2:
            pe.wait_ge(s.wT, 2)
        wait(pe, s.wb, i - 1)
        pe.matmul(f.ps[i % 2][:], f.e_sel[:, e, :], f.wT[:, t * T:(t + 1) * T],
                  start=True, stop=True).then_inc(s.wb_ps, 1)

    def hidden(ep, i):
        w, t = f.w[i // STEPS], i % STEPS
        g = 2 * STEPS * ep + i
        if t == 0:
            pe.wait_ge((s.w0, s.w1)[i // STEPS], 16 * ep + 16)
        for b in range(HB):
            wait(pe, s.gel, HB * (g - 1) + b + 1)
            pe.matmul(f.h_ps[b][:], w[:, b * P:(b + 1) * P], xn[:, t * T:(t + 1) * T],
                      start=True, stop=True).then_inc(s.h_ps, 1)

    def output(ep, i):
        w = f.w[i // STEPS]
        g = 2 * STEPS * ep + i
        wait(pe, s.part, g - 1)
        for b in range(HB):
            pe.wait_ge(s.gel, HB * g + b + 1)
            mm = pe.matmul(f.y_ps[i % 2][:], w[:, HIDDEN + b * P:HIDDEN + (b + 1) * P], f.g[:, i % 2, b, :],
                           start=(b == 0), stop=(b == HB - 1))
        mm.then_inc(s.y_ps, 1)

    def pair(ep, last):
        for i in range(2 * STEPS):
            if i + 1 < 2 * STEPS:
                hidden(ep, i + 1)
            elif not last:
                hidden(ep + 1, 0)
            output(ep, i)

    hidden(0, 0)
    pair(0, False)
    with pe.Fori(1, EXPERTS // 2 - 1) as ep:
        pair(ep, False)
    pair(EXPERTS // 2 - 1, True)


def ffn_scalar(act, s, k, f):
    act.wait_ge(s.shift, 1)
    act.activation(f.ex[:], f.sh[:], ACT.Exp).then_inc(s.ex, 1)
    for i in range(EXPERTS * STEPS):
        act.wait_ge(s.wb_ps, i + 1)
        act.activation(f.wb[:, i * T:(i + 1) * T], f.ps[i % 2][:], ACT.Copy).then_inc(s.wb, 1)

    def pair(ep):
        for i in range(2 * STEPS):
            g = 2 * STEPS * ep + i
            wait(act, s.y_ps, g - 1)
            for b in range(HB):
                act.wait_ge(s.h_ps, HB * g + b + 1)
                act.activation(f.g[:, i % 2, b, :], f.h_ps[b][:], ACT.Gelu_apprx_tanh,
                               bias=f.w[i // STEPS][:, HIDDEN + HB * P + b:HIDDEN + HB * P + b + 1]).then_inc(s.gel, 1)

    pair(0)
    with act.Fori(1, EXPERTS // 2) as ep:
        pair(ep)


def ffn_vector(dve, s, k, f, x):
    lg = f.ps[0][:, 0:TB * EXPERTS].rearrange("p (b e) -> p b e", e=EXPERTS)
    rank = k.rank[:].rearrange("p (b e) -> p b e", e=EXPERTS)
    done = 0

    def chained(instruction):
        nonlocal done
        done += 1
        instruction.then_inc(s.route, 1)
        dve.wait_ge(s.route, done)

    dve.wait_ge(s.logits, 1)
    chained(dve.tensor_reduce(f.c[0][:], lg, AX.X, ALU.max))
    dve.tensor_tensor(rows3(f.sh), lg, per_block(f.c[0]), ALU.subtract).then_inc(s.shift, 1)
    dve.wait_ge(s.ex, 1)
    chained(dve.tensor_reduce(f.c[1][:], rows3(f.ex), AX.X, ALU.add))
    chained(dve.reciprocal(f.c[2][:], f.c[1][:]))
    chained(dve.tensor_tensor(rows3(f.p), rows3(f.ex), per_block(f.c[2]), ALU.mult))

    def largest(p, cm, cc, eq, sel):
        chained(dve.tensor_reduce(cm[:], rows3(p), AX.X, ALU.max))
        chained(dve.tensor_tensor(rows3(eq), rows3(p), per_block(cm), ALU.is_equal))
        chained(dve.tensor_tensor(rows3(eq), rows3(eq), rank, ALU.mult))
        chained(dve.tensor_reduce(cc[:], rows3(eq), AX.X, ALU.max))
        chained(dve.tensor_tensor(rows3(sel), rows3(eq), per_block(cc), ALU.is_equal))

    largest(f.p, f.c[3], f.c[4], f.eq[0], f.sel[0])
    chained(dve.scalar_tensor_tensor(out=f.p2[:], in0=f.sel[0][:], scalar=-2.0, in1=f.p[:],
                                     op0=ALU.mult, op1=ALU.add))
    largest(f.p2, f.c[5], f.c[6], f.eq[1], f.sel[1])
    chained(dve.tensor_tensor(f.both[:], f.sel[0][:], f.sel[1][:], ALU.add))
    chained(dve.tensor_tensor(f.wt[:], f.both[:], f.p[:], ALU.mult))
    chained(dve.tensor_copy(f.w3[:, :, 0:EXPERTS], rows3(f.wt)))
    chained(dve.tensor_tensor(rows3(f.wr1), rows3(f.wt), f.w3[:, :, 0:EXPERTS], ALU.subtract))
    chained(dve.tensor_copy(f.w3[:, :, EXPERTS:2 * EXPERTS], rows3(f.wr1)))
    dve.tensor_tensor(f.w3[:, :, 2 * EXPERTS:], rows3(f.wr1), f.w3[:, :, EXPERTS:2 * EXPERTS],
                      ALU.subtract).then_inc(s.wlo, 1)
    for half in range(2):
        dve.wait_ge(s.wT_ps, half + 1)
        dve.tensor_copy(f.wT[:, half * SEQ:(half + 1) * SEQ],
                        f.ps[half][0:NPAR * EXPERTS, :].bitcast(BF16)).then_inc(s.wT, 1)
    dve.wait_ge(s.wb, EXPERTS * STEPS)

    def pair(ep):
        for i in range(2 * STEPS):
            t = i % STEPS
            g = 2 * STEPS * ep + i
            off = (2 * ep + i // STEPS) * TOK + t * T
            cols = slice(off, off + T) if isinstance(off, int) else bass.ds(off, T)
            dve.wait_ge(s.y_ps, g + 1)
            wait(dve, s.acc, g - 1)
            dve.scalar_tensor_tensor(out=f.part[:, i % 2, :], in0=f.y_ps[i % 2][:],
                                     scalar=f.w[i // STEPS][:, EW - 1:EW], in1=f.wb[:, cols],
                                     op0=ALU.add, op1=ALU.mult).then_inc(s.part, 1)
            dve.wait_ge(s.part, g + 1)
            xc = x[:, t * T:(t + 1) * T]
            dve.tensor_tensor(xc, xc, f.part[:, i % 2, :], ALU.add).then_inc(s.acc, 1)

    pair(0)
    with dve.Fori(1, EXPERTS // 2) as ep:
        pair(ep)


UNITS = 2 * TB
INV2PI = float(np.float32(1 / (2 * np.pi)))
MAGIC = float(1.5 * 2 ** 23)
PI2_A = 6.28125
PI2_B = float(np.float32(2 * np.pi - PI2_A))
PI2_C = float(np.float32(2 * np.pi - PI2_A - PI2_B))
PI_BELOW = 3.1415925


def attention_semaphores(sem, phase):
    s = Group()
    s.w = sem(phase + "_w")
    s.qk_ps = sem(phase + "_qk_ps")
    s.qk = sem(phase + "_qk")
    s.sq = sem(phase + "_sq")
    s.nrm_ps = sem(phase + "_nrm_ps")
    s.ex = sem(phase + "_ex")
    s.sc = sem(phase + "_sc")
    s.v_ps = sem(phase + "_v_ps")
    s.vs = sem(phase + "_vs")
    s.va = sem(phase + "_va")
    s.f_ps = sem(phase + "_f_ps")
    s.t1 = sem(phase + "_t1")
    s.kk = sem(phase + "_kk")
    s.r1 = sem(phase + "_r1")
    s.r2 = sem(phase + "_r2")
    s.r3 = sem(phase + "_r3")
    s.r = sem(phase + "_r")
    s.sn = sem(phase + "_sn")
    s.ab = sem(phase + "_ab")
    s.cs = sem(phase + "_cs")
    s.kv_ps = sem(phase + "_kv_ps")
    s.kvm = sem(phase + "_kvm")
    s.o_ps = sem(phase + "_o_ps")
    s.on = sem(phase + "_on")
    s.oz = sem(phase + "_oz")
    s.orz = sem(phase + "_orz")
    s.od = sem(phase + "_od")
    s.oT_ps = sem(phase + "_oT_ps")
    s.oT = sem(phase + "_oT")
    s.fin_ps = sem(phase + "_fin_ps")
    s.fin = sem(phase + "_fin")
    return s


def att_loads(sp, s, k, a, d):
    sp.dma_start(a.w[:], d.aw).then_inc(s.w, 16)


def unit_of(u):
    if u < TB:
        return True, u // (TB // BATCH), u // 4, u
    return False, (u - TB) // (UNITS // 4), (u - TB) // GROUPS, (u - TB) % GROUPS


def att_tensor(pe, s, k, a, xn, ln_out, r):
    pe.wait_ge(s.w, 16)
    pe.wait_ge(ln_out, CHUNKS * (r + 1))
    for c in range(CHUNKS):
        for i in range(2):
            wait(pe, s.sq, 2 * (c - 1) + i + 1)
            pe.matmul(a.ps[i][:], a.w[:, i * P:(i + 1) * P], xn[:, c * T:(c + 1) * T],
                      start=True, stop=True).then_inc(s.qk_ps, 1)
    pe.wait_ge(s.sq, 2 * CHUNKS)
    for i in range(2):
        for b in range(TB):
            o = (i * TB + b) * HEADS
            mm = pe.matmul(a.kv_ps[0][:, o:o + HEADS], a.sq[:, i, b * P:(b + 1) * P], a.w[:, A_HS:A_HS + HEADS],
                           start=True, stop=True)
    mm.then_inc(s.nrm_ps, 1)
    for c in range(CHUNKS):
        wait(pe, s.vs, c - 1)
        for b in range(4):
            mm = pe.matmul(a.ps[c % 2][:, b * P:(b + 1) * P], xn[:, c * T + b * P:c * T + (b + 1) * P],
                           a.w[:, 2 * P:3 * P], start=True, stop=True)
        mm.then_inc(s.v_ps, 1)

    def angles(u):
        key, b, c, i = unit_of(u)
        wait(pe, s.r1, u - 1)
        if key:
            pe.matmul(a.f_ps[u % 2][:], a.qk[:, 1, i * P:(i + 1) * P], a.w[:, A_RF:A_RF + HEADS * M],
                      start=True, stop=True).then_inc(s.f_ps, 1)
        else:
            pe.matmul(a.f_ps[u % 2][:], a.w[:, A_RF + i * P:A_RF + (i + 1) * P], a.qk[:, 0, c * T:(c + 1) * T],
                      start=True, stop=True).then_inc(s.f_ps, 1)

    def keys(u):
        _, b, _, i = unit_of(u)
        per = TB // BATCH
        if i == 0:
            pe.wait_ge(s.sc, 4)
            pe.wait_ge(s.va, CHUNKS)
        for j, (trig, done) in enumerate(((a.cs, s.cs), (a.sn, s.sn))):
            pe.wait_ge(done, u + 1)
            for g in range(GROUPS):
                o = (j * GROUPS + g) * HG * VW
                mm = pe.matmul(a.kv_ps[b][:, o:o + HG * VW], trig[:, u % 2, g * P:(g + 1) * P],
                               a.va[:, i, g * HG * VW:(g + 1) * HG * VW],
                               start=(i % per == 0 and j == 0 and g == 0), stop=(i % per == per - 1),
                               skip_group_check=True)
        mm.then_inc(s.kv_ps, 1)

    def queries(u):
        _, b, c, g = unit_of(u)
        pe.wait_ge(s.kvm, b + 1)
        pe.wait_ge(s.cs, u + 1)
        pe.wait_ge(s.sn, u + 1)
        if g == 0:
            wait(pe, s.on, 2 * c)
        for t in range(4):
            o = (t % 2) * HEADS * VW + g * HG * VW
            for j, trig in enumerate((a.cs, a.sn)):
                mm = pe.matmul(a.o_ps[t // 2][:, o:o + HG * VW], trig[:, u % 2, t * P:(t + 1) * P],
                               a.kvm[:, b, j * GROUPS + g, :], start=(j == 0), stop=(j == 1),
                               skip_group_check=True)
        mm.then_inc(s.o_ps, 1)

    def out(c):
        pe.wait_ge(s.od, c + 1)
        wait(pe, s.oT, c)
        for t in range(4):
            mm = pe.transpose(a.ps[0][:, t * P:(t + 1) * P], a.od[:, t, :], k.ident[:])
        mm.then_inc(s.oT_ps, 1)
        pe.wait_ge(s.oT, c + 1)
        wait(pe, s.fin, c)
        pe.matmul(a.ps[1][:], a.w[:, 3 * P:4 * P], a.oT[:], start=True, stop=True).then_inc(s.fin_ps, 1)

    angles(0)
    for u in range(UNITS):
        key, b, c, i = unit_of(u)
        if u + 1 < UNITS:
            angles(u + 1)
        if key:
            keys(u)
        else:
            queries(u)
            if i == GROUPS - 1:
                out(c)


def att_scalar(act, s, k, a):
    for c in range(CHUNKS):
        for i in range(2):
            n = 2 * c + i
            act.wait_ge(s.qk_ps, n + 1)
            act.activation(a.qk[:, i, c * T:(c + 1) * T], a.ps[i][:], ACT.Copy).then_inc(s.qk, 1)
            act.activation(a.sq[:, i, c * T:(c + 1) * T], a.ps[i][:], ACT.Square).then_inc(s.sq, 1)
    act.wait_ge(s.nrm_ps, 1)
    act.activation(a.ex[:], a.kv_ps[0][:], ACT.Exp, scale=-0.5).then_inc(s.ex, 1)
    for u in range(UNITS + 1):
        if u >= 1:
            key, b, c, i = unit_of(u - 1)
            if not key and i == GROUPS - 1:
                act.wait_ge(s.oT_ps, c + 1)
                act.activation(a.oT[:], a.ps[0][:], ACT.Copy).then_inc(s.oT, 1)
        if u == UNITS:
            break
        act.wait_ge(s.r, u + 1)
        if u >= 2:
            key = unit_of(u - 2)[0]
            act.wait_ge(s.kv_ps if key else s.o_ps, u - 1 if key else u - 1 - TB)
        act.activation(a.sn[:, u % 2, :], a.r[:, u % 2, :], ACT.Sin).then_inc(s.sn, 1)
        wait(act, s.cs, u)
        act.activation(a.ab[:], a.r[:, u % 2, :], ACT.Abs).then_inc(s.ab, 1)
        act.wait_ge(s.ab, u + 1)
        act.activation(a.cs[:, u % 2, :], a.ab[:], ACT.Sin, bias=k.const[:, C_HPI:C_HPI + 1],
                       scale=-1.0).then_inc(s.cs, 1)


def att_vector(dve, s, k, a, x):
    dve.wait_ge(s.ex, 1)
    dve.tensor_scalar(a.sc[:], a.ex[:], float(M) ** -0.5, None, ALU.mult).then_inc(s.sc, 1)
    dve.wait_ge(s.sc, 1)
    ks = a.sc[:, TB * HEADS:].rearrange("p (b h o) -> p b h o", h=HEADS, o=1)
    va = a.va[:].rearrange("p b (h v) -> p b h v", v=VW)
    for part in range(1):
        dve.tensor_copy(va[:, :, :, DH:VW], ks).then_inc(s.sc, 3)
    for c in range(CHUNKS):
        dve.wait_ge(s.v_ps, c + 1)
        for b in range(4):
            i = dve.tensor_tensor(va[:, 4 * c + b, :, 0:DH],
                                  a.ps[c % 2][:, b * P:(b + 1) * P].rearrange("p (h v) -> p h v", v=DH),
                                  ks[:, 4 * c + b, :, :].broadcast_to([P, HEADS, DH]), ALU.mult)
        i.then_inc(s.vs, 1)
        dve.wait_ge(s.vs, c + 1)
        dve.sem_inc(s.va, 1)

    def reduce(u):
        b = u % 2
        dve.wait_ge(s.f_ps, u + 1)
        dve.tensor_scalar(a.t1[:], a.f_ps[b][:], INV2PI, MAGIC, ALU.mult, ALU.add).then_inc(s.t1, 1)
        dve.wait_ge(s.t1, u + 1)
        dve.tensor_scalar(a.t1[:], a.t1[:], MAGIC, None, ALU.subtract).then_inc(s.kk, 1)
        dve.wait_ge(s.kk, u + 1)
        wait(dve, s.cs, u - 1)
        dve.scalar_tensor_tensor(out=a.r[:, b, :], in0=a.t1[:], scalar=-PI2_A, in1=a.f_ps[b][:],
                                 op0=ALU.mult, op1=ALU.add).then_inc(s.r1, 1)
        dve.wait_ge(s.r1, u + 1)
        dve.scalar_tensor_tensor(out=a.r[:, b, :], in0=a.t1[:], scalar=-PI2_B, in1=a.r[:, b, :],
                                 op0=ALU.mult, op1=ALU.add).then_inc(s.r2, 1)
        dve.wait_ge(s.r2, u + 1)
        dve.scalar_tensor_tensor(out=a.r[:, b, :], in0=a.t1[:], scalar=-PI2_C, in1=a.r[:, b, :],
                                 op0=ALU.mult, op1=ALU.add).then_inc(s.r3, 1)
        dve.wait_ge(s.r3, u + 1)
        dve.tensor_scalar(a.r[:, b, :], a.r[:, b, :], PI_BELOW, -PI_BELOW, ALU.min, ALU.max).then_inc(s.r, 1)

    def mask_kv(b):
        dve.wait_ge(s.kv_ps, (b + 1) * (TB // BATCH))
        w = HG * VW
        dve.tensor_tensor(a.kvm[:, b], a.kv_ps[b][:, 0:2 * GROUPS * w].rearrange("p (g v) -> p g v", v=w),
                          a.w[:, A_MASK:A_MASK + w].rearrange("p (o v) -> p o v", o=1).broadcast_to([P, 2 * GROUPS, w]),
                          ALU.mult).then_inc(s.kvm, 1)

    def divide(c):
        dve.wait_ge(s.o_ps, GROUPS * (c + 1))
        qs = a.sc[:, 4 * c * HEADS:4 * (c + 1) * HEADS].rearrange("p (h o) -> p h o", o=1)
        on = a.on[:].rearrange("p (h v) -> p h v", v=VW)
        n = 2 * HEADS
        wait(dve, s.od, c)
        for t in range(2):
            dve.tensor_tensor(on[:, t * n:(t + 1) * n, :],
                              a.o_ps[t][:, 0:n * VW].rearrange("p (h v) -> p h v", v=VW),
                              qs[:, t * n:(t + 1) * n, :].broadcast_to([P, n, VW]), ALU.mult).then_inc(s.on, 1)
        dve.wait_ge(s.on, 2 * c + 2)
        dve.tensor_scalar(a.z[:].rearrange("p (h o) -> p h o", o=1), on[:, :, DH:VW], 1e-6, None,
                          ALU.max).then_inc(s.oz, 1)
        dve.wait_ge(s.oz, c + 1)
        dve.reciprocal(a.rz[:], a.z[:]).then_inc(s.orz, 1)
        dve.wait_ge(s.orz, c + 1)
        wait(dve, s.oT_ps, c)
        dve.tensor_tensor(a.od[:].rearrange("p t (h v) -> p (t h) v", v=DH), on[:, :, 0:DH],
                          a.rz[:].rearrange("p (h o) -> p h o", o=1).broadcast_to([P, 4 * HEADS, DH]),
                          ALU.mult).then_inc(s.od, 1)

    def residual(c):
        dve.wait_ge(s.fin_ps, c + 1)
        xc = x[:, c * T:(c + 1) * T]
        dve.tensor_tensor(xc, xc, a.ps[1][:], ALU.add).then_inc(s.fin, 1)

    for u in range(UNITS):
        key, b, c, i = unit_of(u)
        reduce(u)
        if u >= 1:
            key, b, c, i = unit_of(u - 1)
            if key and i % (TB // BATCH) == TB // BATCH - 1:
                mask_kv(b)
            if not key and i == GROUPS - 1:
                divide(c)
                residual(c)
    divide(CHUNKS - 1)
    residual(CHUNKS - 1)


def state_space_semaphores(sem, phase):
    s = Group()
    s.wp = sem(phase + "_wp")
    s.wa = sem(phase + "_wa")
    s.wo = sem(phase + "_wo")
    s.weff = sem(phase + "_weff")
    s.x = sem(phase + "_x")
    s.sq = sem(phase + "_sq")
    s.ms = sem(phase + "_ms")
    s.ln = sem(phase + "_ln")
    s.rstd = sem(phase + "_rstd")
    s.pad = sem(phase + "_pad")
    s.hn = sem(phase + "_hn")
    s.xc_ps = sem(phase + "_xc_ps")
    s.xc = sem(phase + "_xc")
    s.z_ps = sem(phase + "_z_ps")
    s.z = sem(phase + "_z")
    s.bcp_ps = sem(phase + "_bcp_ps")
    s.dtr_ps = sem(phase + "_dtr_ps")
    s.hi = sem(phase + "_hi")
    s.dtr = sem(phase + "_dtr")
    s.r1 = sem(phase + "_r1")
    s.mid = sem(phase + "_mid")
    s.bc = sem(phase + "_bc")
    s.d_ps = sem(phase + "_d_ps")
    s.xb = sem(phase + "_xb")
    s.ab = sem(phase + "_ab")
    s.ey = sem(phase + "_ey")
    s.ll = sem(phase + "_ll")
    s.dd = sem(phase + "_dd")
    s.t = sem(phase + "_t")
    s.s1 = sem(phase + "_s1")
    s.delta = sem(phase + "_delta")
    s.u = sem(phase + "_u")
    s.a1 = sem(phase + "_a1")
    s.aneg = sem(phase + "_aneg")
    s.bc_ps = sem(phase + "_bc_ps")
    s.bcs = sem(phase + "_bcs")
    s.a = sem(phase + "_a")
    s.bx = sem(phase + "_bx")
    s.h = sem(phase + "_h")
    s.carry = sem(phase + "_carry")
    s.pd = sem(phase + "_pd")
    s.pp = sem(phase + "_pp")
    s.y_acc = sem(phase + "_y_acc")
    s.yd = sem(phase + "_yd")
    s.gate = sem(phase + "_gate")
    s.out_ps = sem(phase + "_out_ps")
    return s


def build(nc, d):
    with ExitStack() as keep:
        def sb(name, shape, dt=F32, where=keep):
            return where.enter_context(nc.sbuf_tensor(name, shape, dt))

        def psum(name, shape, dt=F32, where=keep):
            return where.enter_context(nc.psum_tensor(name, shape, dt))

        k = Group()
        x0 = sb("x0", [P, TOK])
        xn = sb("xn", [P, TOK])
        k.mean_w = sb("mean_w", [P, P])
        k.const = sb("const", [P, NCONST])
        k.ident = sb("ident", [P, P])
        k.ident_b = sb("ident_b", [P, P], BF16)
        k.rank = sb("rank", [P, TOK // P * EXPERTS])
        e_sel = sb("e_sel", [NPAR * EXPERTS, EXPERTS, P], BF16)
        ln = Group()
        ln.sq = sb("ln_sq", [P, T])
        ln.cen = sb("ln_cen", [P, 2, T])
        ln.rs = sb("ln_rs", [P, 2, T])
        bank = [psum(f"bank{i}", [P, T]) for i in range(2)]
        ln.ps = bank

        def sem(name):
            return keep.enter_context(nc.semaphore(name))

        io = Group()
        io.x, io.consts, io.stored, io.merged, io.wr = (sem("io_" + n) for n in ("x", "consts", "stored", "merged", "wr"))

        m = Group()
        scope = ExitStack()
        def mb(name, shape, dt=F32):
            return sb("m_" + name, shape, dt, scope)
        bc_sel = mb("bc_sel", [NPAR * 2 * STATES, 2 * STATES, P], BF16)
        y_ps = psum("m_y_ps", [P, HALVES, T], F32, scope)
        bc_ps = [psum(f"m_bc_ps{i}", [P, 2, T], F32, scope) for i in range(2)]
        m.wp = mb("wp", [P, PW])
        m.wdt = mb("wdt", [RANK, INNER])
        m.cw = mb("cw", [P, TAPS * INNER])
        m.weff = mb("weff", [P, TAPS, INNER])
        m.wo = mb("wo", [P, OW])
        m.alog = mb("alog", [P, HALVES * STATES])
        m.a1 = mb("a1", [P, HALVES * STATES])
        m.aneg = mb("aneg", [P, HALVES * STATES])
        m.sq = mb("sq", [P, T])
        m.lnv = mb("lnv", [P, T])
        m.rstd = mb("rstd", [P, T])
        m.hn = mb("hn", [P, TAPS - 1 + SEQ])
        m.xc = mb("xc", [P, 2, HALVES, T])
        m.z = mb("z", [P, 2, HALVES, T])
        m.hi = mb("hi", [NPAR * 2 * STATES, T], BF16)
        m.mid = mb("mid", [NPAR * 2 * STATES, T], BF16)
        m.r1 = mb("r1", [NPAR * 2 * STATES, T])
        m.bc = mb("bc", [NPAR * 2 * STATES, 2, T], BF16)
        m.dtr = mb("dtr", [RANK, T])
        m.xb = mb("xb", [P, HALVES, T])
        m.ab = mb("ab", [P, HALVES, T])
        m.ey = mb("ey", [P, HALVES, T])
        m.ll = m.ab
        m.dd = mb("dd", [P, HALVES, T])
        m.delta = mb("delta", [P, 2, HALVES, T])
        m.u = mb("u", [P, 2, HALVES, T])
        m.a = mb("a", [P, RING, HALVES, T])
        m.bcs = mb("bcs", [P, RING, 2, T])
        m.bx = mb("bx", [P, RING, HALVES, T])
        m.h = mb("h", [P, RING, HALVES, T])
        m.p = mb("p", [P, RING, HALVES, T])
        m.carry = mb("carry", [P, HALVES, STATES])
        m.yd = mb("yd", [P, HALVES, T])
        m.yg = m.yd
        scope.close()
        s = state_space_semaphores(sem, "m")


        f = Group()
        scope = ExitStack()
        def fb(name, shape, dt=F32):
            return sb("f_" + name, shape, dt, scope)
        f.w = [fb(f"w{i}", [P, EW]) for i in range(2)]
        f.wr = fb("wr", [P, EXPERTS])
        f.wb = fb("wb", [P, EXPERTS * TOK])
        f.wT = fb("wT", [NPAR * EXPERTS, TOK], BF16)
        f.g = fb("g", [P, 2, HB, T])
        f.part = fb("part", [P, 2, T])
        f.c = [fb(f"c{i}", [P, TB]) for i in range(7)]
        f.sh, f.ex, f.p, f.p2, f.both, f.wt, f.wr1 = (
            fb(n, [P, TB * EXPERTS]) for n in ("sh", "ex", "p", "p2", "both", "wt", "wr1"))
        f.eq = [fb(f"eq{i}", [P, TB * EXPERTS]) for i in range(2)]
        f.sel = [fb(f"sel{i}", [P, TB * EXPERTS]) for i in range(2)]
        f.w3 = fb("w3", [P, TB, NPAR * EXPERTS], BF16)
        f.e_sel = e_sel
        f.h_ps = [psum(f"f_h_ps{i}", [P, T], F32, scope) for i in range(HB)]
        f.y_ps = [psum(f"f_y_ps{i}", [P, T], F32, scope) for i in range(2)]
        f.ps = bank
        scope.close()

        a = Group()
        scope = ExitStack()
        def ab(name, shape, dt=F32):
            return sb("a_" + name, shape, dt, scope)
        a.w = ab("w", [P, AW])
        a.qk = ab("qk", [P, 2, TOK])
        a.sq = ab("sq", [P, 2, TOK])
        a.ex = ab("ex", [P, 2 * TB * HEADS])
        a.sc = ab("sc", [P, 2 * TB * HEADS])
        a.va = ab("va", [P, TB, HEADS * VW])
        a.t1 = ab("t1", [P, T])
        a.r = ab("r", [P, 2, T])
        a.ab = ab("ab", [P, T])
        a.sn = ab("sn", [P, 2, T])
        a.cs = ab("cs", [P, 2, T])
        a.kvm = ab("kvm", [P, BATCH, 2 * GROUPS, HG * VW])
        a.on = ab("on", [P, 4 * HEADS * VW])
        a.z = ab("z", [P, 4 * HEADS])
        a.rz = ab("rz", [P, 4 * HEADS])
        a.od = ab("od", [P, 4, P])
        a.oT = ab("oT", [P, T])
        a.f_ps = [psum(f"a_f_ps{i}", [P, T], F32, scope) for i in range(2)]
        a.kv_ps = [psum(f"a_kv_ps{i}", [P, T], F32, scope) for i in range(2)]
        a.o_ps = [psum(f"a_o_ps{i}", [P, T], F32, scope) for i in range(2)]
        a.ps = bank
        scope.close()

        l = norm_semaphores(sem, "l")
        e1, e2 = (expert_semaphores(sem, n) for n in ("e1", "e2"))
        at = attention_semaphores(sem, "at")

        block = keep.enter_context(nc.Block())
        k.x = lambda c: x0[:, c * T:(c + 1) * T]

        def xcols(j, c):
            off = (j % BATCH) * SEQ + c * T
            return bass.ds(off, T) if not isinstance(off, int) else slice(off, off + T)

        def back(j, c, n, lag):
            kk = 2 * j + c
            if n >= lag:
                return c, n - lag, kk
            if isinstance(kk, int) and kk == 0:
                return None
            return 1 - c, n - lag + STATES, kk - 1

        @block.sync
        def _(sp):
            for name, dst in (("x", x0),):
                for c in range(CHUNKS):
                    sp.dma_start(x0[:, c * T:(c + 1) * T], d.x[:, c * T:(c + 1) * T]).then_inc(io.x, 16)
            sp.dma_start(k.mean_w[:], d.mean_w).then_inc(io.consts, 16)
            sp.dma_start(k.const[:], d.const).then_inc(io.consts, 16)
            sp.dma_start(k.ident[:], d.ident).then_inc(io.consts, 16)
            sp.dma_start(bc_sel[:].bitcast(mybir.dt.uint16), d.bc_sel).then_inc(io.consts, 16)
            sp.dma_start(k.ident_b[:].bitcast(mybir.dt.uint16), d.ident_b).then_inc(io.consts, 16)
            sp.dma_start(k.rank[:], d.rank).then_inc(io.consts, 16)
            sp.dma_start(e_sel[:].bitcast(mybir.dt.uint16), d.e_sel).then_inc(io.consts, 16)

            def load_p(l):
                sp.dma_start(m.wp[:], d.wp[l]).then_inc(s.wp, 16)
                sp.dma_start(m.wdt[:], d.wdt[l]).then_inc(s.wp, 16)
                sp.dma_start(m.cw[:], d.cw[l].broadcast_to([P, TAPS * INNER])).then_inc(s.wp, 16)

            def load_a(l):
                sp.dma_start(m.alog[:], d.alog[l]).then_inc(s.wa, 16)

            def load_o(l):
                sp.dma_start(m.wo[:], d.wo[l]).then_inc(s.wo, 16)

            def layer(l):
                q = 2 * l
                wait(sp, s.xb, 4 * q)
                load_p(l)
                wait(sp, s.aneg, q)
                load_a(l)
                wait(sp, s.x, 2 * q + (CHUNKS if not (isinstance(q, int) and q == 0) else 0))
                load_o(l)
                sp.wait_ge(s.wp, 48 * q + 48)
                sp.sem_inc(s.wp, 48)
                sp.wait_ge(s.wa, 16 * q + 16)
                sp.sem_inc(s.wa, 16)
                sp.wait_ge(s.wo, 16 * q + 16)
                sp.sem_inc(s.wo, 16)

            layer(0)
            with sp.Fori(1, LAYERS) as i:
                layer(i)
            sp.wait_ge(io.merged, CHUNKS)
            sp.dma_start(f.wr[:], d.wr).then_inc(io.wr, 16)
            ffn_loads(sp, e1, k, f, d)
            sp.wait_ge(e1.acc, EXPERTS * STEPS)
            att_loads(sp, at, k, a, d)
            sp.wait_ge(at.fin, CHUNKS)
            sp.dma_start(f.wr[:], d.wr).then_inc(io.wr, 16)
            ffn_loads(sp, e2, k, f, d)
            for c in range(CHUNKS):
                sp.wait_ge(e2.acc, (EXPERTS - 1) * STEPS + c + 1)
                sp.dma_start(d.out[:, c * T:(c + 1) * T], x0[:, c * T:(c + 1) * T]).then_inc(io.stored, 16)
            sp.wait_ge(io.stored, 16 * CHUNKS)

        @block.tensor
        def _(pe):
            pe.wait_ge(io.consts, 112)
            pe.wait_ge(io.x, 16 * CHUNKS)
            ln_tensor(pe, l, k, ln, 0)

            def project(j, c, piece):
                kk = 2 * j + c
                if piece == "ms":
                    pe.wait_ge(s.sq, kk + 1)
                    wait(pe, s.xb, 2 * kk)
                    pe.matmul(bank[1][:], k.mean_w[:], m.sq[:], start=True, stop=True).then_inc(s.ms, 1)
                elif piece == "conv":
                    pe.wait_ge(s.hn, kk + 1)
                    pe.wait_ge(s.weff, j + 1)
                    pe.wait_ge(s.pad, 1)
                    pe.wait_ge(s.ln, kk + 1)
                    for h in range(HALVES):
                        for tap in range(TAPS):
                            mm = pe.matmul(bank[h][:], m.weff[:, tap, h * P:(h + 1) * P],
                                           m.hn[:, c * T + tap:c * T + tap + T],
                                           start=(tap == 0), stop=(tap == TAPS - 1))
                        mm.then_inc(s.xc_ps, 1)
                elif piece == "z":
                    for h in range(HALVES):
                        pe.wait_ge(s.xc, 2 * kk + 1 + h)
                        pe.matmul(bank[h][:], m.wp[:, INNER + h * P:INNER + (h + 1) * P],
                                  m.hn[:, c * T + TAPS - 1:c * T + TAPS - 1 + T],
                                  start=True, stop=True).then_inc(s.z_ps, 1)
                elif piece == "bcd":
                    nb = NPAR * 2 * STATES
                    pe.wait_ge(s.z, 2 * kk + 2)
                    for h in range(HALVES):
                        o = O_WX + h * WX
                        mm = pe.matmul(bank[0][0:nb, :], m.wp[:, o:o + nb], m.xc[:, c, h, :],
                                       start=(h == 0), stop=(h == HALVES - 1))
                    mm.then_inc(s.bcp_ps, 1)
                    for h in range(HALVES):
                        o = O_WX + h * WX + nb
                        mm = pe.matmul(bank[1][0:RANK, :], m.wp[:, o:o + RANK], m.xc[:, c, h, :],
                                       start=(h == 0), stop=(h == HALVES - 1))
                    mm.then_inc(s.dtr_ps, 1)
                elif piece == "dt":
                    pe.wait_ge(s.dtr, kk + 1)
                    pe.wait_ge(s.r1, kk + 1)
                    for h in range(HALVES):
                        pe.matmul(bank[h][:], m.wdt[:, h * P:(h + 1) * P], m.dtr[:],
                                  start=True, stop=True).then_inc(s.d_ps, 1)

            def out_proj(j, c):
                kk = 2 * j + c
                pe.wait_ge(s.gate, kk + 1)
                pe.wait_ge(s.wo, 16 * j + 16)
                for h in range(HALVES):
                    mm = pe.matmul(bank[0][:], m.wo[:, h * P:(h + 1) * P], m.yg[:, h, :],
                                   start=(h == 0), stop=(h == HALVES - 1))
                mm.then_inc(s.out_ps, 1)

            def accumulate(b):
                c, n, kk = b
                if n == 0:
                    wait(pe, s.yd, 2 * kk)
                if n in POOL_N:
                    pe.wait_ge(s.pp, len(POOL_N) * kk + POOL_N.index(n) + 1)
                else:
                    pe.wait_ge(s.pd, len(DVE_N) * kk + DVE_N.index(n) + 1)
                for h in range(HALVES):
                    mm = pe.matmul(y_ps[:, h, :], k.ident[:], m.p[:, n % RING, h, :],
                                   start=(n == 0), stop=(n == STATES - 1))
                mm.then_inc(s.y_acc, 1)

            def broadcast(j, c, n):
                kk = 2 * j + c
                if n == 0:
                    pe.wait_ge(s.bc, kk + 1)
                wait(pe, s.bcs, STATES * kk + n - 1)
                for w in range(2):
                    mm = pe.matmul(bc_ps[n % 2][:, w, :], bc_sel[:, w * STATES + n, :], m.bc[:, c, :],
                                   start=True, stop=True)
                mm.then_inc(s.bc_ps, 1)

            def pair(j, last):
                for c in range(2):
                    nxt = (j, 1) if c == 0 else (j + 1, 0)
                    more = c == 0 or not last
                    for n in range(STATES):
                        broadcast(j, c, n)
                        b = back(j, c, n, 3)
                        if b:
                            accumulate(b)
                        if more and n == 2:
                            project(*nxt, "ms")
                        if n == 5:
                            tail = back(j, c, 0, 1)
                            if tail:
                                out_proj(j if c == 1 else j - 1, 1 - c)
                        if more and n == 7:
                            if (isinstance(j, int) and j == 0 and c == 0) is False:
                                pe.wait_ge(s.x, CHUNKS + 2 * j + c)
                            project(*nxt, "conv")
                        if more and n == 8:
                            project(*nxt, "z")
                        if more and n == 9:
                            project(*nxt, "bcd")
                        if more and n == 11:
                            project(*nxt, "dt")

            for piece in ("ms", "conv", "z", "bcd", "dt"):
                project(0, 0, piece)
            pair(0, False)
            with pe.Fori(1, PAIRS - 1) as j:
                pair(j, False)
            pair(PAIRS - 1, True)
            for n in range(STATES - 3, STATES):
                accumulate((1, n, 2 * PAIRS - 1))
            out_proj(PAIRS - 1, 1)

            pe.wait_ge(io.merged, CHUNKS)
            ln_tensor(pe, l, k, ln, 1)
            pe.wait_ge(io.wr, 16)
            ffn_tensor(pe, e1, k, f, xn, l.out, 1)
            pe.wait_ge(e1.acc, EXPERTS * STEPS)
            ln_tensor(pe, l, k, ln, 2)
            att_tensor(pe, at, k, a, xn, l.out, 2)
            pe.wait_ge(at.fin, CHUNKS)
            ln_tensor(pe, l, k, ln, 3)
            pe.wait_ge(io.wr, 32)
            ffn_tensor(pe, e2, k, f, xn, l.out, 3)

        @block.scalar
        def _(act):
            act.wait_ge(io.consts, 112)
            ln_scalar(act, l, k, ln, 0)

            def project(j, c, piece):
                kk = 2 * j + c
                if piece == "sq":
                    act.wait_ge(s.x, kk + 1)
                    act.activation(m.sq[:], xn[:, xcols(j, c)], ACT.Square).then_inc(s.sq, 1)
                elif piece == "rstd":
                    act.wait_ge(s.ms, kk + 1)
                    act.activation(m.lnv[:], bank[1][:], ACT.Ln, bias=k.const[:, C_EPS:C_EPS + 1]).then_inc(s.ln, 1)
                    act.wait_ge(s.ln, kk + 1)
                    act.activation(m.rstd[:], m.lnv[:], ACT.Exp, scale=-0.5).then_inc(s.rstd, 1)
                elif piece == "silu":
                    wait(act, s.gate, kk - 1)
                    act.wait_ge(s.wp, 48 * j + 48)
                    for h in range(HALVES):
                        act.wait_ge(s.xc_ps, 2 * kk + 1 + h)
                        act.activation(m.xc[:, c, h, :], bank[h][:], ACT.Silu,
                                       bias=m.wp[:, O_CB + h:O_CB + h + 1]).then_inc(s.xc, 1)
                    for h in range(HALVES):
                        act.wait_ge(s.z_ps, 2 * kk + 1 + h)
                        act.activation(m.z[:, c, h, :], bank[h][:], ACT.Silu).then_inc(s.z, 1)
                elif piece == "parts":
                    act.wait_ge(s.bcp_ps, kk + 1)
                    act.activation(m.hi[:], bank[0][0:NPAR * 2 * STATES, :], ACT.Copy).then_inc(s.hi, 1)
                    act.wait_ge(s.dtr_ps, kk + 1)
                    act.activation(m.dtr[:], bank[1][0:RANK, :], ACT.Copy).then_inc(s.dtr, 1)
                elif piece == "softplus":
                    for h in range(HALVES):
                        act.wait_ge(s.d_ps, 2 * kk + 1 + h)
                        act.activation(m.xb[:, h, :], bank[h][:], ACT.Identity,
                                       bias=m.wp[:, O_BDT + h:O_BDT + h + 1]).then_inc(s.xb, 1)
                    act.wait_ge(s.xb, 2 * kk + 2)
                    wait(act, s.s1, kk)
                    act.activation(m.ab[:], m.xb[:], ACT.Abs).then_inc(s.ab, 1)
                    act.wait_ge(s.ab, kk + 1)
                    act.activation(m.ey[:], m.ab[:], ACT.Exp, scale=-1.0).then_inc(s.ey, 1)
                    act.wait_ge(s.ey, kk + 1)
                    act.activation(m.ll[:], m.ey[:], ACT.Ln, bias=1.0).then_inc(s.ll, 1)

            def decay_weights(j):
                act.wait_ge(s.wa, 16 * j + 16)
                act.activation(m.a1[:], m.alog[:], ACT.Exp).then_inc(s.a1, 1)
                act.wait_ge(s.a1, j + 1)
                act.activation(m.aneg[:], m.a1[:], ACT.Copy, scale=-1.0).then_inc(s.aneg, 1)
                act.wait_ge(s.aneg, j + 1)

            def step(j, c, n):
                g = STATES * (2 * j + c) + n
                if n == 0:
                    act.wait_ge(s.delta, 2 * j + c + 1)
                wait(act, s.h, g - RING + 1)
                for h in range(HALVES):
                    a = act.activation(m.a[:, n % RING, h, :], m.delta[:, c, h, :], ACT.Exp,
                                       scale=m.aneg[:, h * STATES + n:h * STATES + n + 1])
                a.then_inc(s.a, 1)
                act.wait_ge(s.bc_ps, g + 1)
                wait(act, s.y_acc, g - RING + 1)
                act.activation(m.bcs[:, n % RING, :, :], bc_ps[n % 2][:], ACT.Copy).then_inc(s.bcs, 1)

            def pair(j, last):
                decay_weights(j)
                for c in range(2):
                    nxt = (j, 1) if c == 0 else (j + 1, 0)
                    more = c == 0 or not last
                    for n in range(STATES):
                        step(j, c, n)
                        if more and n == 1:
                            project(*nxt, "sq")
                        if more and n == 2:
                            project(*nxt, "rstd")
                        if more and n == 8:
                            project(*nxt, "silu")
                        if more and n == 9:
                            project(*nxt, "parts")
                        if more and n == 11:
                            project(*nxt, "softplus")

            for piece in ("sq", "rstd", "silu", "parts", "softplus"):
                project(0, 0, piece)
            pair(0, False)
            with act.Fori(1, PAIRS - 1) as j:
                pair(j, False)
            pair(PAIRS - 1, True)

            ln_scalar(act, l, k, ln, 1)
            ffn_scalar(act, e1, k, f)
            ln_scalar(act, l, k, ln, 2)
            att_scalar(act, at, k, a)
            ln_scalar(act, l, k, ln, 3)
            ffn_scalar(act, e2, k, f)

        @block.vector
        def _(dve):
            dve.memset(m.hn[:, 0:TAPS - 1], 0.0).then_inc(s.pad, 1)
            dve.wait_ge(io.x, 16 * CHUNKS)
            ln_vector(dve, l, k, ln, 0, xn, s.x)

            def project(j, c, piece):
                kk = 2 * j + c
                if piece == "hn":
                    dve.wait_ge(s.rstd, kk + 1)
                    dve.wait_ge(s.wp, 48 * j + 48)
                    wait(dve, s.z_ps, 2 * kk)
                    dve.scalar_tensor_tensor(out=m.hn[:, TAPS - 1 + c * T:TAPS - 1 + (c + 1) * T],
                                             in0=xn[:, xcols(j, c)], scalar=m.wp[:, O_NORM:O_NORM + 1],
                                             in1=m.rstd[:], op0=ALU.mult, op1=ALU.mult).then_inc(s.hn, 1)
                elif piece == "parts":
                    nb = NPAR * 2 * STATES
                    dve.wait_ge(s.hi, kk + 1)
                    dve.scalar_tensor_tensor(out=m.r1[:], in0=m.hi[:], scalar=k.const[0:nb, C_M1:C_M1 + 1],
                                             in1=bank[0][0:nb, :], op0=ALU.mult, op1=ALU.add).then_inc(s.r1, 1)
                    dve.wait_ge(s.r1, kk + 1)
                    dve.tensor_copy(m.mid[:], m.r1[:]).then_inc(s.mid, 1)
                    dve.wait_ge(s.mid, kk + 1)
                    dve.scalar_tensor_tensor(out=m.bc[:, c, :], in0=m.mid[:], scalar=k.const[0:nb, C_M2:C_M2 + 1],
                                             in1=m.r1[:], op0=ALU.mult, op1=ALU.add).then_inc(s.bc, 1)
                elif piece == "delta":
                    dve.wait_ge(s.ey, kk + 1)
                    dve.tensor_scalar(m.dd[:], m.ey[:], 1.0, -1.0, ALU.add, ALU.add).then_inc(s.dd, 1)
                    dve.wait_ge(s.dd, kk + 1)
                    dve.scalar_tensor_tensor(out=m.dd[:], in0=m.dd[:], scalar=-1.0, in1=m.ey[:],
                                             op0=ALU.mult, op1=ALU.add).then_inc(s.t, 1)
                    dve.wait_ge(s.ll, kk + 1)
                    dve.scalar_tensor_tensor(out=m.delta[:, c], in0=m.xb[:], scalar=0.0, in1=m.ll[:],
                                             op0=ALU.max, op1=ALU.add).then_inc(s.s1, 1)
                    dve.wait_ge(s.t, kk + 1)
                    dve.wait_ge(s.s1, kk + 1)
                    dve.tensor_tensor(m.delta[:, c], m.delta[:, c], m.dd[:], ALU.add).then_inc(s.delta, 1)
                    dve.wait_ge(s.delta, kk + 1)
                    dve.tensor_tensor(m.u[:, c], m.delta[:, c], m.xc[:, c], ALU.mult).then_inc(s.u, 1)

            def gate(j, c):
                kk = 2 * j + c
                dve.wait_ge(s.y_acc, STATES * (kk + 1))
                dve.wait_ge(s.wo, 16 * j + 16)
                wait(dve, s.out_ps, kk)
                for h in range(HALVES):
                    dve.scalar_tensor_tensor(out=m.yd[:, h, :], in0=m.xc[:, c, h, :],
                                             scalar=m.wo[:, HALVES * P + h:HALVES * P + h + 1],
                                             in1=y_ps[:, h, :], op0=ALU.mult, op1=ALU.add).then_inc(s.yd, 1)
                dve.wait_ge(s.yd, 2 * kk + 2)
                dve.tensor_tensor(m.yg[:], m.yd[:], m.z[:, c], ALU.mult).then_inc(s.gate, 1)

            def residual(j, c):
                kk = 2 * j + c
                dve.wait_ge(s.out_ps, kk + 1)
                x = xn[:, xcols(j, c)]
                dve.tensor_tensor(x, x, bank[0][:], ALU.add).then_inc(s.x, 1)

            def scan(j, c, n):
                g = STATES * (2 * j + c) + n
                dve.wait_ge(s.a, g + 1)
                dve.wait_ge(s.bx, g + 1)
                wait(dve, s.y_acc, g - RING + 1)
                if c == 1:
                    dve.wait_ge(s.carry, STATES * j + n + 1)
                for h in range(HALVES):
                    init = 0.0 if c == 0 else m.carry[:, h, n:n + 1]
                    i = dve.tensor_tensor_scan(m.h[:, n % RING, h, :], m.a[:, n % RING, h, :],
                                               m.bx[:, n % RING, h, :], init, ALU.mult, ALU.add)
                i.then_inc(s.h, 1)

            def product(b):
                c, n, kk = b
                g = STATES * kk + n
                dve.wait_ge(s.h, g + 1)
                if c == 0:
                    dve.tensor_copy(m.carry[:, :, n:n + 1], m.h[:, n % RING, :, T - 1:T]).then_inc(s.carry, 1)
                if n in DVE_N:
                    wait(dve, s.y_acc, g - RING + 1)
                    cb = m.bcs[:, n % RING, 1:2, :].broadcast_to([P, HALVES, T])
                    dve.tensor_tensor(m.p[:, n % RING], m.h[:, n % RING], cb, ALU.mult).then_inc(s.pd, 1)

            def pair(j, last):
                for c in range(2):
                    nxt = (j, 1) if c == 0 else (j + 1, 0)
                    more = c == 0 or not last
                    for n in range(STATES):
                        scan(j, c, n)
                        b = back(j, c, n, 1)
                        if b:
                            product(b)
                        if more and n == 3:
                            project(*nxt, "hn")
                        tail = back(j, c, 0, 1)
                        if n == 2 and tail:
                            gate(j if c == 1 else j - 1, 1 - c)
                        if n == 6 and tail:
                            residual(j if c == 1 else j - 1, 1 - c)
                        if more and n == 10:
                            project(*nxt, "parts")
                        if more and n == 13:
                            project(*nxt, "delta")

            for piece in ("hn", "parts", "delta"):
                project(0, 0, piece)
            pair(0, False)
            with dve.Fori(1, PAIRS - 1) as j:
                pair(j, False)
            pair(PAIRS - 1, True)
            product((1, STATES - 1, 2 * PAIRS - 1))
            gate(PAIRS - 1, 1)
            residual(PAIRS - 1, 1)
            dve.wait_ge(s.x, CHUNKS + 2 * PAIRS)
            for c in range(CHUNKS):
                cols = slice(c * T, (c + 1) * T)
                dve.tensor_tensor(x0[:, cols], x0[:, cols], xn[:, cols], ALU.add).then_inc(io.merged, 1)
            dve.wait_ge(io.merged, CHUNKS)
            ln_vector(dve, l, k, ln, 1, xn)
            ffn_vector(dve, e1, k, f, x0)
            dve.wait_ge(e1.acc, EXPERTS * STEPS)
            ln_vector(dve, l, k, ln, 2, xn)
            att_vector(dve, at, k, a, x0)
            dve.wait_ge(at.fin, CHUNKS)
            ln_vector(dve, l, k, ln, 3, xn)
            ffn_vector(dve, e2, k, f, x0)

        @block.gpsimd
        def _(pool):
            def fold(j):
                pool.wait_ge(s.wp, 48 * j + 48)
                wait(pool, s.z_ps, 4 * j)
                w = m.wp[:, 0:INNER].rearrange("p (a i) -> p a i", a=1).broadcast_to([P, TAPS, INNER])
                pool.tensor_tensor(m.weff[:], m.cw[:].rearrange("p (a i) -> p a i", a=TAPS), w,
                                   ALU.mult).then_inc(s.weff, 1)

            def spread_u(j, c, n):
                g = STATES * (2 * j + c) + n
                if n == 0:
                    pool.wait_ge(s.u, 2 * j + c + 1)
                pool.wait_ge(s.bcs, g + 1)
                wait(pool, s.h, g - RING + 1)
                bb = m.bcs[:, n % RING, 0:1, :].broadcast_to([P, HALVES, T])
                pool.tensor_tensor(m.bx[:, n % RING], m.u[:, c], bb, ALU.mult).then_inc(s.bx, 1)

            def product(b):
                c, n, kk = b
                if n not in POOL_N:
                    return
                g = STATES * kk + n
                pool.wait_ge(s.h, g + 1)
                wait(pool, s.y_acc, g - RING + 1)
                cb = m.bcs[:, n % RING, 1:2, :].broadcast_to([P, HALVES, T])
                pool.tensor_tensor(m.p[:, n % RING], m.h[:, n % RING], cb, ALU.mult).then_inc(s.pp, 1)

            def pair(j, last):
                for c in range(2):
                    for n in range(STATES):
                        spread_u(j, c, n)
                        b = back(j, c, n, 2)
                        if b:
                            product(b)
                        if c == 1 and n == 4 and not last:
                            fold(j + 1)

            fold(0)
            pair(0, False)
            with pool.Fori(1, PAIRS - 1) as j:
                pair(j, False)
            pair(PAIRS - 1, True)
            for n in range(STATES - 2, STATES):
                product((1, n, 2 * PAIRS - 1))


def pack(inputs):
    get = lambda name: np.ascontiguousarray(inputs[name])
    BF16_ONE = np.uint16(0x3F80)
    a = {}
    a["x"] = np.ascontiguousarray(get("L0_attn_a_x").reshape(TOK, P).T)
    win = get("L0_attn_a_W_in").transpose(0, 2, 1)
    wx = get("L0_attn_a_W_x").transpose(0, 2, 1)
    bcw = wx[:, :, RANK:]
    wx = np.concatenate([bcw, bcw, bcw, wx[:, :, :RANK]], axis=2)
    halves = lambda v: v.reshape(LAYERS, HALVES, P, -1).transpose(0, 2, 1, 3).reshape(LAYERS, P, -1)
    a["wp"] = np.concatenate([win, halves(wx), get("L0_attn_a_norm_w")[:, :, None],
                              halves(get("L0_attn_a_conv_b")), halves(get("L0_attn_a_b_dt"))], axis=2)
    a["wdt"] = get("L0_attn_a_W_dt").transpose(0, 2, 1)
    a["cw"] = get("L0_attn_a_conv_w").transpose(0, 2, 1).reshape(LAYERS, 1, TAPS * INNER)
    a["alog"] = halves(get("L0_attn_a_A_log"))
    a["wo"] = np.concatenate([halves(get("L0_attn_a_W_out").transpose(0, 2, 1)), halves(get("L0_attn_a_D"))], axis=2)
    a["mean_w"] = np.full((P, P), 1.0 / P, np.float32)
    const = np.zeros((P, NCONST), np.float32)
    const[:, C_EPS] = EPS
    const[2 * STATES:, C_M1] = -1.0
    const[4 * STATES:, C_M2] = -1.0
    const[:, C_HPI] = np.pi / 2
    a["const"] = const
    sel = np.zeros((NPAR, 2 * STATES, 2 * STATES, P), np.float32)
    for i in range(2 * STATES):
        sel[:, i, i, :] = 1.0
    a["bc_sel"] = sel.reshape(NPAR * 2 * STATES, 2 * STATES, P).astype(np.uint16) * BF16_ONE
    a["ident"] = np.eye(P, dtype=np.float32)
    a["ident_b"] = np.eye(P, dtype=np.float32).astype(np.uint16) * BF16_ONE
    w2 = get("L0_ffn_w2").reshape(EXPERTS, HB, P, P).transpose(0, 2, 1, 3).reshape(EXPERTS, P, HB * P)
    b1 = get("L0_ffn_b1").reshape(EXPERTS, HB, P).transpose(0, 2, 1)
    a["ew"] = np.concatenate([get("L0_ffn_w1"), w2, b1, get("L0_ffn_b2")[:, :, None]], axis=2)
    a["wr"] = get("L0_ffn_w_router")
    a["rank"] = np.tile(np.arange(EXPERTS, 0, -1, dtype=np.float32), (P, TB))
    esel = np.zeros((NPAR, EXPERTS, EXPERTS, P), np.float32)
    for i in range(EXPERTS):
        esel[:, i, i, :] = 1.0
    a["e_sel"] = esel.reshape(NPAR * EXPERTS, EXPERTS, P).astype(np.uint16) * BF16_ONE
    rf = get("L0_attn_b_rf")
    bd = np.zeros((HEADS, DH, HEADS, M), rf.dtype)
    hs = np.zeros((HEADS, DH, HEADS), np.float32)
    for h in range(HEADS):
        bd[h, :, h, :] = rf.T
        hs[h, :, h] = 1.0
    mask = np.zeros((HG, M, HG, VW), np.float32)
    for h in range(HG):
        mask[h, :, h, :] = 1.0
    a["aw"] = np.concatenate([get("L0_attn_b_" + n).T for n in ("wq", "wk", "wv", "wo")]
                             + [bd.reshape(P, HEADS * M), hs.reshape(P, HEADS), mask.reshape(P, HG * VW)], axis=1)
    return {n: np.ascontiguousarray(v) for n, v in a.items()}


def kernel(**inputs):
    import concourse.bacc as _bacc
    from concourse.bass_utils import run_bass_kernel_spmd as _run

    nc = _bacc.Bacc("TRN2", target_bir_lowering=False, num_devices=1)
    arrays = pack(inputs)
    t = {n: nc.dram_tensor(f"in_{n}", a.shape, mybir.dt.from_np(a.dtype), kind="ExternalInput").ap()
             for n, a in arrays.items()}
    d = Group()
    d.x, d.out, d.mean_w, d.const, d.bc_sel, d.e_sel, d.ident, d.ident_b, d.rank = (
        t.get(n) for n in ("x", "out", "mean_w", "const", "bc_sel", "e_sel", "ident", "ident_b", "rank"))
    d.wp, d.wdt, d.cw, d.alog, d.wo, d.ew, d.wr, d.aw = (
        t.get(n) for n in ("wp", "wdt", "cw", "alog", "wo", "ew", "wr", "aw"))
    d.out = nc.dram_tensor("out", (P, TOK), F32, kind="ExternalOutput").ap()
    build(nc, d)
    r = _run(nc, [{f"in_{n}": a for n, a in arrays.items()}], core_ids=[0])
    out = r.results[0]["out"]
    return np.ascontiguousarray(out.T).reshape(BATCH, SEQ, P)
```

```python
from contextlib import ExitStack

import numpy as np
import concourse.bass as bass
from concourse import mybir

ALU = mybir.AluOpType
ACT = mybir.ActivationFunctionType
AX = mybir.AxisListType
F32 = mybir.dt.float32
BF16 = mybir.dt.bfloat16

P = 128
BATCH, SEQ = 2, 1024
TOK = BATCH * SEQ
T = 512
CHUNKS = TOK // T
LOADED_AHEAD = 26 * 1024
EPS = 1e-5

LAYERS = 4
INNER = 256
HALVES = INNER // P
RANK = 64
STATES = 16
TAPS = 4
PAIRS = LAYERS * BATCH
NPAR = 3
RING = 4
BC_RING = 8
BC_AHEAD = 3
COPY_AHEAD = 2
MEAN_AT = 12
POOL_N = (1, 4, 7, 9, 12, 14)
DVE_N = tuple(n for n in range(STATES) if n not in POOL_N)

EXPERTS = 8
HIDDEN = 512
HB = HIDDEN // P
EW = HIDDEN + HB * P + HB + 1

HEADS = 16
DH = P // HEADS
M = 32
HG = P // M
GROUPS = HEADS // HG
VW = DH + 1

A_RF = 4 * P
A_HS = A_RF + HEADS * M
A_MASK = A_HS + HEADS
AW = A_MASK + HG * VW

O_WX = 2 * INNER
WX = NPAR * 2 * STATES + RANK
O_NORM = O_WX + HALVES * WX
O_CB = O_NORM + 1
O_BDT = O_CB + HALVES
PW = O_BDT + HALVES
OW = HALVES * P + HALVES

C_EPS, C_M1, C_M2, C_HPI, NCONST = 0, 1, 2, 3, 4


class Group:
    pass


def wait(eng, sem, value):
    if isinstance(value, int) and value <= 0:
        return
    eng.wait_ge(sem, value)


def norm_semaphores(sem, phase):
    s = Group()
    s.mean = sem(phase + "_mean")
    s.cen = sem(phase + "_cen")
    s.sq = sem(phase + "_sq")
    s.var = sem(phase + "_var")
    s.ln = sem(phase + "_ln")
    s.rstd = sem(phase + "_rstd")
    s.out = sem(phase + "_out")
    return s


def ln_tensor(pe, s, k, ln, r):
    for c in range(CHUNKS):
        pe.matmul(ln.mean_ps[c][:], k.mean_w[:], k.x(c), start=True, stop=True).then_inc(s.mean, 1)
    for c in range(CHUNKS):
        pe.wait_ge(s.sq, CHUNKS * r + c + 1)
        pe.matmul(ln.var_ps[c][:], k.mean_w[:], ln.s[:, c * T:(c + 1) * T], start=True, stop=True).then_inc(s.var, 1)


def ln_scalar(act, s, k, ln, r, out):
    cols = [slice(c * T, (c + 1) * T) for c in range(CHUNKS)]
    for c in range(CHUNKS):
        act.wait_ge(s.cen, CHUNKS * r + c + 1)
        act.activation(ln.s[:, cols[c]], out[:, cols[c]], ACT.Square).then_inc(s.sq, 1)
    for c in range(CHUNKS):
        act.wait_ge(s.var, CHUNKS * r + c + 1)
        act.activation(ln.s[:, cols[c]], ln.var_ps[c][:], ACT.Ln, bias=k.const[:, C_EPS:C_EPS + 1]).then_inc(s.ln, 1)
    for c in range(CHUNKS):
        act.wait_ge(s.ln, CHUNKS * r + c + 1)
        act.activation(ln.s[:, cols[c]], ln.s[:, cols[c]], ACT.Exp, scale=-0.5).then_inc(s.rstd, 1)


def ln_vector(dve, s, k, ln, r, out, out_sem=None):
    cols = [slice(c * T, (c + 1) * T) for c in range(CHUNKS)]
    for c in range(CHUNKS):
        dve.wait_ge(s.mean, CHUNKS * r + c + 1)
        dve.tensor_tensor(out[:, cols[c]], k.x(c), ln.mean_ps[c][:], ALU.subtract).then_inc(s.cen, 1)
    for c in range(CHUNKS):
        dve.wait_ge(s.rstd, CHUNKS * r + c + 1)
        dve.tensor_tensor(out[:, cols[c]], out[:, cols[c]], ln.s[:, cols[c]], ALU.mult).then_inc(s.out, 1)
        if out_sem:
            dve.wait_ge(s.out, CHUNKS * r + c + 1)
            dve.sem_inc(out_sem, 1)


STEPS = CHUNKS
TB = TOK // P


def expert_semaphores(sem, phase):
    s = Group()
    s.w0 = sem(phase + "_w0")
    s.w1 = sem(phase + "_w1")
    s.logits = sem(phase + "_logits")
    s.shift = sem(phase + "_shift")
    s.ex = sem(phase + "_ex")
    s.route = sem(phase + "_route")
    s.wlo = sem(phase + "_wlo")
    s.wT_ps = sem(phase + "_wT_ps")
    s.wT = sem(phase + "_wT")
    s.wb_ps = sem(phase + "_wb_ps")
    s.wb = sem(phase + "_wb")
    s.h_ps = sem(phase + "_h_ps")
    s.gel = sem(phase + "_gel")
    s.y_ps = sem(phase + "_y_ps")
    s.part = sem(phase + "_part")
    s.acc = sem(phase + "_acc")
    return s


def rows3(t):
    return t[:].rearrange("p (b e) -> p b e", e=EXPERTS)


def per_block(t):
    return t[:].rearrange("p (b o) -> p b o", o=1).broadcast_to([P, TB, EXPERTS])


def ffn_loads(sp, s, k, f, d):
    sp.dma_start(f.w[0][:], d.ew[0]).then_inc(s.w0, 16)
    sp.dma_start(f.w[1][:], d.ew[1]).then_inc(s.w1, 16)
    with sp.Fori(1, EXPERTS // 2) as ep:
        for i, ws in enumerate((s.w0, s.w1)):
            e = 2 * ep + i
            sp.wait_ge(s.part, STEPS * (e - 1))
            sp.dma_start(f.w[i][:], d.ew[e]).then_inc(ws, 16)


def ffn_tensor(pe, s, k, f, xn, ln_out, r):
    pe.wait_ge(ln_out, CHUNKS * (r + 1))
    for b in range(TB):
        mm = pe.matmul(f.ps[0][:, b * EXPERTS:(b + 1) * EXPERTS], xn[:, b * P:(b + 1) * P], f.wr[:],
                       start=True, stop=True)
    mm.then_inc(s.logits, 1)
    pe.wait_ge(s.wlo, 1)
    for half in range(2):
        wT = f.ps[half][0:NPAR * EXPERTS, :].bitcast(BF16)
        for b in range(TB // 2):
            mm = pe.transpose(wT[:, b * P:(b + 1) * P], f.w3[:, half * TB // 2 + b, :], k.ident_b[:])
        mm.then_inc(s.wT_ps, 1)
    for i in range(EXPERTS * STEPS):
        e, t = i // STEPS, i % STEPS
        if i < 2:
            pe.wait_ge(s.wT, 2)
        wait(pe, s.wb, i - 1)
        pe.matmul(f.ps[i % 2][:], f.e_sel[:, e, :], f.wT[:, t * T:(t + 1) * T],
                  start=True, stop=True).then_inc(s.wb_ps, 1)

    def hidden(ep, i):
        w, t = f.w[i // STEPS], i % STEPS
        g = 2 * STEPS * ep + i
        if t == 0:
            pe.wait_ge((s.w0, s.w1)[i // STEPS], 16 * ep + 16)
        for b in range(HB):
            wait(pe, s.gel, HB * (g - 1) + b + 1)
            pe.matmul(f.h_ps[b][:], w[:, b * P:(b + 1) * P], xn[:, t * T:(t + 1) * T],
                      start=True, stop=True).then_inc(s.h_ps, 1)

    def output(ep, i):
        w = f.w[i // STEPS]
        g = 2 * STEPS * ep + i
        wait(pe, s.part, g - 1)
        for b in range(HB):
            pe.wait_ge(s.gel, HB * g + b + 1)
            mm = pe.matmul(f.y_ps[i % 2][:], w[:, HIDDEN + b * P:HIDDEN + (b + 1) * P], f.g[:, i % 2, b, :],
                           start=(b == 0), stop=(b == HB - 1))
        mm.then_inc(s.y_ps, 1)

    def pair(ep, last):
        for i in range(2 * STEPS):
            if i + 1 < 2 * STEPS:
                hidden(ep, i + 1)
            elif not last:
                hidden(ep + 1, 0)
            output(ep, i)

    hidden(0, 0)
    pair(0, False)
    with pe.Fori(1, EXPERTS // 2 - 1) as ep:
        pair(ep, False)
    pair(EXPERTS // 2 - 1, True)


def ffn_scalar(act, s, k, f):
    act.wait_ge(s.shift, 1)
    act.activation(f.ex[:], f.sh[:], ACT.Exp).then_inc(s.ex, 1)
    for i in range(EXPERTS * STEPS):
        act.wait_ge(s.wb_ps, i + 1)
        act.activation(f.wb[:, i * T:(i + 1) * T], f.ps[i % 2][:], ACT.Copy).then_inc(s.wb, 1)

    def pair(ep):
        for i in range(2 * STEPS):
            g = 2 * STEPS * ep + i
            wait(act, s.y_ps, g - 1)
            for b in range(HB):
                act.wait_ge(s.h_ps, HB * g + b + 1)
                act.activation(f.g[:, i % 2, b, :], f.h_ps[b][:], ACT.Gelu_apprx_tanh,
                               bias=f.w[i // STEPS][:, HIDDEN + HB * P + b:HIDDEN + HB * P + b + 1]).then_inc(s.gel, 1)

    pair(0)
    with act.Fori(1, EXPERTS // 2) as ep:
        pair(ep)


def ffn_vector(dve, s, k, f, x):
    lg = f.ps[0][:, 0:TB * EXPERTS].rearrange("p (b e) -> p b e", e=EXPERTS)
    rank = k.rank[:].rearrange("p (b e) -> p b e", e=EXPERTS)
    done = 0

    def chained(instruction):
        nonlocal done
        done += 1
        instruction.then_inc(s.route, 1)
        dve.wait_ge(s.route, done)

    dve.wait_ge(s.logits, 1)
    chained(dve.tensor_reduce(f.c[0][:], lg, AX.X, ALU.max))
    dve.tensor_tensor(rows3(f.sh), lg, per_block(f.c[0]), ALU.subtract).then_inc(s.shift, 1)
    dve.wait_ge(s.ex, 1)
    chained(dve.tensor_reduce(f.c[1][:], rows3(f.ex), AX.X, ALU.add))
    chained(dve.reciprocal(f.c[2][:], f.c[1][:]))
    chained(dve.tensor_tensor(rows3(f.p), rows3(f.ex), per_block(f.c[2]), ALU.mult))

    def largest(p, cm, cc, eq, sel):
        chained(dve.tensor_reduce(cm[:], rows3(p), AX.X, ALU.max))
        chained(dve.tensor_tensor(rows3(eq), rows3(p), per_block(cm), ALU.is_equal))
        chained(dve.tensor_tensor(rows3(eq), rows3(eq), rank, ALU.mult))
        chained(dve.tensor_reduce(cc[:], rows3(eq), AX.X, ALU.max))
        chained(dve.tensor_tensor(rows3(sel), rows3(eq), per_block(cc), ALU.is_equal))

    largest(f.p, f.c[3], f.c[4], f.eq[0], f.sel[0])
    chained(dve.scalar_tensor_tensor(out=f.p2[:], in0=f.sel[0][:], scalar=-2.0, in1=f.p[:],
                                     op0=ALU.mult, op1=ALU.add))
    largest(f.p2, f.c[5], f.c[6], f.eq[1], f.sel[1])
    chained(dve.tensor_tensor(f.both[:], f.sel[0][:], f.sel[1][:], ALU.add))
    chained(dve.tensor_tensor(f.wt[:], f.both[:], f.p[:], ALU.mult))
    chained(dve.tensor_copy(f.w3[:, :, 0:EXPERTS], rows3(f.wt)))
    chained(dve.tensor_tensor(rows3(f.wr1), rows3(f.wt), f.w3[:, :, 0:EXPERTS], ALU.subtract))
    chained(dve.tensor_copy(f.w3[:, :, EXPERTS:2 * EXPERTS], rows3(f.wr1)))
    dve.tensor_tensor(f.w3[:, :, 2 * EXPERTS:], rows3(f.wr1), f.w3[:, :, EXPERTS:2 * EXPERTS],
                      ALU.subtract).then_inc(s.wlo, 1)
    for half in range(2):
        dve.wait_ge(s.wT_ps, half + 1)
        dve.tensor_copy(f.wT[:, half * SEQ:(half + 1) * SEQ],
                        f.ps[half][0:NPAR * EXPERTS, :].bitcast(BF16)).then_inc(s.wT, 1)
    dve.wait_ge(s.wb, EXPERTS * STEPS)

    def pair(ep):
        for i in range(2 * STEPS):
            t = i % STEPS
            g = 2 * STEPS * ep + i
            off = (2 * ep + i // STEPS) * TOK + t * T
            cols = slice(off, off + T) if isinstance(off, int) else bass.ds(off, T)
            dve.wait_ge(s.y_ps, g + 1)
            wait(dve, s.acc, g - 1)
            dve.scalar_tensor_tensor(out=f.part[:, i % 2, :], in0=f.y_ps[i % 2][:],
                                     scalar=f.w[i // STEPS][:, EW - 1:EW], in1=f.wb[:, cols],
                                     op0=ALU.add, op1=ALU.mult).then_inc(s.part, 1)
            dve.wait_ge(s.part, g + 1)
            xc = x[:, t * T:(t + 1) * T]
            dve.tensor_tensor(xc, xc, f.part[:, i % 2, :], ALU.add).then_inc(s.acc, 1)

    pair(0)
    with dve.Fori(1, EXPERTS // 2) as ep:
        pair(ep)


UNITS = 2 * TB
INV2PI = float(np.float32(1 / (2 * np.pi)))
MAGIC = float(1.5 * 2 ** 23)
PI2_A = 6.28125
PI2_B = float(np.float32(2 * np.pi - PI2_A))
PI2_C = float(np.float32(2 * np.pi - PI2_A - PI2_B))
PI_BELOW = 3.1415925


def attention_semaphores(sem, phase):
    s = Group()
    s.w = sem(phase + "_w")
    s.qk_ps = sem(phase + "_qk_ps")
    s.qk = sem(phase + "_qk")
    s.sq = sem(phase + "_sq")
    s.nrm_ps = sem(phase + "_nrm_ps")
    s.ex = sem(phase + "_ex")
    s.sc = sem(phase + "_sc")
    s.v_ps = sem(phase + "_v_ps")
    s.vs = sem(phase + "_vs")
    s.va = sem(phase + "_va")
    s.f_ps = sem(phase + "_f_ps")
    s.t1 = sem(phase + "_t1")
    s.kk = sem(phase + "_kk")
    s.r1 = sem(phase + "_r1")
    s.r2 = sem(phase + "_r2")
    s.r3 = sem(phase + "_r3")
    s.r = sem(phase + "_r")
    s.sn = sem(phase + "_sn")
    s.ab = sem(phase + "_ab")
    s.cs = sem(phase + "_cs")
    s.kv_ps = sem(phase + "_kv_ps")
    s.kvm = sem(phase + "_kvm")
    s.o_ps = sem(phase + "_o_ps")
    s.on = sem(phase + "_on")
    s.oz = sem(phase + "_oz")
    s.orz = sem(phase + "_orz")
    s.od = sem(phase + "_od")
    s.oT_ps = sem(phase + "_oT_ps")
    s.oT = sem(phase + "_oT")
    s.fin_ps = sem(phase + "_fin_ps")
    s.fin = sem(phase + "_fin")
    return s


def att_loads(sp, s, k, a, d):
    sp.dma_start(a.w[:], d.aw).then_inc(s.w, 16)


def unit_of(u):
    if u < TB:
        return True, u // (TB // BATCH), u // 4, u
    return False, (u - TB) // (UNITS // 4), (u - TB) // GROUPS, (u - TB) % GROUPS


def att_tensor(pe, s, k, a, xn, ln_out, r):
    pe.wait_ge(s.w, 16)
    pe.wait_ge(ln_out, CHUNKS * (r + 1))
    for c in range(CHUNKS):
        for i in range(2):
            wait(pe, s.sq, 2 * (c - 1) + i + 1)
            pe.matmul(a.ps[i][:], a.w[:, i * P:(i + 1) * P], xn[:, c * T:(c + 1) * T],
                      start=True, stop=True).then_inc(s.qk_ps, 1)
    pe.wait_ge(s.sq, 2 * CHUNKS)
    for i in range(2):
        for b in range(TB):
            o = (i * TB + b) * HEADS
            mm = pe.matmul(a.kv_ps[0][:, o:o + HEADS], a.sq[:, i, b * P:(b + 1) * P], a.w[:, A_HS:A_HS + HEADS],
                           start=True, stop=True)
    mm.then_inc(s.nrm_ps, 1)
    for c in range(CHUNKS):
        wait(pe, s.vs, c - 1)
        for b in range(4):
            mm = pe.matmul(a.ps[c % 2][:, b * P:(b + 1) * P], xn[:, c * T + b * P:c * T + (b + 1) * P],
                           a.w[:, 2 * P:3 * P], start=True, stop=True)
        mm.then_inc(s.v_ps, 1)

    def angles(u):
        key, b, c, i = unit_of(u)
        wait(pe, s.r1, u - 1)
        if key:
            pe.matmul(a.f_ps[u % 2][:], a.qk[:, 1, i * P:(i + 1) * P], a.w[:, A_RF:A_RF + HEADS * M],
                      start=True, stop=True).then_inc(s.f_ps, 1)
        else:
            pe.matmul(a.f_ps[u % 2][:], a.w[:, A_RF + i * P:A_RF + (i + 1) * P], a.qk[:, 0, c * T:(c + 1) * T],
                      start=True, stop=True).then_inc(s.f_ps, 1)

    def keys(u):
        _, b, _, i = unit_of(u)
        per = TB // BATCH
        if i == 0:
            pe.wait_ge(s.sc, 4)
            pe.wait_ge(s.va, CHUNKS)
        for j, (trig, done) in enumerate(((a.cs, s.cs), (a.sn, s.sn))):
            pe.wait_ge(done, u + 1)
            for g in range(GROUPS):
                o = (j * GROUPS + g) * HG * VW
                mm = pe.matmul(a.kv_ps[b][:, o:o + HG * VW], trig[:, u % 2, g * P:(g + 1) * P],
                               a.va[:, i, g * HG * VW:(g + 1) * HG * VW],
                               start=(i % per == 0 and j == 0 and g == 0), stop=(i % per == per - 1),
                               skip_group_check=True)
        mm.then_inc(s.kv_ps, 1)

    def queries(u):
        _, b, c, g = unit_of(u)
        pe.wait_ge(s.kvm, b + 1)
        pe.wait_ge(s.cs, u + 1)
        pe.wait_ge(s.sn, u + 1)
        if g == 0:
            wait(pe, s.on, 2 * c)
        for t in range(4):
            o = (t % 2) * HEADS * VW + g * HG * VW
            for j, trig in enumerate((a.cs, a.sn)):
                mm = pe.matmul(a.o_ps[t // 2][:, o:o + HG * VW], trig[:, u % 2, t * P:(t + 1) * P],
                               a.kvm[:, b, j * GROUPS + g, :], start=(j == 0), stop=(j == 1),
                               skip_group_check=True)
        mm.then_inc(s.o_ps, 1)

    def out(c):
        pe.wait_ge(s.od, c + 1)
        wait(pe, s.oT, c)
        for t in range(4):
            mm = pe.transpose(a.ps[0][:, t * P:(t + 1) * P], a.od[:, t, :], k.ident[:])
        mm.then_inc(s.oT_ps, 1)
        pe.wait_ge(s.oT, c + 1)
        wait(pe, s.fin, c)
        pe.matmul(a.ps[1][:], a.w[:, 3 * P:4 * P], a.oT[:], start=True, stop=True).then_inc(s.fin_ps, 1)

    angles(0)
    for u in range(UNITS):
        key, b, c, i = unit_of(u)
        if u + 1 < UNITS:
            angles(u + 1)
        if key:
            keys(u)
        else:
            queries(u)
            if i == GROUPS - 1:
                out(c)


def att_scalar(act, s, k, a):
    for c in range(CHUNKS):
        for i in range(2):
            n = 2 * c + i
            act.wait_ge(s.qk_ps, n + 1)
            act.activation(a.qk[:, i, c * T:(c + 1) * T], a.ps[i][:], ACT.Copy).then_inc(s.qk, 1)
            act.activation(a.sq[:, i, c * T:(c + 1) * T], a.ps[i][:], ACT.Square).then_inc(s.sq, 1)
    act.wait_ge(s.nrm_ps, 1)
    act.activation(a.ex[:], a.kv_ps[0][:], ACT.Exp, scale=-0.5).then_inc(s.ex, 1)
    for u in range(UNITS + 1):
        if u >= 1:
            key, b, c, i = unit_of(u - 1)
            if not key and i == GROUPS - 1:
                act.wait_ge(s.oT_ps, c + 1)
                act.activation(a.oT[:], a.ps[0][:], ACT.Copy).then_inc(s.oT, 1)
        if u == UNITS:
            break
        act.wait_ge(s.r, u + 1)
        if u >= 2:
            key = unit_of(u - 2)[0]
            act.wait_ge(s.kv_ps if key else s.o_ps, u - 1 if key else u - 1 - TB)
        act.activation(a.sn[:, u % 2, :], a.r[:, u % 2, :], ACT.Sin).then_inc(s.sn, 1)
        wait(act, s.cs, u)
        act.activation(a.ab[:], a.r[:, u % 2, :], ACT.Abs).then_inc(s.ab, 1)
        act.wait_ge(s.ab, u + 1)
        act.activation(a.cs[:, u % 2, :], a.ab[:], ACT.Sin, bias=k.const[:, C_HPI:C_HPI + 1],
                       scale=-1.0).then_inc(s.cs, 1)


def att_vector(dve, s, k, a, x):
    dve.wait_ge(s.ex, 1)
    dve.tensor_scalar(a.sc[:], a.ex[:], float(M) ** -0.5, None, ALU.mult).then_inc(s.sc, 1)
    dve.wait_ge(s.sc, 1)
    ks = a.sc[:, TB * HEADS:].rearrange("p (b h o) -> p b h o", h=HEADS, o=1)
    va = a.va[:].rearrange("p b (h v) -> p b h v", v=VW)
    for part in range(1):
        dve.tensor_copy(va[:, :, :, DH:VW], ks).then_inc(s.sc, 3)
    for c in range(CHUNKS):
        dve.wait_ge(s.v_ps, c + 1)
        for b in range(4):
            i = dve.tensor_tensor(va[:, 4 * c + b, :, 0:DH],
                                  a.ps[c % 2][:, b * P:(b + 1) * P].rearrange("p (h v) -> p h v", v=DH),
                                  ks[:, 4 * c + b, :, :].broadcast_to([P, HEADS, DH]), ALU.mult)
        i.then_inc(s.vs, 1)
        dve.wait_ge(s.vs, c + 1)
        dve.sem_inc(s.va, 1)

    def reduce(u):
        b = u % 2
        dve.wait_ge(s.f_ps, u + 1)
        dve.tensor_scalar(a.t1[:], a.f_ps[b][:], INV2PI, MAGIC, ALU.mult, ALU.add).then_inc(s.t1, 1)
        dve.wait_ge(s.t1, u + 1)
        dve.tensor_scalar(a.t1[:], a.t1[:], MAGIC, None, ALU.subtract).then_inc(s.kk, 1)
        dve.wait_ge(s.kk, u + 1)
        wait(dve, s.cs, u - 1)
        dve.scalar_tensor_tensor(out=a.r[:, b, :], in0=a.t1[:], scalar=-PI2_A, in1=a.f_ps[b][:],
                                 op0=ALU.mult, op1=ALU.add).then_inc(s.r1, 1)
        dve.wait_ge(s.r1, u + 1)
        dve.scalar_tensor_tensor(out=a.r[:, b, :], in0=a.t1[:], scalar=-PI2_B, in1=a.r[:, b, :],
                                 op0=ALU.mult, op1=ALU.add).then_inc(s.r2, 1)
        dve.wait_ge(s.r2, u + 1)
        dve.scalar_tensor_tensor(out=a.r[:, b, :], in0=a.t1[:], scalar=-PI2_C, in1=a.r[:, b, :],
                                 op0=ALU.mult, op1=ALU.add).then_inc(s.r3, 1)
        dve.wait_ge(s.r3, u + 1)
        dve.tensor_scalar(a.r[:, b, :], a.r[:, b, :], PI_BELOW, -PI_BELOW, ALU.min, ALU.max).then_inc(s.r, 1)

    def mask_kv(b):
        dve.wait_ge(s.kv_ps, (b + 1) * (TB // BATCH))
        w = HG * VW
        dve.tensor_tensor(a.kvm[:, b], a.kv_ps[b][:, 0:2 * GROUPS * w].rearrange("p (g v) -> p g v", v=w),
                          a.w[:, A_MASK:A_MASK + w].rearrange("p (o v) -> p o v", o=1).broadcast_to([P, 2 * GROUPS, w]),
                          ALU.mult).then_inc(s.kvm, 1)

    def divide(c):
        dve.wait_ge(s.o_ps, GROUPS * (c + 1))
        qs = a.sc[:, 4 * c * HEADS:4 * (c + 1) * HEADS].rearrange("p (h o) -> p h o", o=1)
        on = a.on[:].rearrange("p (h v) -> p h v", v=VW)
        n = 2 * HEADS
        wait(dve, s.od, c)
        for t in range(2):
            dve.tensor_tensor(on[:, t * n:(t + 1) * n, :],
                              a.o_ps[t][:, 0:n * VW].rearrange("p (h v) -> p h v", v=VW),
                              qs[:, t * n:(t + 1) * n, :].broadcast_to([P, n, VW]), ALU.mult).then_inc(s.on, 1)
        dve.wait_ge(s.on, 2 * c + 2)
        dve.tensor_scalar(a.z[:].rearrange("p (h o) -> p h o", o=1), on[:, :, DH:VW], 1e-6, None,
                          ALU.max).then_inc(s.oz, 1)
        dve.wait_ge(s.oz, c + 1)
        dve.reciprocal(a.rz[:], a.z[:]).then_inc(s.orz, 1)
        dve.wait_ge(s.orz, c + 1)
        wait(dve, s.oT_ps, c)
        dve.tensor_tensor(a.od[:].rearrange("p t (h v) -> p (t h) v", v=DH), on[:, :, 0:DH],
                          a.rz[:].rearrange("p (h o) -> p h o", o=1).broadcast_to([P, 4 * HEADS, DH]),
                          ALU.mult).then_inc(s.od, 1)

    def residual(c):
        dve.wait_ge(s.fin_ps, c + 1)
        xc = x[:, c * T:(c + 1) * T]
        dve.tensor_tensor(xc, xc, a.ps[1][:], ALU.add).then_inc(s.fin, 1)

    for u in range(UNITS):
        key, b, c, i = unit_of(u)
        reduce(u)
        if u >= 1:
            key, b, c, i = unit_of(u - 1)
            if key and i % (TB // BATCH) == TB // BATCH - 1:
                mask_kv(b)
            if not key and i == GROUPS - 1:
                divide(c)
                residual(c)
    divide(CHUNKS - 1)
    residual(CHUNKS - 1)


def state_space_semaphores(sem, phase):
    s = Group()
    s.wp = sem(phase + "_wp")
    s.wa = sem(phase + "_wa")
    s.wo = sem(phase + "_wo")
    s.weff = sem(phase + "_weff")
    s.x = sem(phase + "_x")
    s.sq = sem(phase + "_sq")
    s.ms = sem(phase + "_ms")
    s.ln = sem(phase + "_ln")
    s.rstd = sem(phase + "_rstd")
    s.pad = sem(phase + "_pad")
    s.hn = sem(phase + "_hn")
    s.xc_ps = sem(phase + "_xc_ps")
    s.xc = sem(phase + "_xc")
    s.z_ps = sem(phase + "_z_ps")
    s.z = sem(phase + "_z")
    s.bcp_ps = sem(phase + "_bcp_ps")
    s.dtr_ps = sem(phase + "_dtr_ps")
    s.hi = sem(phase + "_hi")
    s.dtr = sem(phase + "_dtr")
    s.r1 = sem(phase + "_r1")
    s.mid = sem(phase + "_mid")
    s.bc = sem(phase + "_bc")
    s.d_ps = sem(phase + "_d_ps")
    s.xb = sem(phase + "_xb")
    s.ab = sem(phase + "_ab")
    s.ey = sem(phase + "_ey")
    s.ll = sem(phase + "_ll")
    s.dd = sem(phase + "_dd")
    s.t = sem(phase + "_t")
    s.s1 = sem(phase + "_s1")
    s.delta = sem(phase + "_delta")
    s.u = sem(phase + "_u")
    s.a1 = sem(phase + "_a1")
    s.aneg = sem(phase + "_aneg")
    s.bc_ps = sem(phase + "_bc_ps")
    s.bcs = sem(phase + "_bcs")
    s.a = sem(phase + "_a")
    s.bx = sem(phase + "_bx")
    s.h = sem(phase + "_h")
    s.carry = sem(phase + "_carry")
    s.pd = sem(phase + "_pd")
    s.pp = sem(phase + "_pp")
    s.y_acc = sem(phase + "_y_acc")
    s.yd = sem(phase + "_yd")
    s.gate = sem(phase + "_gate")
    s.out_ps = sem(phase + "_out_ps")
    return s


def build(nc, d):
    with ExitStack() as keep:
        def sb(name, shape, dt=F32, where=keep):
            return where.enter_context(nc.sbuf_tensor(name, shape, dt))

        def psum(name, shape, dt=F32, where=keep):
            return where.enter_context(nc.psum_tensor(name, shape, dt))

        k = Group()
        x0 = sb("x0", [P, TOK])
        xn = sb("xn", [P, TOK])
        k.mean_w = sb("mean_w", [P, P])
        k.const = sb("const", [P, NCONST])
        k.ident = sb("ident", [P, P])
        k.ident_b = sb("ident_b", [P, P], BF16)
        k.rank = sb("rank", [P, TOK // P * EXPERTS])
        e_sel = sb("e_sel", [NPAR * EXPERTS, EXPERTS, P], BF16)
        ln = Group()
        scope = ExitStack()
        sb("ln_past", [P, LOADED_AHEAD], mybir.dt.uint8, scope)
        ln.s = sb("ln_s", [P, TOK], F32, scope)
        ln.mean_ps = [psum(f"ln_mean_ps{c}", [P, T], F32, scope) for c in range(CHUNKS)]
        ln.var_ps = [psum(f"ln_var_ps{c}", [P, T], F32, scope) for c in range(CHUNKS)]
        scope.close()

        bank = [psum(f"bank{i}", [P, T]) for i in range(2)]

        def sem(name):
            return keep.enter_context(nc.semaphore(name))

        io = Group()
        io.x, io.consts, io.stored, io.merged, io.wr = (sem("io_" + n) for n in ("x", "consts", "stored", "merged", "wr"))

        m = Group()
        scope = ExitStack()
        def mb(name, shape, dt=F32):
            return sb("m_" + name, shape, dt, scope)
        bc_sel = mb("bc_sel", [NPAR * 2 * STATES, 2 * STATES, P], BF16)
        y_ps = psum("m_y_ps", [P, HALVES, T], F32, scope)
        bc_ps = [psum(f"m_bc_ps{i}", [P, 2, T], F32, scope) for i in range(2)]
        m.wp = mb("wp", [P, PW])
        m.wdt = mb("wdt", [RANK, INNER])
        m.cw = mb("cw", [P, TAPS * INNER])
        m.wo = mb("wo", [P, OW])
        m.alog = mb("alog", [P, HALVES * STATES])
        m.weff = mb("weff", [P, TAPS, INNER])
        m.a1 = mb("a1", [P, HALVES * STATES])
        m.aneg = mb("aneg", [P, HALVES * STATES])
        m.sq = mb("sq", [P, T])
        m.rstd = mb("rstd", [P, T])
        m.lnv = m.rstd
        m.hn = mb("hn", [P, TAPS - 1 + SEQ])
        m.xc = mb("xc", [P, 2, HALVES, T])
        m.z = mb("z", [P, 2, HALVES, T])
        m.hi = mb("hi", [NPAR * 2 * STATES, T], BF16)
        m.mid = mb("mid", [NPAR * 2 * STATES, T], BF16)
        m.r1 = mb("r1", [NPAR * 2 * STATES, T])
        m.bc = mb("bc", [NPAR * 2 * STATES, 2, T], BF16)
        m.dtr = mb("dtr", [RANK, T])
        m.xb = mb("xb", [P, HALVES, T])
        m.ab = mb("ab", [P, HALVES, T])
        m.ey = mb("ey", [P, HALVES, T])
        m.ll = m.ab
        m.dd = mb("dd", [P, HALVES, T])
        m.delta = mb("delta", [P, 2, HALVES, T])
        m.u = mb("u", [P, 2, HALVES, T])
        m.a = mb("a", [P, RING, HALVES, T])
        m.bcs = mb("bcs", [P, BC_RING, 2, T])
        m.bx = mb("bx", [P, RING, HALVES, T])
        m.h = mb("h", [P, RING, HALVES, T])
        m.p = mb("p", [P, RING, HALVES, T])
        m.carry = mb("carry", [P, HALVES, STATES])
        m.yd = m.xb
        m.yg = m.yd
        scope.close()
        s = state_space_semaphores(sem, "m")


        f = Group()
        scope = ExitStack()
        def fb(name, shape, dt=F32):
            return sb("f_" + name, shape, dt, scope)
        f.w = [fb(f"w{i}", [P, EW]) for i in range(2)]
        f.wr = fb("wr", [P, EXPERTS])
        f.wb = fb("wb", [P, EXPERTS * TOK])
        f.wT = fb("wT", [NPAR * EXPERTS, TOK], BF16)
        f.g = fb("g", [P, 2, HB, T])
        f.part = fb("part", [P, 2, T])
        f.c = [fb(f"c{i}", [P, TB]) for i in range(7)]
        f.sh, f.ex, f.p, f.p2, f.both, f.wt, f.wr1 = (
            fb(n, [P, TB * EXPERTS]) for n in ("sh", "ex", "p", "p2", "both", "wt", "wr1"))
        f.eq = [fb(f"eq{i}", [P, TB * EXPERTS]) for i in range(2)]
        f.sel = [fb(f"sel{i}", [P, TB * EXPERTS]) for i in range(2)]
        f.w3 = fb("w3", [P, TB, NPAR * EXPERTS], BF16)
        f.e_sel = e_sel
        f.h_ps = [psum(f"f_h_ps{i}", [P, T], F32, scope) for i in range(HB)]
        f.y_ps = [psum(f"f_y_ps{i}", [P, T], F32, scope) for i in range(2)]
        f.ps = bank
        scope.close()

        a = Group()
        scope = ExitStack()
        def ab(name, shape, dt=F32):
            return sb("a_" + name, shape, dt, scope)
        a.w = ab("w", [P, AW])
        a.qk = ab("qk", [P, 2, TOK])
        a.sq = ab("sq", [P, 2, TOK])
        a.ex = ab("ex", [P, 2 * TB * HEADS])
        a.sc = ab("sc", [P, 2 * TB * HEADS])
        a.va = ab("va", [P, TB, HEADS * VW])
        a.t1 = ab("t1", [P, T])
        a.r = ab("r", [P, 2, T])
        a.ab = ab("ab", [P, T])
        a.sn = ab("sn", [P, 2, T])
        a.cs = ab("cs", [P, 2, T])
        a.kvm = ab("kvm", [P, BATCH, 2 * GROUPS, HG * VW])
        a.on = ab("on", [P, 4 * HEADS * VW])
        a.z = ab("z", [P, 4 * HEADS])
        a.rz = ab("rz", [P, 4 * HEADS])
        a.od = ab("od", [P, 4, P])
        a.oT = ab("oT", [P, T])
        a.f_ps = [psum(f"a_f_ps{i}", [P, T], F32, scope) for i in range(2)]
        a.kv_ps = [psum(f"a_kv_ps{i}", [P, T], F32, scope) for i in range(2)]
        a.o_ps = [psum(f"a_o_ps{i}", [P, T], F32, scope) for i in range(2)]
        a.ps = bank
        scope.close()

        l = norm_semaphores(sem, "l")
        e1, e2 = (expert_semaphores(sem, n) for n in ("e1", "e2"))
        at = attention_semaphores(sem, "at")

        block = keep.enter_context(nc.Block())
        k.x = lambda c: x0[:, c * T:(c + 1) * T]

        def xcols(j, c):
            off = (j % BATCH) * SEQ + c * T
            return bass.ds(off, T) if not isinstance(off, int) else slice(off, off + T)

        def product_wait(eng, kk, n):
            if n < 0:
                kk, n = kk - 1, n + STATES
            if isinstance(kk, int) and kk < 0:
                return
            if n in POOL_N:
                eng.wait_ge(s.pp, len(POOL_N) * kk + POOL_N.index(n) + 1)
            else:
                eng.wait_ge(s.pd, len(DVE_N) * kk + DVE_N.index(n) + 1)

        def ahead(j, c, n):
            if n < STATES:
                return j, c, n
            return (j, 1, n - STATES) if c == 0 else (j + 1, 0, n - STATES)

        def back(j, c, n, lag):
            kk = 2 * j + c
            if n >= lag:
                return c, n - lag, kk
            if isinstance(kk, int) and kk == 0:
                return None
            return 1 - c, n - lag + STATES, kk - 1

        @block.sync
        def _(sp):
            for name, dst in (("x", x0),):
                for c in range(CHUNKS):
                    sp.dma_start(x0[:, c * T:(c + 1) * T], d.x[:, c * T:(c + 1) * T]).then_inc(io.x, 16)
            sp.dma_start(k.mean_w[:], d.mean_w).then_inc(io.consts, 16)
            sp.dma_start(k.const[:], d.const).then_inc(io.consts, 16)
            sp.dma_start(k.ident[:], d.ident).then_inc(io.consts, 16)
            sp.dma_start(bc_sel[:].bitcast(mybir.dt.uint16), d.bc_sel).then_inc(io.consts, 16)
            sp.dma_start(k.ident_b[:].bitcast(mybir.dt.uint16), d.ident_b).then_inc(io.consts, 16)
            sp.dma_start(k.rank[:], d.rank).then_inc(io.consts, 16)
            sp.dma_start(e_sel[:].bitcast(mybir.dt.uint16), d.e_sel).then_inc(io.consts, 16)

            def load_p(l):
                sp.dma_start(m.wp[:], d.wp[l]).then_inc(s.wp, 16)
                sp.dma_start(m.wdt[:], d.wdt[l]).then_inc(s.wp, 16)
                sp.dma_start(m.cw[:], d.cw[l].broadcast_to([P, TAPS * INNER])).then_inc(s.wp, 16)

            def load_a(l):
                sp.dma_start(m.alog[:], d.alog[l]).then_inc(s.wa, 16)

            def load_o(l):
                sp.dma_start(m.wo[:], d.wo[l]).then_inc(s.wo, 16)

            def layer(l):
                q = 2 * l
                wait(sp, s.xb, 4 * q)
                load_p(l)
                wait(sp, s.aneg, q)
                load_a(l)
                wait(sp, s.x, 2 * q + (CHUNKS if not (isinstance(q, int) and q == 0) else 0))
                load_o(l)
                sp.wait_ge(s.wp, 48 * q + 48)
                sp.sem_inc(s.wp, 48)
                sp.wait_ge(s.wa, 16 * q + 16)
                sp.sem_inc(s.wa, 16)
                sp.wait_ge(s.wo, 16 * q + 16)
                sp.sem_inc(s.wo, 16)

            layer(0)
            with sp.Fori(1, LAYERS) as i:
                layer(i)
            sp.wait_ge(io.merged, CHUNKS)
            sp.dma_start(f.wr[:], d.wr).then_inc(io.wr, 16)
            ffn_loads(sp, e1, k, f, d)
            sp.wait_ge(e1.acc, EXPERTS * STEPS)
            att_loads(sp, at, k, a, d)
            sp.wait_ge(at.fin, CHUNKS)
            sp.dma_start(f.wr[:], d.wr).then_inc(io.wr, 16)
            ffn_loads(sp, e2, k, f, d)
            for c in range(CHUNKS):
                sp.wait_ge(e2.acc, (EXPERTS - 1) * STEPS + c + 1)
                sp.dma_start(d.out[:, c * T:(c + 1) * T], x0[:, c * T:(c + 1) * T]).then_inc(io.stored, 16)
            sp.wait_ge(io.stored, 16 * CHUNKS)

        @block.tensor
        def _(pe):
            pe.wait_ge(io.consts, 112)
            pe.wait_ge(io.x, 16 * CHUNKS)
            ln_tensor(pe, l, k, ln, 0)

            def project(j, c, piece, h=None, part=None):
                kk = 2 * j + c
                if piece == "ms":
                    pe.wait_ge(s.sq, kk + 1)
                    wait(pe, s.xb, 2 * kk)
                    pe.matmul(bank[1][:], k.mean_w[:], m.sq[:], start=True, stop=True).then_inc(s.ms, 1)
                elif piece == "conv":
                    pe.wait_ge(s.hn, kk + 1)
                    pe.wait_ge(s.weff, j + 1)
                    pe.wait_ge(s.pad, 1)
                    pe.wait_ge(s.ln, kk + 1)
                    for tap in range(part * TAPS // 2, (part + 1) * TAPS // 2):
                        mm = pe.matmul(bank[h][:], m.weff[:, tap, h * P:(h + 1) * P],
                                       m.hn[:, c * T + tap:c * T + tap + T],
                                       start=(tap == 0), stop=(tap == TAPS - 1))
                    if part == 1:
                        mm.then_inc(s.xc_ps, 1)
                elif piece == "z":
                    for h in (1, 0):
                        pe.wait_ge(s.xc, 2 * kk + 2 - h)
                        pe.matmul(bank[h][:], m.wp[:, INNER + h * P:INNER + (h + 1) * P],
                                  m.hn[:, c * T + TAPS - 1:c * T + TAPS - 1 + T],
                                  start=True, stop=True).then_inc(s.z_ps, 1)
                elif piece == "bc":
                    pe.wait_ge(s.z, 2 * kk + 2)
                    for h in range(HALVES):
                        o = O_WX + h * WX
                        mm = pe.matmul(bank[0][0:NPAR * 2 * STATES, :], m.wp[:, o:o + NPAR * 2 * STATES],
                                       m.xc[:, c, h, :], start=(h == 0), stop=(h == HALVES - 1))
                    mm.then_inc(s.bcp_ps, 1)
                elif piece == "rank":
                    for h in range(HALVES):
                        o = O_WX + h * WX + NPAR * 2 * STATES
                        mm = pe.matmul(bank[1][0:RANK, :], m.wp[:, o:o + RANK], m.xc[:, c, h, :],
                                       start=(h == 0), stop=(h == HALVES - 1))
                    mm.then_inc(s.dtr_ps, 1)
                elif piece == "dt":
                    pe.wait_ge(s.dtr, kk + 1)
                    pe.wait_ge(s.r1, kk + 1)
                    for h in range(HALVES):
                        pe.matmul(bank[h][:], m.wdt[:, h * P:(h + 1) * P], m.dtr[:],
                                  start=True, stop=True).then_inc(s.d_ps, 1)

            def out_proj(j, c):
                kk = 2 * j + c
                pe.wait_ge(s.gate, kk + 1)
                pe.wait_ge(s.wo, 16 * j + 16)
                for h in range(HALVES):
                    mm = pe.matmul(bank[0][:], m.wo[:, h * P:(h + 1) * P], m.yg[:, h, :],
                                   start=(h == 0), stop=(h == HALVES - 1))
                mm.then_inc(s.out_ps, 1)

            def accumulate(b):
                c, n, kk = b
                if n == 0:
                    wait(pe, s.yd, 2 * kk)
                product_wait(pe, kk, n)
                for h in range(HALVES):
                    mm = pe.matmul(y_ps[:, h, :], k.ident[:], m.p[:, n % RING, h, :],
                                   start=(n == 0), stop=(n == STATES - 1))
                mm.then_inc(s.y_acc, 1)

            def broadcast(j, c, n):
                j, c, n = ahead(j, c, n)
                kk = 2 * j + c
                if n == 0:
                    pe.wait_ge(s.bc, kk + 1)
                wait(pe, s.bcs, STATES * kk + n - 1)
                for w in range(2):
                    mm = pe.matmul(bc_ps[n % 2][:, w, :], bc_sel[:, w * STATES + n, :], m.bc[:, c, :],
                                   start=True, stop=True)
                mm.then_inc(s.bc_ps, 1)

            def pair(j, last):
                for c in range(2):
                    nxt = (j, 1) if c == 0 else (j + 1, 0)
                    more = c == 0 or not last
                    for n in range(STATES):
                        if n + BC_AHEAD < STATES or more:
                            broadcast(j, c, n + BC_AHEAD)
                        b = back(j, c, n, 3)
                        if b:
                            accumulate(b)
                        if n == 4 and back(j, c, 0, 1):
                            out_proj(j if c == 1 else j - 1, 1 - c)
                        if more and n in WHEN_PE:
                            if n == 6 and not (isinstance(j, int) and j == 0 and c == 0):
                                pe.wait_ge(s.x, CHUNKS + 2 * j + c)
                            project(*nxt, *WHEN_PE[n])
                        if n == MEAN_AT and not last:
                            project(j + 1, c, "ms")

            WHEN_PE = {1: ("conv", 1, 0), 2: ("conv", 1, 1), 6: ("conv", 0, 0), 7: ("conv", 0, 1),
                       8: ("z",), 9: ("bc",), 10: ("rank",), 11: ("dt",)}
            project(0, 0, "ms")
            for piece in WHEN_PE.values():
                project(0, 0, *piece)
            project(0, 1, "ms")
            for n in range(BC_AHEAD):
                broadcast(0, 0, n)
            pair(0, False)
            with pe.Fori(1, PAIRS - 1) as j:
                pair(j, False)
            pair(PAIRS - 1, True)
            for n in range(STATES - 3, STATES):
                accumulate((1, n, 2 * PAIRS - 1))
            out_proj(PAIRS - 1, 1)

            pe.wait_ge(io.merged, CHUNKS)
            ln_tensor(pe, l, k, ln, 1)
            pe.wait_ge(io.wr, 16)
            ffn_tensor(pe, e1, k, f, xn, l.out, 1)
            pe.wait_ge(e1.acc, EXPERTS * STEPS)
            ln_tensor(pe, l, k, ln, 2)
            att_tensor(pe, at, k, a, xn, l.out, 2)
            pe.wait_ge(at.fin, CHUNKS)
            ln_tensor(pe, l, k, ln, 3)
            pe.wait_ge(io.wr, 32)
            ffn_tensor(pe, e2, k, f, xn, l.out, 3)

        @block.scalar
        def _(act):
            act.wait_ge(io.consts, 112)
            ln_scalar(act, l, k, ln, 0, xn)

            def project(j, c, piece):
                kk = 2 * j + c
                if piece == "sq":
                    act.wait_ge(s.x, kk + 1)
                    act.activation(m.sq[:], xn[:, xcols(j, c)], ACT.Square).then_inc(s.sq, 1)
                elif piece == "rstd":
                    act.wait_ge(s.ms, kk + 1)
                    wait(act, s.hn, kk)
                    act.activation(m.lnv[:], bank[1][:], ACT.Ln, bias=k.const[:, C_EPS:C_EPS + 1]).then_inc(s.ln, 1)
                    act.wait_ge(s.ln, kk + 1)
                    act.activation(m.rstd[:], m.lnv[:], ACT.Exp, scale=-0.5).then_inc(s.rstd, 1)
                elif piece == "silu":
                    wait(act, s.gate, kk - 1)
                    act.wait_ge(s.wp, 48 * j + 48)
                    for h in (1, 0):
                        act.wait_ge(s.xc_ps, 2 * kk + 2 - h)
                        act.activation(m.xc[:, c, h, :], bank[h][:], ACT.Silu,
                                       bias=m.wp[:, O_CB + h:O_CB + h + 1]).then_inc(s.xc, 1)
                    for h in (1, 0):
                        act.wait_ge(s.z_ps, 2 * kk + 2 - h)
                        act.activation(m.z[:, c, h, :], bank[h][:], ACT.Silu).then_inc(s.z, 1)
                elif piece == "parts":
                    act.wait_ge(s.bcp_ps, kk + 1)
                    act.activation(m.hi[:], bank[0][0:NPAR * 2 * STATES, :], ACT.Copy).then_inc(s.hi, 1)
                elif piece == "rank":
                    act.wait_ge(s.dtr_ps, kk + 1)
                    act.activation(m.dtr[:], bank[1][0:RANK, :], ACT.Copy).then_inc(s.dtr, 1)
                elif piece == "softplus":
                    for h in range(HALVES):
                        act.wait_ge(s.d_ps, 2 * kk + 1 + h)
                        act.activation(m.xb[:, h, :], bank[h][:], ACT.Identity,
                                       bias=m.wp[:, O_BDT + h:O_BDT + h + 1]).then_inc(s.xb, 1)
                elif piece == "log1p":
                    act.wait_ge(s.xb, 2 * kk + 2)
                    wait(act, s.s1, kk)
                    act.activation(m.ab[:], m.xb[:], ACT.Abs).then_inc(s.ab, 1)
                    act.wait_ge(s.ab, kk + 1)
                    act.activation(m.ey[:], m.ab[:], ACT.Exp, scale=-1.0).then_inc(s.ey, 1)
                    act.wait_ge(s.ey, kk + 1)
                    act.activation(m.ll[:], m.ey[:], ACT.Ln, bias=1.0).then_inc(s.ll, 1)

            def decay_weights(j):
                act.wait_ge(s.wa, 16 * j + 16)
                act.activation(m.a1[:], m.alog[:], ACT.Exp).then_inc(s.a1, 1)
                act.wait_ge(s.a1, j + 1)
                act.activation(m.aneg[:], m.a1[:], ACT.Copy, scale=-1.0).then_inc(s.aneg, 1)
                act.wait_ge(s.aneg, j + 1)

            def copy(j, c, n):
                j, c, n = ahead(j, c, n)
                kk = 2 * j + c
                act.wait_ge(s.bc_ps, STATES * kk + n + 1)
                product_wait(act, kk, n - BC_RING)
                act.activation(m.bcs[:, n % BC_RING, :, :], bc_ps[n % 2][:], ACT.Copy).then_inc(s.bcs, 1)

            def decay(j, c, n):
                g = STATES * (2 * j + c) + n
                if n == 0:
                    act.wait_ge(s.delta, 2 * j + c + 1)
                wait(act, s.h, g - RING + 1)
                for h in range(HALVES):
                    a = act.activation(m.a[:, n % RING, h, :], m.delta[:, c, h, :], ACT.Exp,
                                       scale=m.aneg[:, h * STATES + n:h * STATES + n + 1])
                a.then_inc(s.a, 1)

            def pair(j, last):
                decay_weights(j)
                for c in range(2):
                    nxt = (j, 1) if c == 0 else (j + 1, 0)
                    more = c == 0 or not last
                    for n in range(STATES):
                        if n + COPY_AHEAD < STATES or more:
                            copy(j, c, n + COPY_AHEAD)
                        decay(j, c, n)
                        if more and n in WHEN_ACT:
                            project(*nxt, WHEN_ACT[n])
                        if n == MEAN_AT - 1 and not last:
                            project(j + 1, c, "sq")
                        if n == MEAN_AT and not last:
                            project(j + 1, c, "rstd")

            WHEN_ACT = {8: "silu", 9: "parts", 10: "rank", 11: "softplus", MEAN_AT: "log1p"}
            project(0, 0, "sq")
            project(0, 0, "rstd")
            for piece in WHEN_ACT.values():
                project(0, 0, piece)
            project(0, 1, "sq")
            project(0, 1, "rstd")
            for n in range(COPY_AHEAD):
                copy(0, 0, n)
            pair(0, False)
            with act.Fori(1, PAIRS - 1) as j:
                pair(j, False)
            pair(PAIRS - 1, True)

            ln_scalar(act, l, k, ln, 1, xn)
            ffn_scalar(act, e1, k, f)
            ln_scalar(act, l, k, ln, 2, xn)
            att_scalar(act, at, k, a)
            ln_scalar(act, l, k, ln, 3, xn)
            ffn_scalar(act, e2, k, f)

        @block.vector
        def _(dve):
            dve.memset(m.hn[:, 0:TAPS - 1], 0.0).then_inc(s.pad, 1)
            dve.wait_ge(io.x, 16 * CHUNKS)
            ln_vector(dve, l, k, ln, 0, xn, s.x)

            def project(j, c, piece):
                kk = 2 * j + c
                if piece == "hn":
                    dve.wait_ge(s.rstd, kk + 1)
                    dve.wait_ge(s.wp, 48 * j + 48)
                    wait(dve, s.z_ps, 2 * kk)
                    dve.scalar_tensor_tensor(out=m.hn[:, TAPS - 1 + c * T:TAPS - 1 + (c + 1) * T],
                                             in0=xn[:, xcols(j, c)], scalar=m.wp[:, O_NORM:O_NORM + 1],
                                             in1=m.rstd[:], op0=ALU.mult, op1=ALU.mult).then_inc(s.hn, 1)
                elif piece == "parts":
                    nb = NPAR * 2 * STATES
                    dve.wait_ge(s.hi, kk + 1)
                    dve.scalar_tensor_tensor(out=m.r1[:], in0=m.hi[:], scalar=k.const[0:nb, C_M1:C_M1 + 1],
                                             in1=bank[0][0:nb, :], op0=ALU.mult, op1=ALU.add).then_inc(s.r1, 1)
                    dve.wait_ge(s.r1, kk + 1)
                    dve.tensor_copy(m.mid[:], m.r1[:]).then_inc(s.mid, 1)
                    dve.wait_ge(s.mid, kk + 1)
                    dve.scalar_tensor_tensor(out=m.bc[:, c, :], in0=m.mid[:], scalar=k.const[0:nb, C_M2:C_M2 + 1],
                                             in1=m.r1[:], op0=ALU.mult, op1=ALU.add).then_inc(s.bc, 1)
                elif piece == "lost":
                    dve.wait_ge(s.ey, kk + 1)
                    dve.tensor_scalar(m.dd[:], m.ey[:], 1.0, -1.0, ALU.add, ALU.add).then_inc(s.dd, 1)
                    dve.wait_ge(s.dd, kk + 1)
                    dve.scalar_tensor_tensor(out=m.dd[:], in0=m.dd[:], scalar=-1.0, in1=m.ey[:],
                                             op0=ALU.mult, op1=ALU.add).then_inc(s.t, 1)
                elif piece == "delta":
                    dve.wait_ge(s.ll, kk + 1)
                    dve.scalar_tensor_tensor(out=m.delta[:, c], in0=m.xb[:], scalar=0.0, in1=m.ll[:],
                                             op0=ALU.max, op1=ALU.add).then_inc(s.s1, 1)
                    dve.wait_ge(s.t, kk + 1)
                    dve.wait_ge(s.s1, kk + 1)
                    dve.tensor_tensor(m.delta[:, c], m.delta[:, c], m.dd[:], ALU.add).then_inc(s.delta, 1)
                    dve.wait_ge(s.delta, kk + 1)
                    dve.tensor_tensor(m.u[:, c], m.delta[:, c], m.xc[:, c], ALU.mult).then_inc(s.u, 1)

            def gate(j, c):
                kk = 2 * j + c
                dve.wait_ge(s.y_acc, STATES * (kk + 1))
                dve.wait_ge(s.wo, 16 * j + 16)
                wait(dve, s.out_ps, kk)
                for h in range(HALVES):
                    dve.scalar_tensor_tensor(out=m.yd[:, h, :], in0=m.xc[:, c, h, :],
                                             scalar=m.wo[:, HALVES * P + h:HALVES * P + h + 1],
                                             in1=y_ps[:, h, :], op0=ALU.mult, op1=ALU.add).then_inc(s.yd, 1)
                dve.wait_ge(s.yd, 2 * kk + 2)
                dve.tensor_tensor(m.yg[:], m.yd[:], m.z[:, c], ALU.mult).then_inc(s.gate, 1)

            def residual(j, c):
                kk = 2 * j + c
                dve.wait_ge(s.out_ps, kk + 1)
                x = xn[:, xcols(j, c)]
                dve.tensor_tensor(x, x, bank[0][:], ALU.add).then_inc(s.x, 1)

            def scan(j, c, n):
                g = STATES * (2 * j + c) + n
                dve.wait_ge(s.a, g + 1)
                dve.wait_ge(s.bx, g + 1)
                product_wait(dve, 2 * j + c, n - RING)
                if c == 1:
                    dve.wait_ge(s.carry, STATES * j + n + 1)
                for h in range(HALVES):
                    init = 0.0 if c == 0 else m.carry[:, h, n:n + 1]
                    i = dve.tensor_tensor_scan(m.h[:, n % RING, h, :], m.a[:, n % RING, h, :],
                                               m.bx[:, n % RING, h, :], init, ALU.mult, ALU.add)
                i.then_inc(s.h, 1)

            def product(b):
                c, n, kk = b
                g = STATES * kk + n
                dve.wait_ge(s.h, g + 1)
                if c == 0:
                    dve.tensor_copy(m.carry[:, :, n:n + 1], m.h[:, n % RING, :, T - 1:T]).then_inc(s.carry, 1)
                if n in DVE_N:
                    wait(dve, s.y_acc, g - RING + 1)
                    cb = m.bcs[:, n % BC_RING, 1:2, :].broadcast_to([P, HALVES, T])
                    dve.tensor_tensor(m.p[:, n % RING], m.h[:, n % RING], cb, ALU.mult).then_inc(s.pd, 1)

            def pair(j, last):
                for c in range(2):
                    nxt = (j, 1) if c == 0 else (j + 1, 0)
                    more = c == 0 or not last
                    for n in range(STATES):
                        scan(j, c, n)
                        product((c, n, 2 * j + c))
                        tail = back(j, c, 0, 1)
                        if n == 2 and tail:
                            gate(j if c == 1 else j - 1, 1 - c)
                        if n == 5 and tail:
                            residual(j if c == 1 else j - 1, 1 - c)
                        if more and n in WHEN_DVE:
                            project(*nxt, WHEN_DVE[n])

            WHEN_DVE = {0: "hn", 10: "parts", 12: "lost", 13: "delta"}
            for piece in WHEN_DVE.values():
                project(0, 0, piece)
            pair(0, False)
            with dve.Fori(1, PAIRS - 1) as j:
                pair(j, False)
            pair(PAIRS - 1, True)
            gate(PAIRS - 1, 1)
            residual(PAIRS - 1, 1)
            dve.wait_ge(s.x, CHUNKS + 2 * PAIRS)
            for c in range(CHUNKS):
                cols = slice(c * T, (c + 1) * T)
                dve.tensor_tensor(x0[:, cols], x0[:, cols], xn[:, cols], ALU.add).then_inc(io.merged, 1)
            dve.wait_ge(io.merged, CHUNKS)
            ln_vector(dve, l, k, ln, 1, xn)
            ffn_vector(dve, e1, k, f, x0)
            dve.wait_ge(e1.acc, EXPERTS * STEPS)
            ln_vector(dve, l, k, ln, 2, xn)
            att_vector(dve, at, k, a, x0)
            dve.wait_ge(at.fin, CHUNKS)
            ln_vector(dve, l, k, ln, 3, xn)
            ffn_vector(dve, e2, k, f, x0)

        @block.gpsimd
        def _(pool):
            def fold(j):
                pool.wait_ge(s.wp, 48 * j + 48)
                wait(pool, s.z_ps, 4 * j)
                w = m.wp[:, 0:INNER].rearrange("p (a i) -> p a i", a=1).broadcast_to([P, TAPS, INNER])
                pool.tensor_tensor(m.weff[:], m.cw[:].rearrange("p (a i) -> p a i", a=TAPS), w,
                                   ALU.mult).then_inc(s.weff, 1)

            def spread_u(j, c, n):
                g = STATES * (2 * j + c) + n
                if n == 0:
                    pool.wait_ge(s.u, 2 * j + c + 1)
                pool.wait_ge(s.bcs, g + 1)
                wait(pool, s.h, g - RING + 1)
                bb = m.bcs[:, n % BC_RING, 0:1, :].broadcast_to([P, HALVES, T])
                pool.tensor_tensor(m.bx[:, n % RING], m.u[:, c], bb, ALU.mult).then_inc(s.bx, 1)

            def product(b):
                c, n, kk = b
                if n not in POOL_N:
                    return
                g = STATES * kk + n
                pool.wait_ge(s.h, g + 1)
                wait(pool, s.y_acc, g - RING + 1)
                cb = m.bcs[:, n % BC_RING, 1:2, :].broadcast_to([P, HALVES, T])
                pool.tensor_tensor(m.p[:, n % RING], m.h[:, n % RING], cb, ALU.mult).then_inc(s.pp, 1)

            def pair(j, last):
                for c in range(2):
                    for n in range(STATES):
                        spread_u(j, c, n)
                        b = back(j, c, n, 1)
                        if b:
                            product(b)
                        if c == 1 and n == 0 and not last:
                            fold(j + 1)

            fold(0)
            pair(0, False)
            with pool.Fori(1, PAIRS - 1) as j:
                pair(j, False)
            pair(PAIRS - 1, True)
            product((1, STATES - 1, 2 * PAIRS - 1))


def pack(inputs):
    get = lambda name: np.ascontiguousarray(inputs[name])
    BF16_ONE = np.uint16(0x3F80)
    a = {}
    a["x"] = np.ascontiguousarray(get("L0_attn_a_x").reshape(TOK, P).T)
    win = get("L0_attn_a_W_in").transpose(0, 2, 1)
    wx = get("L0_attn_a_W_x").transpose(0, 2, 1)
    bcw = wx[:, :, RANK:]
    wx = np.concatenate([bcw, bcw, bcw, wx[:, :, :RANK]], axis=2)
    halves = lambda v: v.reshape(LAYERS, HALVES, P, -1).transpose(0, 2, 1, 3).reshape(LAYERS, P, -1)
    a["wp"] = np.concatenate([win, halves(wx), get("L0_attn_a_norm_w")[:, :, None],
                              halves(get("L0_attn_a_conv_b")), halves(get("L0_attn_a_b_dt"))], axis=2)
    a["wdt"] = get("L0_attn_a_W_dt").transpose(0, 2, 1)
    a["cw"] = get("L0_attn_a_conv_w").transpose(0, 2, 1).reshape(LAYERS, 1, TAPS * INNER)
    a["alog"] = halves(get("L0_attn_a_A_log"))
    a["wo"] = np.concatenate([halves(get("L0_attn_a_W_out").transpose(0, 2, 1)), halves(get("L0_attn_a_D"))], axis=2)
    a["mean_w"] = np.full((P, P), 1.0 / P, np.float32)
    const = np.zeros((P, NCONST), np.float32)
    const[:, C_EPS] = EPS
    const[2 * STATES:, C_M1] = -1.0
    const[4 * STATES:, C_M2] = -1.0
    const[:, C_HPI] = np.pi / 2
    a["const"] = const
    sel = np.zeros((NPAR, 2 * STATES, 2 * STATES, P), np.float32)
    for i in range(2 * STATES):
        sel[:, i, i, :] = 1.0
    a["bc_sel"] = sel.reshape(NPAR * 2 * STATES, 2 * STATES, P).astype(np.uint16) * BF16_ONE
    a["ident"] = np.eye(P, dtype=np.float32)
    a["ident_b"] = np.eye(P, dtype=np.float32).astype(np.uint16) * BF16_ONE
    w2 = get("L0_ffn_w2").reshape(EXPERTS, HB, P, P).transpose(0, 2, 1, 3).reshape(EXPERTS, P, HB * P)
    b1 = get("L0_ffn_b1").reshape(EXPERTS, HB, P).transpose(0, 2, 1)
    a["ew"] = np.concatenate([get("L0_ffn_w1"), w2, b1, get("L0_ffn_b2")[:, :, None]], axis=2)
    a["wr"] = get("L0_ffn_w_router")
    a["rank"] = np.tile(np.arange(EXPERTS, 0, -1, dtype=np.float32), (P, TB))
    esel = np.zeros((NPAR, EXPERTS, EXPERTS, P), np.float32)
    for i in range(EXPERTS):
        esel[:, i, i, :] = 1.0
    a["e_sel"] = esel.reshape(NPAR * EXPERTS, EXPERTS, P).astype(np.uint16) * BF16_ONE
    rf = get("L0_attn_b_rf")
    bd = np.zeros((HEADS, DH, HEADS, M), rf.dtype)
    hs = np.zeros((HEADS, DH, HEADS), np.float32)
    for h in range(HEADS):
        bd[h, :, h, :] = rf.T
        hs[h, :, h] = 1.0
    mask = np.zeros((HG, M, HG, VW), np.float32)
    for h in range(HG):
        mask[h, :, h, :] = 1.0
    a["aw"] = np.concatenate([get("L0_attn_b_" + n).T for n in ("wq", "wk", "wv", "wo")]
                             + [bd.reshape(P, HEADS * M), hs.reshape(P, HEADS), mask.reshape(P, HG * VW)], axis=1)
    return {n: np.ascontiguousarray(v) for n, v in a.items()}


def kernel(**inputs):
    import concourse.bacc as _bacc
    from concourse.bass_utils import run_bass_kernel_spmd as _run

    nc = _bacc.Bacc("TRN2", target_bir_lowering=False, num_devices=1)
    arrays = pack(inputs)
    t = {n: nc.dram_tensor(f"in_{n}", a.shape, mybir.dt.from_np(a.dtype), kind="ExternalInput").ap()
             for n, a in arrays.items()}
    d = Group()
    d.x, d.out, d.mean_w, d.const, d.bc_sel, d.e_sel, d.ident, d.ident_b, d.rank = (
        t.get(n) for n in ("x", "out", "mean_w", "const", "bc_sel", "e_sel", "ident", "ident_b", "rank"))
    d.wp, d.wdt, d.cw, d.alog, d.wo, d.ew, d.wr, d.aw = (
        t.get(n) for n in ("wp", "wdt", "cw", "alog", "wo", "ew", "wr", "aw"))
    d.out = nc.dram_tensor("out", (P, TOK), F32, kind="ExternalOutput").ap()
    build(nc, d)
    r = _run(nc, [{f"in_{n}": a for n, a in arrays.items()}], core_ids=[0])
    out = r.results[0]["out"]
    return np.ascontiguousarray(out.T).reshape(BATCH, SEQ, P)
```

```python
from contextlib import ExitStack

import numpy as np
import concourse.bass as bass
from concourse import mybir

ALU = mybir.AluOpType
ACT = mybir.ActivationFunctionType
AX = mybir.AxisListType
F32 = mybir.dt.float32
BF16 = mybir.dt.bfloat16
F32R = mybir.dt.float32r

P = 128
BATCH, SEQ = 2, 1024
TOK = BATCH * SEQ
T = 512
CHUNKS = TOK // T
PHASE_BYTES = 108 * 1024
EPS = 1e-5

LAYERS = 4
INNER = 256
HALVES = INNER // P
RANK = 64
STATES = 16
TAPS = 4
PAIRS = LAYERS * BATCH
NPAR = 3
RING = 4
BC_RING = 8
BC_AHEAD = 3
COPY_AHEAD = 2
OUT_AT = 11
MEAN_AT = 12
HN_AT = 14
POOL_N = (1, 4, 7, 9, 12, 14)
DVE_N = tuple(n for n in range(STATES) if n not in POOL_N)

EXPERTS = 8
HIDDEN = 512
HB = HIDDEN // P
EW = HIDDEN + HB * P + HB + 1

HEADS = 16
DH = P // HEADS
M = 32
HG = P // M
GROUPS = HEADS // HG
VW = DH + 1

A_RF = 4 * P
A_HS = A_RF + HEADS * M
A_MASK = A_HS + HEADS
AW = A_MASK + HG * VW

O_WX = 2 * INNER
WX = NPAR * 2 * STATES + RANK
O_NORM = O_WX + HALVES * WX
O_CB = O_NORM + 1
O_BDT = O_CB + HALVES
PW = O_BDT + HALVES
OW = HALVES * P + HALVES

C_EPS, C_M1, C_M2, C_HPI, C_MAGIC, NCONST = 0, 1, 2, 3, 4, 5


class Group:
    pass


def wait(eng, sem, value):
    if isinstance(value, int) and value <= 0:
        return
    eng.wait_ge(sem, value)


def norm_semaphores(sem, phase):
    s = Group()
    s.mean = sem(phase + "_mean")
    s.cen = sem(phase + "_cen")
    s.sq = sem(phase + "_sq")
    s.var = sem(phase + "_var")
    s.ln = sem(phase + "_ln")
    s.rstd = sem(phase + "_rstd")
    s.out = sem(phase + "_out")
    return s


def ln_mean(pe, s, k, ln, c):
    pe.matmul(ln.ps[c][:], k.mean_w[:], k.x(c), start=True, stop=True).then_inc(s.mean, 1)


def ln_variance(pe, s, k, ln, r, c):
    pe.wait_ge(s.sq, CHUNKS * r + c + 1)
    pe.matmul(ln.ps[c][:], k.mean_w[:], ln.s[:, c * T:(c + 1) * T], start=True, stop=True).then_inc(s.var, 1)


def ln_scalar(act, s, k, ln, r, out):
    cols = [slice(c * T, (c + 1) * T) for c in range(CHUNKS)]
    for c in range(CHUNKS):
        act.wait_ge(s.cen, CHUNKS * r + c + 1)
        act.activation(ln.s[:, cols[c]], out[:, cols[c]], ACT.Square).then_inc(s.sq, 1)
    for c in range(CHUNKS):
        act.wait_ge(s.var, CHUNKS * r + c + 1)
        act.activation(ln.s[:, cols[c]], ln.ps[c][:], ACT.Ln, bias=k.const[:, C_EPS:C_EPS + 1]).then_inc(s.ln, 1)
    for c in range(CHUNKS):
        act.wait_ge(s.ln, CHUNKS * r + c + 1)
        act.activation(ln.s[:, cols[c]], ln.s[:, cols[c]], ACT.Exp, scale=-0.5).then_inc(s.rstd, 1)


def ln_center(dve, s, k, ln, r, out, c):
    dve.wait_ge(s.mean, CHUNKS * r + c + 1)
    dve.tensor_tensor(out[:, c * T:(c + 1) * T], k.x(c), ln.ps[c][:], ALU.subtract).then_inc(s.cen, 1)


def ln_scale(dve, s, ln, r, out, out_sem=None):
    cols = [slice(c * T, (c + 1) * T) for c in range(CHUNKS)]
    for c in range(CHUNKS):
        dve.wait_ge(s.rstd, CHUNKS * r + c + 1)
        dve.tensor_tensor(out[:, cols[c]], out[:, cols[c]], ln.s[:, cols[c]], ALU.mult).then_inc(s.out, 1)
        if out_sem:
            dve.wait_ge(s.out, CHUNKS * r + c + 1)
            dve.sem_inc(out_sem, 1)


STEPS = CHUNKS
TB = TOK // P


def expert_semaphores(sem, phase):
    s = Group()
    s.w0 = sem(phase + "_w0")
    s.w1 = sem(phase + "_w1")
    s.wh = sem(phase + "_wh")
    s.wl = sem(phase + "_wl")
    s.xh = sem(phase + "_xh")
    s.xl = sem(phase + "_xl")
    s.logits = sem(phase + "_logits")
    s.shift = sem(phase + "_shift")
    s.ex = sem(phase + "_ex")
    s.route = sem(phase + "_route")
    s.wlo = sem(phase + "_wlo")
    s.wT_ps = sem(phase + "_wT_ps")
    s.wT = sem(phase + "_wT")
    s.wb_ps = sem(phase + "_wb_ps")
    s.wb = sem(phase + "_wb")
    s.h_ps = sem(phase + "_h_ps")
    s.gel = sem(phase + "_gel")
    s.gh = sem(phase + "_gh")
    s.gl = sem(phase + "_gl")
    s.y_ps = sem(phase + "_y_ps")
    s.part = sem(phase + "_part")
    s.acc = sem(phase + "_acc")
    return s


def rows3(t):
    return t[:].rearrange("p (b e) -> p b e", e=EXPERTS)


def per_block(t):
    return t[:].rearrange("p (b o) -> p b o", o=1).broadcast_to([P, TB, EXPERTS])


def ffn_loads(sp, s, k, f, d):
    sp.dma_start(f.w[0][:], d.ew[0]).then_inc(s.w0, 16)
    sp.dma_start(f.w[1][:], d.ew[1]).then_inc(s.w1, 16)
    with sp.Fori(1, EXPERTS // 2) as ep:
        for i, ws in enumerate((s.w0, s.w1)):
            e = 2 * ep + i
            sp.wait_ge(s.part, STEPS * (e - 1))
            sp.dma_start(f.w[i][:], d.ew[e]).then_inc(ws, 16)


def ffn_tensor(pe, s, k, f, xn, ln_out, r, before_last=None):
    def logits():
        for b in range(TB):
            mm = pe.matmul(f.ps[0][:, b * EXPERTS:(b + 1) * EXPERTS], xn[:, b * P:(b + 1) * P], f.wr[:],
                           start=True, stop=True)
        mm.then_inc(s.logits, 1)

    def hidden(ep, i):
        e, t = i // STEPS, i % STEPS
        g = 2 * STEPS * ep + i
        cols = slice(t * T, (t + 1) * T)
        if t == 0:
            pe.wait_ge(s.wl, 2 * ep + e + 1)
        if isinstance(g, int) and g < STEPS:
            pe.wait_ge(s.xl, t + 1)
        for b in range(HB):
            rows = slice(b * P, (b + 1) * P)
            wait(pe, s.gel, HB * (g - 1) + b + 1)
            pe.matmul(f.h_ps[b][:], f.wh[e][:, rows], f.xh[:, cols], start=True, stop=False)
            pe.matmul(f.h_ps[b][:], f.wh[e][:, rows], f.xl[:, cols], start=False, stop=False)
            pe.matmul(f.h_ps[b][:], f.wl[e][:, rows], f.xh[:, cols], start=False, stop=True).then_inc(s.h_ps, 1)

    def weights(ep, i):
        e, t = 2 * ep + i // STEPS, i % STEPS
        sel = slice(e * P, (e + 1) * P) if isinstance(e, int) else bass.ds(e * P, P)
        pe.matmul(f.ps[i % 2][:], f.e_sel[:, sel], f.wT[:, t * T:(t + 1) * T],
                  start=True, stop=True).then_inc(s.wb_ps, 1)

    def output(ep, i, with_weights=True):
        e = i // STEPS
        g = 2 * STEPS * ep + i
        rows = [slice(HIDDEN + b * P, HIDDEN + (b + 1) * P) for b in range(HB)]
        wait(pe, s.part, g - 1)
        for b in range(HB):
            if b % 2 == 0:
                pe.wait_ge(s.gh, 2 * g + b // 2 + 1)
            pe.matmul(f.y_ps[i % 2][:], f.wh[e][:, rows[b]], f.gh[:, i % 2, b, :], start=(b == 0), stop=False)
            if b == 0 and with_weights:
                weights(ep, i)
            pe.matmul(f.y_ps[i % 2][:], f.wl[e][:, rows[b]], f.gh[:, i % 2, b, :], start=False, stop=False)
        for b in range(HB):
            if b % 2 == 0:
                pe.wait_ge(s.gl, 2 * g + b // 2 + 1)
            mm = pe.matmul(f.y_ps[i % 2][:], f.wh[e][:, rows[b]], f.gl[:, i % 2, b, :],
                           start=False, stop=(b == HB - 1))
        mm.then_inc(s.y_ps, 1)

    def turn_weights():
        pe.wait_ge(s.wlo, 1)
        for half in range(2):
            wT = f.ps[half][0:NPAR * EXPERTS, :].bitcast(BF16)
            for b in range(TB // 2):
                mm = pe.transpose(wT[:, b * P:(b + 1) * P], f.w3[:, half * TB // 2 + b, :], k.ident_b[:])
            mm.then_inc(s.wT_ps, 1)
        pe.wait_ge(s.wT, 2)

    def pair(ep, first=False, last=False):
        for i in range(2 * STEPS):
            if i + 1 < 2 * STEPS:
                hidden(ep, i + 1)
            elif not last:
                hidden(ep + 1, 0)
            elif before_last:
                before_last()
            output(ep, i, with_weights=not (first and i < 2))
            if first and i == 1:
                turn_weights()
                weights(ep, 0)
                weights(ep, 1)

    pe.wait_ge(ln_out, CHUNKS * (r + 1))
    hidden(0, 0)
    logits()
    pair(0, first=True)
    with pe.Fori(1, EXPERTS // 2 - 1) as ep:
        pair(ep)
    pair(EXPERTS // 2 - 1, last=True)


def ffn_scalar(act, s, k, f, xn, ln_out, r):
    for c in range(CHUNKS):
        cols = slice(c * T, (c + 1) * T)
        act.wait_ge(ln_out, CHUNKS * r + c + 1)
        act.activation(f.xh[:, cols], xn[:, cols], ACT.Copy).then_inc(s.xh, 1)

    def pair(ep, first=False):
        for i in range(2 * STEPS):
            g = 2 * STEPS * ep + i
            e = i // STEPS
            for b in range(HB):
                if b % 2 == 0:
                    wait(act, s.gl, 2 * (g - 2) + b // 2 + 1)
                act.wait_ge(s.h_ps, HB * g + b + 1)
                act.activation(f.g[:, i % 2, b, :], f.h_ps[b][:], ACT.Gelu_apprx_tanh,
                               bias=f.w[e][:, HIDDEN + HB * P + b:HIDDEN + HB * P + b + 1]).then_inc(s.gel, 1)
                if b % 2 == 1:
                    act.wait_ge(s.gel, HB * g + b + 1)
                    wait(act, s.y_ps, g - 1)
                    act.activation(f.gh[:, i % 2, b - 1:b + 1, :], f.g[:, i % 2, b - 1:b + 1, :],
                                   ACT.Copy).then_inc(s.gh, 1)
            if first and i == 0:
                act.wait_ge(s.shift, 1)
                act.activation(f.ex[:], f.sh[:], ACT.Exp).then_inc(s.ex, 1)

    pair(0, first=True)
    with act.Fori(1, EXPERTS // 2) as ep:
        pair(ep)


def ffn_pool(pool, s, f, xn, ln_out, r):
    for c in range(CHUNKS):
        cols = slice(c * T, (c + 1) * T)
        pool.wait_ge(s.xh, c + 1)
        pool.tensor_tensor(f.xl[:, cols], xn[:, cols], f.xh[:, cols].bitcast(F32), ALU.subtract).then_inc(s.xl, 1)

    def pair(ep):
        for i in range(2 * STEPS):
            g = 2 * STEPS * ep + i
            wait(pool, s.y_ps, g - 1)
            for half in range(2):
                b = slice(2 * half, 2 * half + 2)
                pool.wait_ge(s.gh, 2 * g + half + 1)
                pool.tensor_tensor(f.gl[:, i % 2, b, :], f.g[:, i % 2, b, :], f.gh[:, i % 2, b, :].bitcast(F32),
                                   ALU.subtract).then_inc(s.gl, 1)

    pair(0)
    with pool.Fori(1, EXPERTS // 2) as ep:
        pair(ep)


def split_weights(dve, s, f, ep, i):
    n = HIDDEN + HB * P
    e = 2 * ep + i
    dve.wait_ge((s.w0, s.w1)[i], 16 * ep + 16)
    wait(dve, s.y_ps, STEPS * (e - 1))
    dve.tensor_copy(f.wh[i][:], f.w[i][:, 0:n]).then_inc(s.wh, 1)
    dve.wait_ge(s.wh, e + 1)
    dve.tensor_tensor(f.wl[i][:], f.w[i][:, 0:n], f.wh[i][:].bitcast(F32), ALU.subtract).then_inc(s.wl, 1)


def ffn_vector(dve, s, k, f, x, before_last=None):
    lg = f.ps[0][:, 0:TB * EXPERTS].rearrange("p (b e) -> p b e", e=EXPERTS)
    rank = k.rank[:].rearrange("p (b e) -> p b e", e=EXPERTS)
    done = 0

    def chained(instruction):
        nonlocal done
        done += 1
        instruction.then_inc(s.route, 1)
        dve.wait_ge(s.route, done)

    dve.wait_ge(s.logits, 1)
    chained(dve.tensor_reduce(f.c[0][:], lg, AX.X, ALU.max))
    dve.tensor_tensor(rows3(f.sh), lg, per_block(f.c[0]), ALU.subtract).then_inc(s.shift, 1)
    dve.wait_ge(s.ex, 1)
    chained(dve.tensor_reduce(f.c[1][:], rows3(f.ex), AX.X, ALU.add))
    chained(dve.reciprocal(f.c[2][:], f.c[1][:]))
    chained(dve.tensor_tensor(rows3(f.p), rows3(f.ex), per_block(f.c[2]), ALU.mult))

    def largest(p, cm, cc, eq, sel):
        chained(dve.tensor_reduce(cm[:], rows3(p), AX.X, ALU.max))
        chained(dve.tensor_tensor(rows3(eq), rows3(p), per_block(cm), ALU.is_equal))
        chained(dve.tensor_tensor(rows3(eq), rows3(eq), rank, ALU.mult))
        chained(dve.tensor_reduce(cc[:], rows3(eq), AX.X, ALU.max))
        chained(dve.tensor_tensor(rows3(sel), rows3(eq), per_block(cc), ALU.is_equal))

    largest(f.p, f.c[3], f.c[4], f.eq[0], f.sel[0])
    chained(dve.scalar_tensor_tensor(out=f.p2[:], in0=f.sel[0][:], scalar=-2.0, in1=f.p[:],
                                     op0=ALU.mult, op1=ALU.add))
    largest(f.p2, f.c[5], f.c[6], f.eq[1], f.sel[1])
    chained(dve.tensor_tensor(f.both[:], f.sel[0][:], f.sel[1][:], ALU.add))
    chained(dve.tensor_tensor(f.wt[:], f.both[:], f.p[:], ALU.mult))
    chained(dve.tensor_copy(f.w3[:, :, 0:EXPERTS], rows3(f.wt)))
    chained(dve.tensor_tensor(rows3(f.wr1), rows3(f.wt), f.w3[:, :, 0:EXPERTS], ALU.subtract))
    chained(dve.tensor_copy(f.w3[:, :, EXPERTS:2 * EXPERTS], rows3(f.wr1)))
    dve.tensor_tensor(f.w3[:, :, 2 * EXPERTS:], rows3(f.wr1), f.w3[:, :, EXPERTS:2 * EXPERTS],
                      ALU.subtract).then_inc(s.wlo, 1)
    for half in range(2):
        dve.wait_ge(s.wT_ps, half + 1)
        dve.tensor_copy(f.wT[:, half * SEQ:(half + 1) * SEQ],
                        f.ps[half][0:NPAR * EXPERTS, :].bitcast(BF16)).then_inc(s.wT, 1)

    def pair(ep, last=False):
        for i in range(2 * STEPS):
            t = i % STEPS
            g = 2 * STEPS * ep + i
            if last and i == 2 * STEPS - 1 and before_last:
                before_last()
            dve.wait_ge(s.wb_ps, g + 1)
            dve.tensor_copy(f.wb[:, i % 2, :], f.ps[i % 2][:]).then_inc(s.wb, 1)
            dve.wait_ge(s.wb, g + 1)
            dve.wait_ge(s.y_ps, g + 1)
            wait(dve, s.acc, g - 1)
            dve.scalar_tensor_tensor(out=f.part[:, i % 2, :], in0=f.y_ps[i % 2][:],
                                     scalar=f.w[i // STEPS][:, EW - 1:EW], in1=f.wb[:, i % 2, :],
                                     op0=ALU.add, op1=ALU.mult).then_inc(s.part, 1)
            dve.wait_ge(s.part, g + 1)
            xc = x[:, t * T:(t + 1) * T]
            dve.tensor_tensor(xc, xc, f.part[:, i % 2, :], ALU.add).then_inc(s.acc, 1)
            if i == 1:
                split_weights(dve, s, f, ep, 1)
            if i == 2 * STEPS - 3 and not last:
                split_weights(dve, s, f, ep + 1, 0)

    pair(0)
    with dve.Fori(1, EXPERTS // 2 - 1) as ep:
        pair(ep)
    pair(EXPERTS // 2 - 1, last=True)


UNITS = 2 * TB
INV2PI = float(np.float32(1 / (2 * np.pi)))
MAGIC = float(1.5 * 2 ** 23)
PI2_A = 6.28125
PI2_B = float(np.float32(2 * np.pi - PI2_A))
PI_BELOW = 3.1415925
F_SLOTS = 4
R_SLOTS = 3
T1_SLOTS = 2


def attention_semaphores(sem, phase):
    s = Group()
    s.w = sem(phase + "_w")
    s.qk_ps = sem(phase + "_qk_ps")
    s.qk = sem(phase + "_qk")
    s.sq = sem(phase + "_sq")
    s.nrm_ps = sem(phase + "_nrm_ps")
    s.ex = sem(phase + "_ex")
    s.sc = sem(phase + "_sc")
    s.ones = sem(phase + "_ones")
    s.v_ps = sem(phase + "_v_ps")
    s.va = sem(phase + "_va")
    s.f_ps = sem(phase + "_f_ps")
    s.t1 = sem(phase + "_t1")
    s.kk = sem(phase + "_kk")
    s.r1 = sem(phase + "_r1")
    s.r2 = sem(phase + "_r2")
    s.r = sem(phase + "_r")
    s.sn = sem(phase + "_sn")
    s.ab = sem(phase + "_ab")
    s.cs = sem(phase + "_cs")
    s.kv_ps = sem(phase + "_kv_ps")
    s.kvm = sem(phase + "_kvm")
    s.o_ps = sem(phase + "_o_ps")
    s.on = sem(phase + "_on")
    s.oz = sem(phase + "_oz")
    s.orz = sem(phase + "_orz")
    s.od = sem(phase + "_od")
    s.oT_ps = sem(phase + "_oT_ps")
    s.oT = sem(phase + "_oT")
    s.fin_ps = sem(phase + "_fin_ps")
    s.fin = sem(phase + "_fin")
    return s


def att_loads(sp, s, k, a, d):
    sp.dma_start(a.w[:], d.aw).then_inc(s.w, 16)


def unit_of(u):
    if u < TB:
        return True, u // (TB // BATCH), u // 4, u
    return False, (u - TB) // (UNITS // 4), (u - TB) // GROUPS, (u - TB) % GROUPS


def finished_chunk(u):
    if TB <= u < UNITS and unit_of(u)[3] == GROUPS - 1:
        return unit_of(u)[2]
    return None


def att_tensor(pe, s, k, a, xn, ln_out, r, before_last):
    pe.wait_ge(s.w, 16)
    for c in range(CHUNKS):
        pe.wait_ge(ln_out, CHUNKS * r + c + 1)
        for i in (1, 0):
            wait(pe, s.qk, 2 * (c - 1) + 2 - i)
            pe.matmul(a.ps[i][:], a.w[:, i * P:(i + 1) * P], xn[:, c * T:(c + 1) * T],
                      start=True, stop=True).then_inc(s.qk_ps, 1)

    def angles(u):
        key, b, c, i = unit_of(u)
        wait(pe, s.r1, u - F_SLOTS + 1)
        pe.wait_ge(s.qk, 2 * (i // 4 if key else c) + (1 if key else 2))
        if key:
            pe.matmul(a.f_ps[u % F_SLOTS][:], a.qk[:, 1, i * P:(i + 1) * P], a.w[:, A_RF:A_RF + HEADS * M],
                      start=True, stop=True).then_inc(s.f_ps, 1)
        else:
            pe.matmul(a.f_ps[u % F_SLOTS][:], a.w[:, A_RF + i * P:A_RF + (i + 1) * P], a.qk[:, 0, c * T:(c + 1) * T],
                      start=True, stop=True).then_inc(s.f_ps, 1)

    def norms():
        pe.wait_ge(s.sq, 2 * CHUNKS)
        for i in range(2):
            for b in range(TB):
                o = (i * TB + b) * HEADS
                mm = pe.matmul(a.kv_ps[0][:, o:o + HEADS], a.sq[:, i, b * P:(b + 1) * P], a.w[:, A_HS:A_HS + HEADS],
                               start=True, stop=True)
        mm.then_inc(s.nrm_ps, 1)

    def values(c):
        if c < 2:
            pe.wait_ge(s.qk, 2 * CHUNKS)
        wait(pe, s.va, c - 1)
        for b in range(4):
            mm = pe.matmul(a.ps[c % 2][:, b * P:(b + 1) * P], xn[:, c * T + b * P:c * T + (b + 1) * P],
                           a.w[:, 2 * P:3 * P], start=True, stop=True)
        mm.then_inc(s.v_ps, 1)

    def keys(u):
        _, b, c, i = unit_of(u)
        per = TB // BATCH
        if i == 0:
            pe.wait_ge(s.ones, 1)
        if i % 4 == 0:
            pe.wait_ge(s.va, c + 1)
        for j, (trig, done) in enumerate(((a.sn, s.sn), (a.cs, s.cs))):
            pe.wait_ge(done, u + 1)
            for g in range(GROUPS):
                o = (j * GROUPS + g) * HG * VW
                mm = pe.matmul(a.kv_ps[b][:, o:o + HG * VW], trig[:, u % R_SLOTS, g * P:(g + 1) * P],
                               a.va[:, i, g * HG * VW:(g + 1) * HG * VW],
                               start=(i % per == 0 and j == 0 and g == 0), stop=(i % per == per - 1),
                               skip_group_check=True)
        mm.then_inc(s.kv_ps, 1)

    def queries(u):
        _, b, c, g = unit_of(u)
        pe.wait_ge(s.kvm, BATCH)
        pe.wait_ge(s.sn, u + 1)
        pe.wait_ge(s.cs, u + 1)
        if g == 0:
            wait(pe, s.on, 2 * c)
        for t in range(4):
            o = (t % 2) * HEADS * VW + g * HG * VW
            for j, trig in enumerate((a.sn, a.cs)):
                mm = pe.matmul(a.o_ps[t // 2][:, o:o + HG * VW], trig[:, u % R_SLOTS, t * P:(t + 1) * P],
                               a.kvm[:, b, j * GROUPS + g, :], start=(j == 0), stop=(j == 1),
                               skip_group_check=True)
        mm.then_inc(s.o_ps, 1)

    def turn(c):
        pe.wait_ge(s.od, c + 1)
        wait(pe, s.oT, c)
        for t in range(4):
            mm = pe.transpose(a.ps[0][:, t * P:(t + 1) * P], a.od[:, t, :], k.ident[:])
        mm.then_inc(s.oT_ps, 1)

    def project(c):
        pe.wait_ge(s.oT, c + 1)
        wait(pe, s.fin, c)
        pe.matmul(a.ps[1][:], a.w[:, 3 * P:4 * P], a.oT[:], start=True, stop=True).then_inc(s.fin_ps, 1)

    for u in range(F_SLOTS):
        angles(u)
    norms()
    values(0)
    values(1)
    for u in range(UNITS + 3):
        if u + F_SLOTS < UNITS:
            angles(u + F_SLOTS)
        if u < UNITS:
            (keys if u < TB else queries)(u)
        if u in (0, 4):
            values(2 + u // 4)
        c = finished_chunk(u - 1)
        if c is not None:
            if c == CHUNKS - 1:
                before_last()
            turn(c)
        c = finished_chunk(u - 3)
        if c is not None:
            project(c)


def att_scalar(act, s, k, a):
    for c in range(CHUNKS):
        for n, i in enumerate((1, 0)):
            act.wait_ge(s.qk_ps, 2 * c + n + 1)
            act.activation(a.qk[:, i, c * T:(c + 1) * T], a.ps[i][:], ACT.Copy).then_inc(s.qk, 1)

    def multiples(u):
        act.wait_ge(s.f_ps, u + 1)
        wait(act, s.r2, u - T1_SLOTS + 1)
        act.activation(a.t1[:, u % T1_SLOTS, :], a.f_ps[u % F_SLOTS][:], ACT.Identity,
                       bias=k.const[:, C_MAGIC:C_MAGIC + 1], scale=INV2PI).then_inc(s.t1, 1)

    multiples(0)
    multiples(1)
    def sines(u):
        act.wait_ge(s.r, u + 1)
        if u >= R_SLOTS:
            v = u - R_SLOTS
            act.wait_ge(s.kv_ps if v < TB else s.o_ps, v % TB + 1)
        act.activation(a.sn[:, u % R_SLOTS, :], a.r[:, u % R_SLOTS, :], ACT.Sin).then_inc(s.sn, 1)
        wait(act, s.cs, u)
        act.activation(a.ab[:], a.r[:, u % R_SLOTS, :], ACT.Abs).then_inc(s.ab, 1)
        act.wait_ge(s.ab, u + 1)
        act.activation(a.cs[:, u % R_SLOTS, :], a.ab[:], ACT.Sin, bias=k.const[:, C_HPI:C_HPI + 1],
                       scale=-1.0).then_inc(s.cs, 1)

    for u in range(UNITS + 2):
        if u < UNITS:
            sines(u)
        if u == R_SLOTS - 1:
            act.wait_ge(s.nrm_ps, 1)
            act.activation(a.ex[:], a.kv_ps[0][:], ACT.Exp, scale=-0.5).then_inc(s.ex, 1)
        if u + 2 < UNITS:
            multiples(u + 2)
        c = finished_chunk(u - 2)
        if c is not None:
            act.wait_ge(s.oT_ps, c + 1)
            wait(act, s.fin_ps, c)
            act.activation(a.oT[:], a.ps[0][:], ACT.Copy).then_inc(s.oT, 1)


def att_pool(pool, s, a):
    for c in range(CHUNKS):
        for n, i in enumerate((1, 0)):
            pool.wait_ge(s.qk, 2 * c + n + 1)
            v = a.qk[:, i, c * T:(c + 1) * T]
            pool.tensor_tensor(a.sq[:, i, c * T:(c + 1) * T], v, v, ALU.mult).then_inc(s.sq, 1)


def att_vector(dve, s, k, a, x, before_last):
    def reduce(u):
        m = a.t1[:, u % T1_SLOTS, :]
        r = a.r[:, u % R_SLOTS, :]
        dve.wait_ge(s.t1, u + 1)
        dve.tensor_scalar(m, m, MAGIC, None, ALU.subtract).then_inc(s.kk, 1)
        dve.wait_ge(s.kk, u + 1)
        wait(dve, s.ab, u - R_SLOTS + 1)
        dve.scalar_tensor_tensor(out=r, in0=m, scalar=-PI2_A, in1=a.f_ps[u % F_SLOTS][:],
                                 op0=ALU.mult, op1=ALU.add).then_inc(s.r1, 1)
        dve.wait_ge(s.r1, u + 1)
        dve.scalar_tensor_tensor(out=r, in0=m, scalar=-PI2_B, in1=r,
                                 op0=ALU.mult, op1=ALU.add).then_inc(s.r2, 1)
        dve.wait_ge(s.r2, u + 1)
        dve.tensor_scalar(r, r, PI_BELOW, -PI_BELOW, ALU.min, ALU.max).then_inc(s.r, 1)

    ks = a.sc[:, TB * HEADS:].rearrange("p (b h o) -> p b h o", h=HEADS, o=1)
    va = a.va[:].rearrange("p b (h v) -> p b h v", v=VW)

    def scales():
        dve.wait_ge(s.ex, 1)
        dve.tensor_scalar(a.sc[:], a.ex[:], float(M) ** -0.5, None, ALU.mult).then_inc(s.sc, 1)
        dve.wait_ge(s.sc, 1)
        dve.tensor_copy(va[:, :, :, DH:VW], ks).then_inc(s.ones, 1)

    def values(c):
        dve.wait_ge(s.v_ps, c + 1)
        i = dve.tensor_tensor(va[:, 4 * c:4 * c + 4, :, 0:DH],
                              a.ps[c % 2][:].rearrange("p (b h v) -> p b h v", b=4, v=DH),
                              ks[:, 4 * c:4 * c + 4, :, :].broadcast_to([P, 4, HEADS, DH]), ALU.mult)
        i.then_inc(s.va, 1)

    def mask_kv(b):
        dve.wait_ge(s.kv_ps, (b + 1) * (TB // BATCH))
        w = HG * VW
        dve.tensor_tensor(a.kvm[:, b], a.kv_ps[b][:, 0:2 * GROUPS * w].rearrange("p (g v) -> p g v", v=w),
                          a.w[:, A_MASK:A_MASK + w].rearrange("p (o v) -> p o v", o=1).broadcast_to([P, 2 * GROUPS, w]),
                          ALU.mult).then_inc(s.kvm, 1)

    def divide(c):
        dve.wait_ge(s.o_ps, GROUPS * (c + 1))
        qs = a.sc[:, 4 * c * HEADS:4 * (c + 1) * HEADS].rearrange("p (h o) -> p h o", o=1)
        on = a.on[:].rearrange("p (h v) -> p h v", v=VW)
        n = 2 * HEADS
        wait(dve, s.od, c)
        for t in range(2):
            dve.tensor_tensor(on[:, t * n:(t + 1) * n, :],
                              a.o_ps[t][:, 0:n * VW].rearrange("p (h v) -> p h v", v=VW),
                              qs[:, t * n:(t + 1) * n, :].broadcast_to([P, n, VW]), ALU.mult).then_inc(s.on, 1)
        dve.wait_ge(s.on, 2 * c + 2)
        dve.tensor_scalar(a.z[:].rearrange("p (h o) -> p h o", o=1), on[:, :, DH:VW], 1e-6, None,
                          ALU.max).then_inc(s.oz, 1)
        dve.wait_ge(s.oz, c + 1)
        dve.reciprocal(a.rz[:], a.z[:]).then_inc(s.orz, 1)
        dve.wait_ge(s.orz, c + 1)
        wait(dve, s.oT_ps, c)
        dve.tensor_tensor(a.od[:].rearrange("p t (h v) -> p (t h) v", v=DH), on[:, :, 0:DH],
                          a.rz[:].rearrange("p (h o) -> p h o", o=1).broadcast_to([P, 4 * HEADS, DH]),
                          ALU.mult).then_inc(s.od, 1)

    def residual(c):
        dve.wait_ge(s.fin_ps, c + 1)
        xc = x[:, c * T:(c + 1) * T]
        dve.tensor_tensor(xc, xc, a.ps[1][:], ALU.add).then_inc(s.fin, 1)

    for u in range(R_SLOTS + 1):
        reduce(u)
    scales()
    values(0)
    for u in range(UNITS + 4):
        if R_SLOTS < u + 1 < UNITS:
            reduce(u + 1)
        if u in (0, 1, 5):
            values(1 + (u + 3) // 4)
        if u in (TB // BATCH, TB):
            mask_kv(u // (TB // BATCH) - 1)
        c = finished_chunk(u - 1)
        if c is not None:
            divide(c)
            if c == CHUNKS - 1:
                before_last()
        c = finished_chunk(u - 4)
        if c is not None:
            residual(c)


def state_space_semaphores(sem, phase):
    s = Group()
    s.wp = sem(phase + "_wp")
    s.wa = sem(phase + "_wa")
    s.wo = sem(phase + "_wo")
    s.weff = sem(phase + "_weff")
    s.x = sem(phase + "_x")
    s.sq = sem(phase + "_sq")
    s.ms = sem(phase + "_ms")
    s.ln = sem(phase + "_ln")
    s.rstd = sem(phase + "_rstd")
    s.pad = sem(phase + "_pad")
    s.hn = sem(phase + "_hn")
    s.xc_ps = sem(phase + "_xc_ps")
    s.xc = sem(phase + "_xc")
    s.z_ps = sem(phase + "_z_ps")
    s.z = sem(phase + "_z")
    s.bcp_ps = sem(phase + "_bcp_ps")
    s.dtr_ps = sem(phase + "_dtr_ps")
    s.hi = sem(phase + "_hi")
    s.dtr = sem(phase + "_dtr")
    s.r1 = sem(phase + "_r1")
    s.mid = sem(phase + "_mid")
    s.bc = sem(phase + "_bc")
    s.d_ps = sem(phase + "_d_ps")
    s.xb = sem(phase + "_xb")
    s.ab = sem(phase + "_ab")
    s.ey = sem(phase + "_ey")
    s.ll = sem(phase + "_ll")
    s.dd = sem(phase + "_dd")
    s.t = sem(phase + "_t")
    s.s1 = sem(phase + "_s1")
    s.delta = sem(phase + "_delta")
    s.u = sem(phase + "_u")
    s.a1 = sem(phase + "_a1")
    s.aneg = sem(phase + "_aneg")
    s.bc_ps = sem(phase + "_bc_ps")
    s.bcs = sem(phase + "_bcs")
    s.a = sem(phase + "_a")
    s.bx = sem(phase + "_bx")
    s.h = sem(phase + "_h")
    s.carry = sem(phase + "_carry")
    s.pd = sem(phase + "_pd")
    s.pp = sem(phase + "_pp")
    s.y_acc = sem(phase + "_y_acc")
    s.yd = sem(phase + "_yd")
    s.gate = sem(phase + "_gate")
    s.out_ps = sem(phase + "_out_ps")
    return s


def build(nc, d):
    with ExitStack() as keep:
        def sb(name, shape, dt=F32, where=keep):
            return where.enter_context(nc.sbuf_tensor(name, shape, dt))

        def psum(name, shape, dt=F32, where=keep):
            return where.enter_context(nc.psum_tensor(name, shape, dt))

        k = Group()
        x0 = sb("x0", [P, TOK])
        xn = sb("xn", [P, TOK])
        k.mean_w = sb("mean_w", [P, P])
        k.const = sb("const", [P, NCONST])
        k.ident = sb("ident", [P, P])
        k.ident_b = sb("ident_b", [P, P], BF16)
        k.rank = sb("rank", [P, TOK // P * EXPERTS])
        e_sel = sb("e_sel", [NPAR * EXPERTS, EXPERTS * P], BF16)
        ln = Group()
        scope = ExitStack()
        sb("ln_past", [P, PHASE_BYTES], mybir.dt.uint8, scope)
        ln.s = sb("ln_s", [P, TOK], F32, scope)
        scope.close()
        bank = [psum(f"bank{i}", [P, T]) for i in range(2)]
        ln.ps = [psum(f"ln_ps{c}", [P, T], F32, scope) for c in range(CHUNKS)]
        scope.close()

        def sem(name):
            return keep.enter_context(nc.semaphore(name))

        io = Group()
        io.x, io.consts, io.stored, io.merged, io.wr = (sem("io_" + n) for n in ("x", "consts", "stored", "merged", "wr"))

        m = Group()
        scope = ExitStack()

        def mb(name, shape, dt=F32):
            return sb("m_" + name, shape, dt, scope)
        bc_sel = mb("bc_sel", [NPAR * 2 * STATES, 2 * STATES, P], BF16)
        y_ps = psum("m_y_ps", [P, HALVES, T], F32, scope)
        bc_ps = [psum(f"m_bc_ps{i}", [P, 2, T], F32, scope) for i in range(2)]
        m.wp = mb("wp", [P, PW])
        m.wdt = mb("wdt", [RANK, INNER])
        m.cw = mb("cw", [P, TAPS * INNER])
        m.wo = mb("wo", [P, OW])
        m.alog = mb("alog", [P, HALVES * STATES])
        m.weff = mb("weff", [P, TAPS, INNER])
        m.a1 = mb("a1", [P, HALVES * STATES])
        m.aneg = mb("aneg", [P, HALVES * STATES])
        m.sq = mb("sq", [P, T])
        m.rstd = mb("rstd", [P, T])
        m.lnv = m.rstd
        m.hn = mb("hn", [P, TAPS - 1 + SEQ])
        m.xc = mb("xc", [P, 2, HALVES, T])
        m.z = mb("z", [P, 2, HALVES, T])
        m.hi = mb("hi", [NPAR * 2 * STATES, T], BF16)
        m.mid = mb("mid", [NPAR * 2 * STATES, T], BF16)
        m.r1 = mb("r1", [NPAR * 2 * STATES, T])
        m.bc = mb("bc", [NPAR * 2 * STATES, 2, T], BF16)
        m.dtr = mb("dtr", [RANK, T])
        m.xb = mb("xb", [P, HALVES, T])
        m.ab = mb("ab", [P, HALVES, T])
        m.ey = mb("ey", [P, HALVES, T])
        m.ll = m.ab
        m.dd = mb("dd", [P, HALVES, T])
        m.delta = mb("delta", [P, 2, HALVES, T])
        m.u = mb("u", [P, 2, HALVES, T])
        m.a = mb("a", [P, RING, HALVES, T])
        m.bcs = mb("bcs", [P, BC_RING, 2, T])
        m.bx = mb("bx", [P, RING, HALVES, T])
        m.h = mb("h", [P, RING, HALVES, T])
        m.p = mb("p", [P, RING, HALVES, T])
        m.carry = mb("carry", [P, HALVES, STATES])
        m.yd = mb("yd", [P, HALVES, T])
        m.yg = m.yd
        scope.close()
        s = state_space_semaphores(sem, "m")

        f = Group()
        scope = ExitStack()

        def fb(name, shape, dt=F32):
            return sb("f_" + name, shape, dt, scope)
        f.w = [fb(f"w{i}", [P, EW]) for i in range(2)]
        f.wr = fb("wr", [P, EXPERTS])
        f.wh, f.wl = ([fb(f"{n}{i}", [P, HIDDEN + HB * P], F32R) for i in range(2)] for n in ("wh", "wl"))
        f.g = fb("g", [P, 2, HB, T])
        f.gh = fb("gh", [P, 2, HB, T], F32R)
        f.gl = fb("gl", [P, 2, HB, T], F32R)
        f.xh = fb("xh", [P, TOK], F32R)
        f.xl = fb("xl", [P, TOK], F32R)
        f.wT = fb("wT", [NPAR * EXPERTS, TOK], BF16)
        f.part = fb("part", [P, 2, T])
        f.wb = fb("wb", [P, 2, T])
        f.c = [fb(f"c{i}", [P, TB]) for i in range(7)]
        f.sh, f.ex, f.p, f.p2, f.both, f.wt, f.wr1 = (
            fb(n, [P, TB * EXPERTS]) for n in ("sh", "ex", "p", "p2", "both", "wt", "wr1"))
        f.eq = [fb(f"eq{i}", [P, TB * EXPERTS]) for i in range(2)]
        f.sel = [fb(f"sel{i}", [P, TB * EXPERTS]) for i in range(2)]
        f.w3 = fb("w3", [P, TB, NPAR * EXPERTS], BF16)
        f.e_sel = e_sel
        f.h_ps = [psum(f"f_h_ps{i}", [P, T], F32, scope) for i in range(HB)]
        f.y_ps = [psum(f"f_y_ps{i}", [P, T], F32, scope) for i in range(2)]
        f.ps = bank
        scope.close()

        a = Group()
        scope = ExitStack()

        def ab(name, shape, dt=F32):
            return sb("a_" + name, shape, dt, scope)
        a.w = ab("w", [P, AW])
        a.qk = ab("qk", [P, 2, TOK])
        a.sq = ab("sq", [P, 2, TOK])
        a.ex = ab("ex", [P, 2 * TB * HEADS])
        a.sc = ab("sc", [P, 2 * TB * HEADS])
        a.va = ab("va", [P, TB, HEADS * VW])
        a.t1 = ab("t1", [P, T1_SLOTS, T])
        a.r = ab("r", [P, R_SLOTS, T])
        a.ab = ab("ab", [P, T])
        a.sn = ab("sn", [P, R_SLOTS, T])
        a.cs = ab("cs", [P, R_SLOTS, T])
        a.kvm = ab("kvm", [P, BATCH, 2 * GROUPS, HG * VW])
        a.on = ab("on", [P, 4 * HEADS * VW])
        a.z = ab("z", [P, 4 * HEADS])
        a.rz = ab("rz", [P, 4 * HEADS])
        a.od = ab("od", [P, 4, P])
        a.oT = ab("oT", [P, T])
        a.f_ps = [psum(f"a_f_ps{i}", [P, T], F32, scope) for i in range(F_SLOTS)]
        a.kv_ps = [psum(f"a_kv_ps{i}", [P, T], F32, scope) for i in range(2)]
        a.o_ps = a.kv_ps
        a.ps = bank
        scope.close()

        l = norm_semaphores(sem, "l")
        e1, e2 = (expert_semaphores(sem, n) for n in ("e1", "e2"))
        at = attention_semaphores(sem, "at")

        block = keep.enter_context(nc.Block())
        k.x = lambda c: x0[:, c * T:(c + 1) * T]

        def xcols(j, c):
            off = (j % BATCH) * SEQ + c * T
            return bass.ds(off, T) if not isinstance(off, int) else slice(off, off + T)

        def product_wait(eng, kk, n):
            if n < 0:
                kk, n = kk - 1, n + STATES
            if isinstance(kk, int) and kk < 0:
                return
            if n in POOL_N:
                eng.wait_ge(s.pp, len(POOL_N) * kk + POOL_N.index(n) + 1)
            else:
                eng.wait_ge(s.pd, len(DVE_N) * kk + DVE_N.index(n) + 1)

        def ahead(j, c, n):
            if n < STATES:
                return j, c, n
            return (j, 1, n - STATES) if c == 0 else (j + 1, 0, n - STATES)

        def back(j, c, n, lag):
            kk = 2 * j + c
            if n >= lag:
                return c, n - lag, kk
            if isinstance(kk, int) and kk == 0:
                return None
            return 1 - c, n - lag + STATES, kk - 1

        @block.sync
        def _(sp):
            for c in range(CHUNKS):
                sp.dma_start(x0[:, c * T:(c + 1) * T], d.x[:, c * T:(c + 1) * T]).then_inc(io.x, 16)
            sp.dma_start(k.mean_w[:], d.mean_w).then_inc(io.consts, 16)
            sp.dma_start(k.const[:], d.const).then_inc(io.consts, 16)
            sp.dma_start(k.ident[:], d.ident).then_inc(io.consts, 16)
            sp.dma_start(bc_sel[:].bitcast(mybir.dt.uint16), d.bc_sel).then_inc(io.consts, 16)
            sp.dma_start(k.ident_b[:].bitcast(mybir.dt.uint16), d.ident_b).then_inc(io.consts, 16)
            sp.dma_start(k.rank[:], d.rank).then_inc(io.consts, 16)
            sp.dma_start(e_sel[:].bitcast(mybir.dt.uint16), d.e_sel).then_inc(io.consts, 16)

            def load_p(l):
                sp.dma_start(m.wp[:], d.wp[l]).then_inc(s.wp, 16)
                sp.dma_start(m.wdt[:], d.wdt[l]).then_inc(s.wp, 16)
                sp.dma_start(m.cw[:], d.cw[l].broadcast_to([P, TAPS * INNER])).then_inc(s.wp, 16)

            def load_a(l):
                sp.dma_start(m.alog[:], d.alog[l]).then_inc(s.wa, 16)

            def load_o(l):
                sp.dma_start(m.wo[:], d.wo[l]).then_inc(s.wo, 16)

            def layer(l):
                q = 2 * l
                wait(sp, s.xb, 4 * q)
                load_p(l)
                wait(sp, s.aneg, q)
                load_a(l)
                wait(sp, s.x, 2 * q + (CHUNKS if not (isinstance(q, int) and q == 0) else 0))
                load_o(l)
                sp.wait_ge(s.wp, 48 * q + 48)
                sp.sem_inc(s.wp, 48)
                sp.wait_ge(s.wa, 16 * q + 16)
                sp.sem_inc(s.wa, 16)
                sp.wait_ge(s.wo, 16 * q + 16)
                sp.sem_inc(s.wo, 16)

            layer(0)
            with sp.Fori(1, LAYERS) as i:
                layer(i)
            sp.wait_ge(io.merged, CHUNKS)
            sp.dma_start(f.wr[:], d.wr).then_inc(io.wr, 16)
            ffn_loads(sp, e1, k, f, d)
            sp.wait_ge(e1.acc, EXPERTS * STEPS)
            att_loads(sp, at, k, a, d)
            sp.wait_ge(at.fin, CHUNKS)
            sp.dma_start(f.wr[:], d.wr).then_inc(io.wr, 16)
            ffn_loads(sp, e2, k, f, d)
            for c in range(CHUNKS):
                sp.wait_ge(e2.acc, (EXPERTS - 1) * STEPS + c + 1)
                sp.dma_start(d.out[:, c * T:(c + 1) * T], x0[:, c * T:(c + 1) * T]).then_inc(io.stored, 16)
            sp.wait_ge(io.stored, 16 * CHUNKS)

        @block.tensor
        def _(pe):
            pe.wait_ge(io.consts, 112)
            pe.wait_ge(io.x, 16 * CHUNKS)
            for c in range(CHUNKS):
                ln_mean(pe, l, k, ln, c)
            for c in range(CHUNKS):
                ln_variance(pe, l, k, ln, 0, c)

            def project(j, c, piece, h=None, part=None):
                kk = 2 * j + c
                if piece == "ms":
                    pe.wait_ge(s.sq, kk + 1)
                    wait(pe, s.xb, 2 * kk)
                    pe.matmul(bank[1][:], k.mean_w[:], m.sq[:], start=True, stop=True).then_inc(s.ms, 1)
                elif piece == "conv":
                    pe.wait_ge(s.hn, kk + 1)
                    pe.wait_ge(s.weff, j + 1)
                    pe.wait_ge(s.pad, 1)
                    pe.wait_ge(s.ln, kk + 1)
                    for tap in range(part * TAPS // 2, (part + 1) * TAPS // 2):
                        mm = pe.matmul(bank[h][:], m.weff[:, tap, h * P:(h + 1) * P],
                                       m.hn[:, c * T + tap:c * T + tap + T],
                                       start=(tap == 0), stop=(tap == TAPS - 1))
                    if part == 1:
                        mm.then_inc(s.xc_ps, 1)
                elif piece == "z":
                    for h in (1, 0):
                        pe.wait_ge(s.xc, 2 * kk + 2 - h)
                        pe.matmul(bank[h][:], m.wp[:, INNER + h * P:INNER + (h + 1) * P],
                                  m.hn[:, c * T + TAPS - 1:c * T + TAPS - 1 + T],
                                  start=True, stop=True).then_inc(s.z_ps, 1)
                elif piece == "bc":
                    pe.wait_ge(s.z, 2 * kk + 2)
                    for h in range(HALVES):
                        o = O_WX + h * WX
                        mm = pe.matmul(bank[1][0:NPAR * 2 * STATES, :], m.wp[:, o:o + NPAR * 2 * STATES],
                                       m.xc[:, c, h, :], start=(h == 0), stop=(h == HALVES - 1))
                    mm.then_inc(s.bcp_ps, 1)
                elif piece == "rank":
                    for h in range(HALVES):
                        o = O_WX + h * WX + NPAR * 2 * STATES
                        mm = pe.matmul(bank[0][0:RANK, :], m.wp[:, o:o + RANK], m.xc[:, c, h, :],
                                       start=(h == 0), stop=(h == HALVES - 1))
                    mm.then_inc(s.dtr_ps, 1)
                elif piece == "dt":
                    pe.wait_ge(s.dtr, kk + 1)
                    pe.wait_ge(s.r1, kk + 1)
                    for h in range(HALVES):
                        pe.matmul(bank[h][:], m.wdt[:, h * P:(h + 1) * P], m.dtr[:],
                                  start=True, stop=True).then_inc(s.d_ps, 1)

            def out_proj(j, c):
                kk = 2 * j + c
                pe.wait_ge(s.gate, kk + 1)
                pe.wait_ge(s.wo, 16 * j + 16)
                for h in range(HALVES):
                    mm = pe.matmul(bank[0][:], m.wo[:, h * P:(h + 1) * P], m.yg[:, h, :],
                                   start=(h == 0), stop=(h == HALVES - 1))
                mm.then_inc(s.out_ps, 1)

            def accumulate(b):
                c, n, kk = b
                if n == 0:
                    wait(pe, s.yd, 2 * kk)
                product_wait(pe, kk, n)
                for h in range(HALVES):
                    mm = pe.matmul(y_ps[:, h, :], k.ident[:], m.p[:, n % RING, h, :],
                                   start=(n == 0), stop=(n == STATES - 1))
                mm.then_inc(s.y_acc, 1)

            def broadcast(j, c, n):
                j, c, n = ahead(j, c, n)
                kk = 2 * j + c
                if n == 0:
                    pe.wait_ge(s.bc, kk + 1)
                wait(pe, s.bcs, STATES * kk + n - 1)
                for w in range(2):
                    mm = pe.matmul(bc_ps[n % 2][:, w, :], bc_sel[:, w * STATES + n, :], m.bc[:, c, :],
                                   start=True, stop=True)
                mm.then_inc(s.bc_ps, 1)

            def pair(j, last):
                for c in range(2):
                    nxt = (j, 1) if c == 0 else (j + 1, 0)
                    more = c == 0 or not last
                    for n in range(STATES):
                        if n + BC_AHEAD < STATES or more:
                            broadcast(j, c, n + BC_AHEAD)
                        b = back(j, c, n, 3)
                        if b:
                            accumulate(b)
                        if n == OUT_AT and back(j, c, 0, 1):
                            pe.wait_ge(s.xb, 2 * (2 * j + c) + (4 if more else 2))
                            out_proj(j if c == 1 else j - 1, 1 - c)
                        if more and n in WHEN_PE:
                            if WHEN_PE[n] == ("conv", 0, 0) and back(j, c, 0, 1):
                                pe.wait_ge(s.x, CHUNKS + 2 * j + c - 1)
                            project(*nxt, *WHEN_PE[n])
                        if n == MEAN_AT and not last:
                            project(j + 1, c, "ms")

            WHEN_PE = {0: ("conv", 1, 0), 1: ("conv", 1, 1), 2: ("conv", 0, 0), 3: ("conv", 0, 1),
                       4: ("z",), 6: ("bc",), 8: ("rank",), 10: ("dt",)}
            project(0, 0, "ms")
            for piece in WHEN_PE.values():
                project(0, 0, *piece)
            project(0, 1, "ms")
            for n in range(BC_AHEAD):
                broadcast(0, 0, n)
            pair(0, False)
            with pe.Fori(1, PAIRS - 1) as j:
                pair(j, False)
            pair(PAIRS - 1, True)
            for n in range(STATES - 3, STATES):
                accumulate((1, n, 2 * PAIRS - 1))
            out_proj(PAIRS - 1, 1)

            pe.wait_ge(s.yd, 4 * PAIRS)
            pe.wait_ge(s.bcs, 2 * PAIRS * STATES)
            for c in range(CHUNKS):
                pe.wait_ge(io.merged, c + 1)
                ln_mean(pe, l, k, ln, c)
            for c in range(CHUNKS):
                ln_variance(pe, l, k, ln, 1, c)
            pe.wait_ge(io.wr, 16)

            def means_during_experts():
                for c in range(CHUNKS - 1):
                    pe.wait_ge(e1.gel, HB * EXPERTS * STEPS - HB + c + 1)
                    pe.wait_ge(e1.acc, (EXPERTS - 1) * STEPS + c + 1)
                    ln_mean(pe, l, k, ln, c)

            def rest_of_norm(done, count, r):
                for c in range(CHUNKS - 1):
                    ln_variance(pe, l, k, ln, r, c)
                pe.wait_ge(done, count)
                ln_mean(pe, l, k, ln, CHUNKS - 1)
                ln_variance(pe, l, k, ln, r, CHUNKS - 1)

            ffn_tensor(pe, e1, k, f, xn, l.out, 1, means_during_experts)
            rest_of_norm(e1.acc, EXPERTS * STEPS, 2)

            def means_during_attention():
                pe.wait_ge(at.r1, UNITS)
                for c in range(CHUNKS - 1):
                    pe.wait_ge(at.fin, c + 1)
                    ln_mean(pe, l, k, ln, c)

            att_tensor(pe, at, k, a, xn, l.out, 2, means_during_attention)
            rest_of_norm(at.fin, CHUNKS, 3)
            pe.wait_ge(io.wr, 32)
            ffn_tensor(pe, e2, k, f, xn, l.out, 3)

        @block.scalar
        def _(act):
            act.wait_ge(io.consts, 112)
            ln_scalar(act, l, k, ln, 0, xn)

            def project(j, c, piece):
                kk = 2 * j + c
                if piece == "sq":
                    act.wait_ge(s.x, kk + 1)
                    act.activation(m.sq[:], xn[:, xcols(j, c)], ACT.Square).then_inc(s.sq, 1)
                elif piece == "rstd":
                    act.wait_ge(s.ms, kk + 1)
                    wait(act, s.hn, kk)
                    act.activation(m.lnv[:], bank[1][:], ACT.Ln, bias=k.const[:, C_EPS:C_EPS + 1]).then_inc(s.ln, 1)
                    act.wait_ge(s.ln, kk + 1)
                    act.activation(m.rstd[:], m.lnv[:], ACT.Exp, scale=-0.5).then_inc(s.rstd, 1)
                elif piece == "silu":
                    wait(act, s.gate, kk - 1)
                    act.wait_ge(s.wp, 48 * j + 48)
                    for h in (1, 0):
                        act.wait_ge(s.xc_ps, 2 * kk + 2 - h)
                        act.activation(m.xc[:, c, h, :], bank[h][:], ACT.Silu,
                                       bias=m.wp[:, O_CB + h:O_CB + h + 1]).then_inc(s.xc, 1)
                    for h in (1, 0):
                        act.wait_ge(s.z_ps, 2 * kk + 2 - h)
                        act.activation(m.z[:, c, h, :], bank[h][:], ACT.Silu).then_inc(s.z, 1)
                elif piece == "parts":
                    act.wait_ge(s.bcp_ps, kk + 1)
                    act.activation(m.hi[:], bank[1][0:NPAR * 2 * STATES, :], ACT.Copy).then_inc(s.hi, 1)
                elif piece == "rank":
                    act.wait_ge(s.dtr_ps, kk + 1)
                    act.activation(m.dtr[:], bank[0][0:RANK, :], ACT.Copy).then_inc(s.dtr, 1)
                elif piece == "softplus":
                    for h in range(HALVES):
                        act.wait_ge(s.d_ps, 2 * kk + 1 + h)
                        act.activation(m.xb[:, h, :], bank[h][:], ACT.Identity,
                                       bias=m.wp[:, O_BDT + h:O_BDT + h + 1]).then_inc(s.xb, 1)
                elif piece == "exp":
                    act.wait_ge(s.xb, 2 * kk + 2)
                    wait(act, s.s1, kk)
                    act.activation(m.ab[:], m.xb[:], ACT.Abs).then_inc(s.ab, 1)
                    act.wait_ge(s.ab, kk + 1)
                    act.activation(m.ey[:], m.ab[:], ACT.Exp, scale=-1.0).then_inc(s.ey, 1)
                elif piece == "log1p":
                    act.wait_ge(s.ey, kk + 1)
                    act.activation(m.ll[:], m.ey[:], ACT.Ln, bias=1.0).then_inc(s.ll, 1)

            def decay_weights(j):
                act.wait_ge(s.wa, 16 * j + 16)
                act.activation(m.a1[:], m.alog[:], ACT.Exp).then_inc(s.a1, 1)
                act.wait_ge(s.a1, j + 1)
                act.activation(m.aneg[:], m.a1[:], ACT.Copy, scale=-1.0).then_inc(s.aneg, 1)
                act.wait_ge(s.aneg, j + 1)

            def copy(j, c, n):
                j, c, n = ahead(j, c, n)
                kk = 2 * j + c
                act.wait_ge(s.bc_ps, STATES * kk + n + 1)
                product_wait(act, kk, n - BC_RING)
                act.activation(m.bcs[:, n % BC_RING, :, :], bc_ps[n % 2][:], ACT.Copy).then_inc(s.bcs, 1)

            def decay(j, c, n):
                g = STATES * (2 * j + c) + n
                if n == 0:
                    act.wait_ge(s.delta, 2 * j + c + 1)
                wait(act, s.h, g - RING + 1)
                for h in range(HALVES):
                    a = act.activation(m.a[:, n % RING, h, :], m.delta[:, c, h, :], ACT.Exp,
                                       scale=m.aneg[:, h * STATES + n:h * STATES + n + 1])
                a.then_inc(s.a, 1)

            def pair(j, last):
                decay_weights(j)
                for c in range(2):
                    nxt = (j, 1) if c == 0 else (j + 1, 0)
                    more = c == 0 or not last
                    for n in range(STATES):
                        if n + COPY_AHEAD < STATES or more:
                            copy(j, c, n + COPY_AHEAD)
                        decay(j, c, n)
                        if more and n in WHEN_ACT:
                            for piece in WHEN_ACT[n]:
                                project(*nxt, piece)
                        if n == MEAN_AT - 1 and not last:
                            project(j + 1, c, "sq")
                        if n == MEAN_AT and not last:
                            project(j + 1, c, "rstd")

            WHEN_ACT = {4: ("silu",), 6: ("parts",), 8: ("rank",), 10: ("softplus",), 11: ("exp",), MEAN_AT: ("log1p",)}
            project(0, 0, "sq")
            project(0, 0, "rstd")
            for pieces in WHEN_ACT.values():
                for piece in pieces:
                    project(0, 0, piece)
            project(0, 1, "sq")
            project(0, 1, "rstd")
            for n in range(COPY_AHEAD):
                copy(0, 0, n)
            pair(0, False)
            with act.Fori(1, PAIRS - 1) as j:
                pair(j, False)
            pair(PAIRS - 1, True)

            ln_scalar(act, l, k, ln, 1, xn)
            ffn_scalar(act, e1, k, f, xn, l.out, 1)
            ln_scalar(act, l, k, ln, 2, xn)
            att_scalar(act, at, k, a)
            ln_scalar(act, l, k, ln, 3, xn)
            ffn_scalar(act, e2, k, f, xn, l.out, 3)

        @block.vector
        def _(dve):
            dve.memset(m.hn[:, 0:TAPS - 1], 0.0).then_inc(s.pad, 1)
            dve.wait_ge(io.x, 16 * CHUNKS)
            for c in range(CHUNKS):
                ln_center(dve, l, k, ln, 0, xn, c)
            ln_scale(dve, l, ln, 0, xn, s.x)

            def project(j, c, piece):
                kk = 2 * j + c
                if piece == "hn":
                    dve.wait_ge(s.rstd, kk + 1)
                    dve.wait_ge(s.wp, 48 * j + 48)
                    wait(dve, s.z_ps, 2 * kk)
                    dve.scalar_tensor_tensor(out=m.hn[:, TAPS - 1 + c * T:TAPS - 1 + (c + 1) * T],
                                             in0=xn[:, xcols(j, c)], scalar=m.wp[:, O_NORM:O_NORM + 1],
                                             in1=m.rstd[:], op0=ALU.mult, op1=ALU.mult).then_inc(s.hn, 1)
                elif piece == "parts":
                    nb = NPAR * 2 * STATES
                    dve.wait_ge(s.hi, kk + 1)
                    dve.scalar_tensor_tensor(out=m.r1[:], in0=m.hi[:], scalar=k.const[0:nb, C_M1:C_M1 + 1],
                                             in1=bank[1][0:nb, :], op0=ALU.mult, op1=ALU.add).then_inc(s.r1, 1)
                    dve.wait_ge(s.r1, kk + 1)
                    dve.tensor_copy(m.mid[:], m.r1[:]).then_inc(s.mid, 1)
                    dve.wait_ge(s.mid, kk + 1)
                    dve.scalar_tensor_tensor(out=m.bc[:, c, :], in0=m.mid[:], scalar=k.const[0:nb, C_M2:C_M2 + 1],
                                             in1=m.r1[:], op0=ALU.mult, op1=ALU.add).then_inc(s.bc, 1)
                elif piece == "lost":
                    dve.wait_ge(s.ey, kk + 1)
                    dve.tensor_scalar(m.dd[:], m.ey[:], 1.0, -1.0, ALU.add, ALU.add).then_inc(s.dd, 1)
                    dve.wait_ge(s.dd, kk + 1)
                    dve.scalar_tensor_tensor(out=m.dd[:], in0=m.dd[:], scalar=-1.0, in1=m.ey[:],
                                             op0=ALU.mult, op1=ALU.add).then_inc(s.t, 1)
                elif piece == "delta":
                    dve.wait_ge(s.ll, kk + 1)
                    dve.scalar_tensor_tensor(out=m.delta[:, c], in0=m.xb[:], scalar=0.0, in1=m.ll[:],
                                             op0=ALU.max, op1=ALU.add).then_inc(s.s1, 1)
                    dve.wait_ge(s.t, kk + 1)
                    dve.wait_ge(s.s1, kk + 1)
                    dve.tensor_tensor(m.delta[:, c], m.delta[:, c], m.dd[:], ALU.add).then_inc(s.delta, 1)
                    dve.wait_ge(s.delta, kk + 1)
                    dve.tensor_tensor(m.u[:, c], m.delta[:, c], m.xc[:, c], ALU.mult).then_inc(s.u, 1)

            def gate(j, c):
                kk = 2 * j + c
                dve.wait_ge(s.y_acc, STATES * (kk + 1))
                dve.wait_ge(s.wo, 16 * j + 16)
                wait(dve, s.out_ps, kk)
                for h in range(HALVES):
                    dve.scalar_tensor_tensor(out=m.yd[:, h, :], in0=m.xc[:, c, h, :],
                                             scalar=m.wo[:, HALVES * P + h:HALVES * P + h + 1],
                                             in1=y_ps[:, h, :], op0=ALU.mult, op1=ALU.add).then_inc(s.yd, 1)
                dve.wait_ge(s.yd, 2 * kk + 2)
                dve.tensor_tensor(m.yg[:], m.yd[:], m.z[:, c], ALU.mult).then_inc(s.gate, 1)

            def residual(j, c):
                kk = 2 * j + c
                dve.wait_ge(s.out_ps, kk + 1)
                x = xn[:, xcols(j, c)]
                dve.tensor_tensor(x, x, bank[0][:], ALU.add).then_inc(s.x, 1)

            def scan(j, c, n):
                g = STATES * (2 * j + c) + n
                dve.wait_ge(s.a, g + 1)
                dve.wait_ge(s.bx, g + 1)
                product_wait(dve, 2 * j + c, n - RING)
                if c == 1:
                    dve.wait_ge(s.carry, STATES * j + n + 1)
                for h in range(HALVES):
                    init = 0.0 if c == 0 else m.carry[:, h, n:n + 1]
                    i = dve.tensor_tensor_scan(m.h[:, n % RING, h, :], m.a[:, n % RING, h, :],
                                               m.bx[:, n % RING, h, :], init, ALU.mult, ALU.add)
                i.then_inc(s.h, 1)

            def product(b):
                c, n, kk = b
                g = STATES * kk + n
                dve.wait_ge(s.h, g + 1)
                if c == 0:
                    dve.tensor_copy(m.carry[:, :, n:n + 1], m.h[:, n % RING, :, T - 1:T]).then_inc(s.carry, 1)
                if n in DVE_N:
                    wait(dve, s.y_acc, g - RING + 1)
                    cb = m.bcs[:, n % BC_RING, 1:2, :].broadcast_to([P, HALVES, T])
                    dve.tensor_tensor(m.p[:, n % RING], m.h[:, n % RING], cb, ALU.mult).then_inc(s.pd, 1)

            def pair(j, last):
                for c in range(2):
                    nxt = (j, 1) if c == 0 else (j + 1, 0)
                    more = c == 0 or not last
                    for n in range(STATES):
                        scan(j, c, n)
                        product((c, n, 2 * j + c))
                        tail = back(j, c, 0, 1)
                        if n == 2 and tail:
                            gate(j if c == 1 else j - 1, 1 - c)
                        if n == OUT_AT + 1 and tail:
                            residual(j if c == 1 else j - 1, 1 - c)
                        if more and n in WHEN_DVE:
                            project(*nxt, WHEN_DVE[n])
                        if n == HN_AT and not last:
                            project(j + 1, c, "hn")

            WHEN_DVE = {7: "parts", 11: "lost", MEAN_AT: "delta"}
            project(0, 0, "hn")
            for piece in WHEN_DVE.values():
                project(0, 0, piece)
            project(0, 1, "hn")
            pair(0, False)
            with dve.Fori(1, PAIRS - 1) as j:
                pair(j, False)
            pair(PAIRS - 1, True)

            def merge(c):
                cols = slice(c * T, (c + 1) * T)
                dve.tensor_tensor(x0[:, cols], x0[:, cols], xn[:, cols], ALU.add).then_inc(io.merged, 1)

            dve.wait_ge(s.x, CHUNKS + 2 * PAIRS - 1)
            for c in range(CHUNKS - 1):
                merge(c)
            gate(PAIRS - 1, 1)
            residual(PAIRS - 1, 1)
            dve.wait_ge(s.x, CHUNKS + 2 * PAIRS)
            merge(CHUNKS - 1)

            def centers(r, chunks):
                for c in chunks:
                    ln_center(dve, l, k, ln, r, xn, c)

            most = range(CHUNKS - 1)
            centers(1, range(CHUNKS))
            split_weights(dve, e1, f, 0, 0)
            ln_scale(dve, l, ln, 1, xn)
            ffn_vector(dve, e1, k, f, x0, lambda: centers(2, most))
            centers(2, [CHUNKS - 1])
            ln_scale(dve, l, ln, 2, xn)
            att_vector(dve, at, k, a, x0, lambda: centers(3, most))
            centers(3, [CHUNKS - 1])
            split_weights(dve, e2, f, 0, 0)
            ln_scale(dve, l, ln, 3, xn)
            ffn_vector(dve, e2, k, f, x0)

        @block.gpsimd
        def _(pool):
            def fold(j):
                pool.wait_ge(s.wp, 48 * j + 48)
                wait(pool, s.z_ps, 4 * j)
                w = m.wp[:, 0:INNER].rearrange("p (a i) -> p a i", a=1).broadcast_to([P, TAPS, INNER])
                pool.tensor_tensor(m.weff[:], m.cw[:].rearrange("p (a i) -> p a i", a=TAPS), w,
                                   ALU.mult).then_inc(s.weff, 1)

            def spread_u(j, c, n):
                g = STATES * (2 * j + c) + n
                if n == 0:
                    pool.wait_ge(s.u, 2 * j + c + 1)
                pool.wait_ge(s.bcs, g + 1)
                wait(pool, s.h, g - RING + 1)
                bb = m.bcs[:, n % BC_RING, 0:1, :].broadcast_to([P, HALVES, T])
                pool.tensor_tensor(m.bx[:, n % RING], m.u[:, c], bb, ALU.mult).then_inc(s.bx, 1)

            def product(b):
                c, n, kk = b
                if n not in POOL_N:
                    return
                g = STATES * kk + n
                pool.wait_ge(s.h, g + 1)
                wait(pool, s.y_acc, g - RING + 1)
                cb = m.bcs[:, n % BC_RING, 1:2, :].broadcast_to([P, HALVES, T])
                pool.tensor_tensor(m.p[:, n % RING], m.h[:, n % RING], cb, ALU.mult).then_inc(s.pp, 1)

            def pair(j, last):
                for c in range(2):
                    for n in range(STATES):
                        spread_u(j, c, n)
                        b = back(j, c, n, 2)
                        if b:
                            product(b)
                        if c == 0 and n == 14 and not last:
                            fold(j + 1)

            fold(0)
            pair(0, False)
            with pool.Fori(1, PAIRS - 1) as j:
                pair(j, False)
            pair(PAIRS - 1, True)
            for n in range(STATES - 2, STATES):
                product((1, n, 2 * PAIRS - 1))

            ffn_pool(pool, e1, f, xn, l.out, 1)
            att_pool(pool, at, a)
            ffn_pool(pool, e2, f, xn, l.out, 3)


def pack(inputs):
    get = lambda name: np.ascontiguousarray(inputs[name])
    BF16_ONE = np.uint16(0x3F80)
    a = {}
    a["x"] = np.ascontiguousarray(get("L0_attn_a_x").reshape(TOK, P).T)
    win = get("L0_attn_a_W_in").transpose(0, 2, 1)
    wx = get("L0_attn_a_W_x").transpose(0, 2, 1)
    bcw = wx[:, :, RANK:]
    wx = np.concatenate([bcw, bcw, bcw, wx[:, :, :RANK]], axis=2)
    halves = lambda v: v.reshape(LAYERS, HALVES, P, -1).transpose(0, 2, 1, 3).reshape(LAYERS, P, -1)
    a["wp"] = np.concatenate([win, halves(wx), get("L0_attn_a_norm_w")[:, :, None],
                              halves(get("L0_attn_a_conv_b")), halves(get("L0_attn_a_b_dt"))], axis=2)
    a["wdt"] = get("L0_attn_a_W_dt").transpose(0, 2, 1)
    a["cw"] = get("L0_attn_a_conv_w").transpose(0, 2, 1).reshape(LAYERS, 1, TAPS * INNER)
    a["alog"] = halves(get("L0_attn_a_A_log"))
    a["wo"] = np.concatenate([halves(get("L0_attn_a_W_out").transpose(0, 2, 1)), halves(get("L0_attn_a_D"))], axis=2)
    a["mean_w"] = np.full((P, P), 1.0 / P, np.float32)
    const = np.zeros((P, NCONST), np.float32)
    const[:, C_EPS] = EPS
    const[2 * STATES:, C_M1] = -1.0
    const[4 * STATES:, C_M2] = -1.0
    const[:, C_HPI] = np.pi / 2
    const[:, C_MAGIC] = MAGIC
    a["const"] = const
    sel = np.zeros((NPAR, 2 * STATES, 2 * STATES, P), np.float32)
    for i in range(2 * STATES):
        sel[:, i, i, :] = 1.0
    a["bc_sel"] = sel.reshape(NPAR * 2 * STATES, 2 * STATES, P).astype(np.uint16) * BF16_ONE
    a["ident"] = np.eye(P, dtype=np.float32)
    a["ident_b"] = np.eye(P, dtype=np.float32).astype(np.uint16) * BF16_ONE
    w2 = get("L0_ffn_w2").reshape(EXPERTS, HB, P, P).transpose(0, 2, 1, 3).reshape(EXPERTS, P, HB * P)
    b1 = get("L0_ffn_b1").reshape(EXPERTS, HB, P).transpose(0, 2, 1)
    a["ew"] = np.concatenate([get("L0_ffn_w1"), w2, b1, get("L0_ffn_b2")[:, :, None]], axis=2)
    a["wr"] = get("L0_ffn_w_router")
    a["rank"] = np.tile(np.arange(EXPERTS, 0, -1, dtype=np.float32), (P, TB))
    esel = np.zeros((NPAR, EXPERTS, EXPERTS, P), np.float32)
    for i in range(EXPERTS):
        esel[:, i, i, :] = 1.0
    a["e_sel"] = esel.reshape(NPAR * EXPERTS, EXPERTS * P).astype(np.uint16) * BF16_ONE
    rf = get("L0_attn_b_rf")
    bd = np.zeros((HEADS, DH, HEADS, M), rf.dtype)
    hs = np.zeros((HEADS, DH, HEADS), np.float32)
    for h in range(HEADS):
        bd[h, :, h, :] = rf.T
        hs[h, :, h] = 1.0
    mask = np.zeros((HG, M, HG, VW), np.float32)
    for h in range(HG):
        mask[h, :, h, :] = 1.0
    a["aw"] = np.concatenate([get("L0_attn_b_" + n).T for n in ("wq", "wk", "wv", "wo")]
                             + [bd.reshape(P, HEADS * M), hs.reshape(P, HEADS), mask.reshape(P, HG * VW)], axis=1)
    return {n: np.ascontiguousarray(v) for n, v in a.items()}


def kernel(**inputs):
    import concourse.bacc as _bacc
    from concourse.bass_utils import run_bass_kernel_spmd as _run

    nc = _bacc.Bacc("TRN2", target_bir_lowering=False, num_devices=1)
    arrays = pack(inputs)
    t = {n: nc.dram_tensor(f"in_{n}", a.shape, mybir.dt.from_np(a.dtype), kind="ExternalInput").ap()
             for n, a in arrays.items()}
    d = Group()
    d.x, d.mean_w, d.const, d.bc_sel, d.e_sel, d.ident, d.ident_b, d.rank = (
        t.get(n) for n in ("x", "mean_w", "const", "bc_sel", "e_sel", "ident", "ident_b", "rank"))
    d.wp, d.wdt, d.cw, d.alog, d.wo, d.ew, d.wr, d.aw = (
        t.get(n) for n in ("wp", "wdt", "cw", "alog", "wo", "ew", "wr", "aw"))
    d.out = nc.dram_tensor("out", (P, TOK), F32, kind="ExternalOutput").ap()
    build(nc, d)
    r = _run(nc, [{f"in_{n}": a for n, a in arrays.items()}], core_ids=[0])
    out = r.results[0]["out"]
    return np.ascontiguousarray(out.T).reshape(BATCH, SEQ, P)
```
